# Optimizing a Trainium2 kernel written in Bass

```python
import numpy as np
import jax
import jax.numpy as jnp

def _softmax(x, axis=-1):
    return jax.nn.softmax(x, axis=axis)

def _gelu(x):
    return jax.nn.gelu(x, approximate=True)

def _silu(x):
    return jax.nn.silu(x)

def _sigmoid(x):
    return jax.nn.sigmoid(x)

def _layernorm(x, axis=-1, eps=1e-05):
    m = jnp.mean(x, axis=axis, keepdims=True)
    v = jnp.var(x, axis=axis, keepdims=True)
    return (x - m) / jnp.sqrt(v + eps)

def _scatter_add(tgt, idx, src, axis=0):
    return tgt.at[idx].add(src)

def _segment_sum(src, seg, n):
    return jax.ops.segment_sum(src, seg, n)
kernel_name = 'mk_seq_preln_d1_jaxref_r4_4b2a0f'

def setup_inputs(seed: int=0):
    np.random.seed(seed)
    _w = jnp.asarray

    def _L0_attn_setup():
        import jax, jax.numpy as jnp
        import numpy as np
        DIM = 256
        N_HEADS = 16
        HEAD_DIM = DIM // N_HEADS

        def apply_rope(x):
            T, D = (x.shape[-2], x.shape[-1])
            half = D // 2
            theta = 10000.0 ** (-jnp.arange(half, dtype=jnp.float32) / half)
            pos = jnp.arange(T, dtype=jnp.float32)
            freqs = pos[:, None] * theta[None, :]
            cos, sin = (jnp.cos(freqs), jnp.sin(freqs))
            x1 = x[..., :half]
            q = half // 2
            rot = jnp.concatenate([-x1[..., q:], x1[..., :q]], axis=-1)
            x_rot = x1 * cos + rot * sin
            return jnp.concatenate([x_rot, x[..., half:]], axis=-1)
        key = jax.random.key(seed)
        ks = jax.random.split(key, 9)
        B, T = (2, 512)
        s = 0.02
        return {'x': jax.random.normal(ks[0], (B, T, DIM), dtype=jnp.float32), 'Wq': jax.random.normal(ks[1], (DIM, DIM), dtype=jnp.float32) * s, 'bq': jnp.zeros((DIM,), dtype=jnp.float32), 'Wk': jax.random.normal(ks[2], (DIM, HEAD_DIM), dtype=jnp.float32) * s, 'bk': jnp.zeros((HEAD_DIM,), dtype=jnp.float32), 'Wv': jax.random.normal(ks[3], (DIM, HEAD_DIM), dtype=jnp.float32) * s, 'bv': jnp.zeros((HEAD_DIM,), dtype=jnp.float32), 'Wo': jax.random.normal(ks[4], (DIM, DIM), dtype=jnp.float32) * s, 'bo': jnp.zeros((DIM,), dtype=jnp.float32)}
    _L0_attn_in = _L0_attn_setup()

    def _L0_ffn_setup():
        import jax, jax.numpy as jnp
        import numpy as np
        E = 8
        K = 2
        D = 256
        P = 1024
        key = jax.random.key(seed)
        ks = jax.random.split(key, 8)
        s = lambda fan_in: 1.0 / np.sqrt(fan_in)
        x = jax.random.normal(ks[0], (2, 512, D), dtype=jnp.float32)
        W1 = jax.random.normal(ks[1], (E, D, P), dtype=jnp.float32) * s(D)
        b1 = jax.random.normal(ks[2], (E, P), dtype=jnp.float32) * 0.01
        W2 = jax.random.normal(ks[3], (E, P, D), dtype=jnp.float32) * s(P)
        b2 = jax.random.normal(ks[4], (E, D), dtype=jnp.float32) * 0.01
        Wr = jax.random.normal(ks[5], (D, E), dtype=jnp.float32) * s(D)
        br = jax.random.normal(ks[6], (E,), dtype=jnp.float32) * 0.01
        return {'x': x, 'W1': W1, 'b1': b1, 'W2': W2, 'b2': b2, 'Wr': Wr, 'br': br}
    _L0_ffn_in = _L0_ffn_setup()
    _d = {'L0_attn_x': _L0_attn_in['x'], 'L0_attn_Wq': _L0_attn_in['Wq'], 'L0_attn_bq': _L0_attn_in['bq'], 'L0_attn_Wk': _L0_attn_in['Wk'], 'L0_attn_bk': _L0_attn_in['bk'], 'L0_attn_Wv': _L0_attn_in['Wv'], 'L0_attn_bv': _L0_attn_in['bv'], 'L0_attn_Wo': _L0_attn_in['Wo'], 'L0_attn_bo': _L0_attn_in['bo'], 'L0_ffn_W1': _L0_ffn_in['W1'], 'L0_ffn_b1': _L0_ffn_in['b1'], 'L0_ffn_W2': _L0_ffn_in['W2'], 'L0_ffn_b2': _L0_ffn_in['b2'], 'L0_ffn_Wr': _L0_ffn_in['Wr'], 'L0_ffn_br': _L0_ffn_in['br']}
    _x0 = _d['L0_attn_x']
    _d['L0_attn_x'] = jax.random.normal(jax.random.fold_in(jax.random.key(seed), 1), (8, 512, 256), dtype=_x0.dtype)
    del _x0
    return _d

def reference(L0_attn_x, L0_attn_Wq, L0_attn_bq, L0_attn_Wk, L0_attn_bk, L0_attn_Wv, L0_attn_bv, L0_attn_Wo, L0_attn_bo, L0_ffn_W1, L0_ffn_b1, L0_ffn_W2, L0_ffn_b2, L0_ffn_Wr, L0_ffn_br):

    def _L0_attn_ref(x, Wq, bq, Wk, bk, Wv, bv, Wo, bo):
        import jax, jax.numpy as jnp
        import numpy as np
        DIM = 256
        N_HEADS = 16
        HEAD_DIM = DIM // N_HEADS

        def apply_rope(x):
            T, D = (x.shape[-2], x.shape[-1])
            half = D // 2
            theta = 10000.0 ** (-jnp.arange(half, dtype=jnp.float32) / half)
            pos = jnp.arange(T, dtype=jnp.float32)
            freqs = pos[:, None] * theta[None, :]
            cos, sin = (jnp.cos(freqs), jnp.sin(freqs))
            x1 = x[..., :half]
            q = half // 2
            rot = jnp.concatenate([-x1[..., q:], x1[..., :q]], axis=-1)
            x_rot = x1 * cos + rot * sin
            return jnp.concatenate([x_rot, x[..., half:]], axis=-1)
        B, T, C = x.shape
        H, D = (N_HEADS, HEAD_DIM)
        q = (x @ Wq + bq).reshape(B, T, H, D).transpose(0, 2, 1, 3)
        k = x @ Wk + bk
        v = x @ Wv + bv
        q = apply_rope(q)
        k = apply_rope(k)
        att = jnp.einsum('bhqd,bkd->bhqk', q, k) / jnp.sqrt(jnp.float32(D))
        causal = jnp.tril(jnp.ones((T, T), dtype=bool))
        att = jnp.where(causal[None, None], att, jnp.float32(-jnp.inf))
        att = jax.nn.softmax(att, axis=-1)
        out = jnp.einsum('bhqk,bkd->bhqd', att, v)
        out = out.transpose(0, 2, 1, 3).reshape(B, T, C)
        return out @ Wo + bo

    def _L0_ffn_ref(x, W1, b1, W2, b2, Wr, br):
        import jax, jax.numpy as jnp
        import numpy as np
        E = 8
        K = 2
        D = 256
        P = 1024
        B, S, _ = x.shape
        xf = x.reshape(B * S, D)
        scores = xf @ Wr + br
        _, top_idx = jax.lax.top_k(scores, K)
        mask = jax.nn.one_hot(top_idx, E, dtype=scores.dtype).sum(-2) > 0
        router_weights = jax.nn.softmax(jnp.where(mask, scores, -jnp.inf), axis=-1)
        h = jax.nn.gelu(jnp.einsum('td,edp->etp', xf, W1) + b1[:, None, :])
        y = jnp.einsum('etp,epd->etd', h, W2) + b2[:, None, :]
        out = jnp.einsum('te,etd->td', router_weights, y)
        return out.reshape(B, S, D)
    x = L0_attn_x
    x = x + _L0_attn_ref(_layernorm(x, axis=-1), L0_attn_Wq, L0_attn_bq, L0_attn_Wk, L0_attn_bk, L0_attn_Wv, L0_attn_bv, L0_attn_Wo, L0_attn_bo)
    x = x + _L0_ffn_ref(_layernorm(x, axis=-1), L0_ffn_W1, L0_ffn_b1, L0_ffn_W2, L0_ffn_b2, L0_ffn_Wr, L0_ffn_br)
    return x

_drawn_inputs = setup_inputs


def setup_inputs(seed=0):
    import zlib

    import numpy as np

    out = dict(_drawn_inputs(seed))
    spreads = {'L0_attn_bq': (0.0, 0.8),
     'L0_attn_bk': (0.0, 0.8),
     'L0_attn_bv': (0.0, 0.1),
     'L0_attn_bo': (0.0, 0.1)}
    factors = {'L0_attn_Wq': 5.7, 'L0_attn_Wk': 5.276, 'L0_ffn_b1': 8.0, 'L0_ffn_b2': 8.0}
    for name, (base, spread) in spreads.items():
        noise = np.random.default_rng([zlib.crc32(name.encode()), seed]).standard_normal(out[name].shape)
        drawn = base * np.exp(spread * noise) if base else spread * noise
        out[name] = jnp.asarray(drawn.astype(out[name].dtype))
    for name, factor in factors.items():
        out[name] = (out[name] * factor).astype(out[name].dtype)
    return out
```

```python
from contextlib import ExitStack

import numpy as np

import concourse.bass as bass
from concourse import mybir

F32 = mybir.dt.float32
F32R = mybir.dt.float32r
BF16 = mybir.dt.bfloat16
I32 = mybir.dt.int32
ALU = mybir.AluOpType
ACT = mybir.ActivationFunctionType
AX = mybir.AxisListType

P = 128
B, T, D = 8, 512, 256
H, HD = 16, 16
QT = T // P
KD = D // P
NT = B * QT
N = B * T
E, F = 8, 1024
KF = F // P
EPS = 1e-5
QSCALE = HD ** -0.5
PAIRS = H // 2
GROUPS = H // 4
BIG = -1e38

S_BANKS = 4 + 8 + 16 + 16
HALF_BANKS = S_BANKS // 2
T_BANKS = 10

MAX_BLOCKS = (2 * N + E * (P - 1)) // P
LIST_ROWS = E * (N // P) + 1
PAD = 2 * N
WE = KD * F + KF * D

NBIAS = E * KF + KD + 1
EARLY = 1

PREP = 15
ROUTE = 32
R_SCORES, R_MASKS, R_DIFF, R_RANK = 1, 20, 21, 25
TABLE, ROWS_AT, IDS_AT = 24, 12, 17

C_ID, C_MA, C_MB, C_REV, C_BASE, C_CNT, C_BLK, C_COL, C_IDS = (
    0, 128, 129, 130, 138, 146, 178, 178 + MAX_BLOCKS, 179 + MAX_BLOCKS)
C_END = C_IDS + 2 * QT
CB_ID, CB_S, CB_T, CB_U, CB_ONE, CB_END = 0, 128, 256, 384, 512, 640


def constants():
    row = np.arange(P)
    c = np.zeros((P, C_END), np.float32)
    c[:, C_ID:C_ID + P] = np.eye(P)
    c[:96, C_MA] = (row[:96] % 32) < 16
    c[:96, C_MB] = (row[:96] % 32) >= 16
    c[96:100, C_MA] = [1, 0, 1, 0]
    c[96:100, C_MB] = [0, 1, 0, 1]
    c[:, C_REV:C_REV + E] = E - np.arange(E)
    c[:, C_BASE:C_BASE + E] = N * np.arange(E)
    c[:, C_CNT:C_CNT + N // P] = P * np.arange(N // P)
    c[:, C_BLK:C_BLK + MAX_BLOCKS] = np.arange(MAX_BLOCKS)
    c[:, C_COL] = row
    c[:, C_IDS:C_END] = row[:, None] + (N * np.arange(2)[:, None] + P * np.arange(QT) - T).reshape(1, -1)
    b = np.zeros((P, CB_END), np.float32)
    b[:, CB_ID:CB_ID + P] = np.eye(P)
    b[:, CB_S:CB_S + P] = np.where(row[None, :] > row[:, None], BIG, 0)
    b[:, CB_T:CB_T + P] = np.where(row[:, None] > row[None, :], BIG, 0)
    b[:, CB_U:CB_U + P] = row[:, None] < row[None, :]
    b[:, CB_ONE:CB_ONE + P] = 1
    half = HD // 2
    theta = np.float32(10000.0) ** (-np.arange(half, dtype=np.float32) / np.float32(half))
    freqs = np.arange(T, dtype=np.float32)[:, None] * theta[None, :].astype(np.float32)
    cos, sin = np.cos(freqs).astype(np.float32).T, np.sin(freqs).astype(np.float32).T
    rope = np.zeros((P, 2, T), np.float32)
    for r in range(P):
        d = r % HD
        if d < half:
            rope[r, 0] = cos[d]
            rope[r, 1] = -sin[d] if d < half // 2 else sin[d]
        else:
            rope[r, 0] = 1
    return c, b, rope


def rotation():
    q = HD // 4
    return [i + q if i % HD < q else i - q if i % HD < 2 * q else i for i in range(32)]


def layer(nc, x, Wq, bq, Wk, bk, Wv, bv, Wo, bo, W1, b1, W2, b2, Wr, br, const, constb, rope, out):
    xn2_dram = nc.dram_tensor("xn2_rows", (N, D), F32, kind="Internal").ap()
    list_dram = nc.dram_tensor("expert_lists", (LIST_ROWS * P, 1), I32, kind="Internal").ap()
    y_dram = nc.dram_tensor("expert_rows", (2 * N, D), F32, kind="Internal").ap()

    with ExitStack() as ctx:
        def sem(name):
            return ctx.enter_context(nc.semaphore(name))

        def sb(name, shape, dt=F32, stack=ctx):
            return stack.enter_context(nc.sbuf_tensor(name, shape, dt))

        S = [ctx.enter_context(nc.psum_tensor(f"S{i}", [P, 512], F32)) for i in range(2)]
        TT = [ctx.enter_context(nc.psum_tensor(f"T{i}", [P, 512], F32)) for i in range(2)]
        PV = [ctx.enter_context(nc.psum_tensor(f"PV{i}", [P, 512], F32)) for i in range(2)]
        M = [ctx.enter_context(nc.psum_tensor(f"M{i}", [P, 512], F32)) for i in range(2)]

        cst = sb("cst", [P, C_END])
        cstb = sb("cstb", [P, CB_END], BF16)
        ident = cst[:, C_ID:C_ID + P]
        identb = cstb[:, CB_ID:CB_ID + P]
        xres = sb("xres", [P, NT, D])
        gate = sb("gate", [P, 2, NT])
        biasT = sb("biasT", [P, NBIAS])
        blk_expert = sb("blk_expert", [P, MAX_BLOCKS], I32)
        slots = sb("slots", [P, MAX_BLOCKS], I32)
        slot_tok = sb("slot_tok", [P, MAX_BLOCKS], I32)
        b2b = sb("b2b", [P, E, D])

        ffn = ExitStack()
        W = sb("W", [P, E, WE], F32, ffn)
        slot_now = [sb(f"slot_now{i}", [P, 1], I32, ffn) for i in range(2)]
        tok_now = [sb(f"tok_now{i}", [P, 1], I32, ffn) for i in range(2)]
        xg = [sb(f"xg{i}", [P, D], F32, ffn) for i in range(2)]
        xgT = [sb(f"xgT{i}", [P, KD, P], F32, ffn) for i in range(2)]
        hs = sb("hs", [P, F], F32, ffn)
        hT = sb("hT", [P, KF, P], F32, ffn)
        yrow = [sb(f"yrow{i}", [P, D], F32, ffn) for i in range(2)]
        ffn.close()

        sb("early_experts", [P, EARLY, WE])
        ropes = sb("ropes", [P, 2, T])
        wq = sb("wq", [P, KD, D])
        wkv1 = sb("wkv1", [P, KD, 2 * HD])
        wkv = sb("wkv", [P, KD, P])
        wo = sb("wo", [P, KD, D])
        wr = sb("wr", [P, KD, E])
        bob = sb("bob", [P, D])
        brb = sb("brb", [P, E])
        brow = sb("brow", [NBIAS, P])
        padrows = sb("padrows", [P, LIST_ROWS], I32)
        minus_half = sb("minus_half", [P, QT])
        ones = sb("ones", [P, T])
        st = [sb(f"st{i}", [P, QT, 6]) for i in range(2)]
        mv = [sb(f"mv{i}", [P, QT, 2]) for i in range(2)]
        veps = [sb(f"veps{i}", [P, QT]) for i in range(2)]
        rstd = [sb(f"rstd{i}", [P, QT]) for i in range(2)]
        xh = [sb(f"xh{i}", [P, QT, D]) for i in range(2)]
        xT = [sb(f"xT{i}", [P, KD, T]) for i in range(2)]
        qraw = sb("qraw", [P, 3, T])
        qrot = sb("qrot", [P, 3, T])
        qhi = sb("qhi", [P, 2, T], F32R)
        qlo = sb("qlo", [P, 2, T], F32R)
        khl = sb("khl", [P, T], F32R)
        KK = [[sb(f"K{p}{s}", [P, T], F32R) for s in range(2)] for p in range(2)]
        QQ = [sb(f"Q{p}", [P, PAIRS, T], F32R) for p in range(2)]
        Va = [sb(f"V{p}", [P, QT, 32]) for p in range(2)]
        nmax = sb("nmax", [P, QT, H])
        nsplit = sb("nsplit", [P, QT, 2 * H], F32R)
        mT = sb("mT", [2 * H, T], F32R)
        prob = sb("prob", [P, T_BANKS, 512])
        oT = sb("oT", [P, GROUPS, T])
        rden = sb("rden", [P, QT, H])
        on = sb("on", [P, QT, D])
        oT2 = sb("oT2", [P, KD, T])
        sc = sb("sc", [P, QT, E])
        tmp = sb("tmp", [P, QT, E])
        oh = sb("oh", [P, 2, QT, E])
        top = sb("top", [P, 2, QT])
        first = sb("first", [P, QT])
        gex = sb("gex", [P, QT])
        gsum = sb("gsum", [P, QT])
        maskb = sb("maskb", [P, QT, E], BF16)
        cum = sb("cum", [P, QT + 1, E])
        cumb = sb("cumb", [P, QT, E], BF16)
        rank = sb("rank", [P, QT, E])
        posf = sb("posf", [P, 2, QT])
        pos = sb("pos", [P, 2, QT], I32)
        idf = sb("idf", [P, 2, QT])
        idi = sb("idi", [P, 2, QT], I32)
        cumlast = sb("cumlast", [P, E], BF16)
        tot = sb("tot", [P, E])
        over = sb("over", [P, E, N // P])
        nblk = sb("nblk", [P, E])
        ends = sb("ends", [P, E])
        zeros8 = sb("zeros8", [P, E])
        le = sb("le", [P, MAX_BLOCKS, E])
        lec = sb("lec", [P, E])
        lecn = sb("lecn", [P, E])
        colv = sb("colv", [P, 4])
        rowi = sb("rowi", [P, 1], I32)
        ids_r = sb("ids_r", [MAX_BLOCKS, P], I32)
        ids_f = sb("ids_f", [MAX_BLOCKS, P])
        sl_f = sb("sl_f", [P, MAX_BLOCKS])
        sl_g = sb("sl_g", [P, MAX_BLOCKS])
        blk_f = sb("blk_f", [P, MAX_BLOCKS])

        x_in = [sem(f"x_in{i}") for i in range(2)]
        setup_in = sem("setup_in")
        list_init = sem("list_init")
        weights_in = [sem(f"weights_in{e}") for e in range(E)]
        weights_ready = sem("weights_ready")
        prep = sem("prep")
        bias_row = sem("bias_row")
        stats = [sem("stats_ln1"), sem("stats_ln2")]
        aggr = [sem("aggr_ln1"), sem("aggr_ln2")]
        eps_in = [sem("eps_ln1"), sem("eps_ln2")]
        rstd_s = [sem("rstd_ln1"), sem("rstd_ln2")]
        xh_s = [sem("xh_ln1"), sem("xh_ln2")]
        xt_full = [sem("xt_full_ln1"), sem("xt_full_ln2")]
        xt_sb = [sem("xt_sb_ln1"), sem("xt_sb_ln2")]
        bo_added = sem("bo_added")
        qkv_full = sem("qkv_full")
        qkv_sb = sem("qkv_sb")
        shuffled = sem("shuffled")
        rope_mul = sem("rope_mul")
        roped = sem("roped")
        hi_s = sem("hi_s")
        klo_s = sem("klo_s")
        ka_s = sem("ka_s")
        split_s = sem("split_s")
        stack_in = [sem("stack_in0"), sem("stack_in1")]
        s_full = sem("s_full")
        s_max = sem("s_max")
        nsplit_s = sem("nsplit_s")
        mt_full = sem("mt_full")
        mt_sb = sem("mt_sb")
        m_in = sem("m_in")
        t_full = sem("t_full")
        exps = sem("exps")
        v_full = sem("v_full")
        v_sb = sem("v_sb")
        pv_full = sem("pv_full")
        ot_sb = sem("ot_sb")
        otr_full = sem("otr_full")
        rden_s = sem("rden_s")
        on_s = sem("on_s")
        ott_full = sem("ott_full")
        ott_sb = sem("ott_sb")
        wo_full = sem("wo_full")
        x2_s = sem("x2_s")
        xn2_out = sem("xn2_out")
        sc_full = sem("sc_full")
        gexp = sem("gexp")
        route = sem("route")
        rank_full = sem("rank_full")
        listed = sem("listed")
        table = sem("table")
        tot_full = sem("tot_full")
        rows_in = sem("rows_in")
        slots_full = sem("slots_full")
        now_s = sem("now_s")
        gath = [sem("gath0"), sem("gath1")]
        xgt_full = sem("xgt_full")
        xgt_sb = sem("xgt_sb")
        f1_full = sem("f1_full")
        hs0 = sem("hs0")
        hs1 = sem("hs1")
        htr_full = sem("htr_full")
        z_s = sem("z_s")
        gelu_s = sem("gelu_s")
        f2_full = sem("f2_full")
        y_s = sem("y_s")
        snow_s = sem("snow_s")
        scat = [sem("scat0"), sem("scat1")]
        y_in = [sem(f"y_in{c}") for c in range(B)]
        half_sum = sem("half_sum")
        sum_s = sem("sum_s")
        out_done = sem("out_done")
        settled = sem("settled")

        NSETUP = 20

        def steps(eng, prologue, step, last):
            prologue()
            step(0, 0, True, False, True)
            with eng.Fori(0, 2) as j:
                step(2 * j + 1, 1, True, True, True)
                step(2 * j + 2, 0, True, True, True)
            step(5, 1, True, True, True)
            step(6, 0, True, True, False)
            step(7, 1, False, True, False)
            last()

        def half_banks(t):
            for qt, nh in ((0, 4), (1, 2), (2, 1), (3, 1)):
                for h in range(8 * t, 8 * t + 8, nh):
                    yield qt, h, nh

        BANKS = [*half_banks(0), *half_banks(1)]

        def banks_of(g, k):
            if g == 0:
                return range(0)
            at = T_BANKS * (g - 1) + k
            return range(S_BANKS * at // (3 * T_BANKS), S_BANKS * (at + 1) // (3 * T_BANKS))

        def blocks(eng, body):
            body(0, 0, True)
            body(1, 1, True)
            with eng.Fori(1, (MAX_BLOCKS - 1) // 2) as j:
                body(2 * j, 0, True)
                body(2 * j + 1, 1, True)
            body(MAX_BLOCKS - 1, 0, False)

        def settle(eng, at):
            if not isinstance(at, int):
                eng.sem_inc(settled, 1)

        assert MAX_BLOCKS % 2 == 1 and S_BANKS % 2 == 0

        block = ctx.enter_context(nc.Block())

        @block.sync
        def _(sp):
            def load(dst, src):
                sp.dma_start(dst, src).then_inc(setup_in, 16)

            for b in range(B):
                if b == 2:
                    load(cst[:, :], const)
                    load(prob[:, 0:2, :].rearrange("p a n -> p (a n)")[:, 0:CB_END], constb)
                    load(wq[:, :, :], Wq.rearrange("(k p) n -> p k n", p=P))
                    load(wkv1[:, :, 0:HD], Wk.rearrange("(k p) n -> p k n", p=P))
                    load(wkv1[:, :, HD:2 * HD], Wv.rearrange("(k p) n -> p k n", p=P))
                    load(brow[0:E * KF, :], b1.rearrange("e (k p) -> (e k) p", p=P))
                    load(brow[E * KF:E * KF + KD, :], bq.rearrange("(k p) -> k p", p=P))
                    for r in range(6):
                        load(brow[NBIAS - 1:NBIAS, HD * r:HD * r + HD], bk.rearrange("(a n) -> a n", a=1))
                    for r in range(6, 8):
                        load(brow[NBIAS - 1:NBIAS, HD * r:HD * r + HD], bv.rearrange("(a n) -> a n", a=1))
                    load(ropes[:, :, :], rope)
                    load(wo[:, :, :], Wo.rearrange("(k p) n -> p k n", p=P))
                    load(wr[:, :, :], Wr.rearrange("(k p) n -> p k n", p=P))
                    load(bob[:, :], bo.partition_broadcast(P))
                    load(brb[:, :], br.partition_broadcast(P))
                if b >= 2:
                    sp.wait_ge(x_in[b % 2], 16 * (b // 2))
                sp.dma_start(xres[:, QT * b:QT * b + QT, :],
                             x[b].rearrange("(i p) d -> p i d", p=P)).then_inc(x_in[b % 2], 16)
            sp.wait_ge(prep, 1)
            sp.dma_start(list_dram.rearrange("(p n) a -> p (n a)", p=P), padrows[:, :]).then_inc(list_init, 16)

            def weights(e):
                sp.dma_start(W[:, e, 0:KD * F].rearrange("p (k n) -> p k n", k=KD),
                             W1[e].rearrange("(k p) n -> p k n", p=P)).then_inc(weights_in[e], 16)
                sp.dma_start(W[:, e, KD * F:WE].rearrange("p (k n) -> p k n", k=KF),
                             W2[e].rearrange("(k p) n -> p k n", p=P)).then_inc(weights_in[e], 16)

            def stack(b, par, t):
                sp.wait_ge(split_s, 3 * b + (1 if t == 0 else 3))
                for g in range(4):
                    pair = 4 * t + g
                    for part, src in ((0, qhi), (1, qhi), (2, qlo)):
                        sp.dma_start(QQ[par][32 * part:32 * part + 32, pair, :].bitcast(F32),
                                     src[32 * g:32 * g + 32, t, :].bitcast(F32)).then_inc(stack_in[t], 16)

            def prologue():
                stack(0, 0, 0)
                stack(0, 0, 1)
                for e in range(EARLY):
                    weights(e)
                sp.dma_start(b2b[:, :, :], b2.partition_broadcast(P)).then_inc(weights_in[0], 16)

            def step(s, par, a, d, _):
                sp.wait_ge(mt_sb, s + 1)
                for part in range(2):
                    for one in range(2):
                        at = H * part + one
                        sp.dma_start(QQ[par][96 + 2 * part + one:97 + 2 * part + one, :, :].bitcast(F32),
                                     mT[at:at + H - 1:2, :].bitcast(F32)).then_inc(m_in, 16)
                if a:
                    stack(s + 1, 1 - par, 0)
                    stack(s + 1, 1 - par, 1)
                if d:
                    store(s - 1)

            def store(b):
                sp.wait_ge(xh_s[1], QT * b + QT)
                sp.dma_start(xn2_dram[bass.ds(T * b, T), :].rearrange("(i p) d -> p i d", p=P),
                             xh[1][:, :, :]).then_inc(xn2_out, 16)

            steps(sp, prologue, step, lambda: store(B - 1))
            sp.wait_ge(table, TABLE)
            sp.wait_ge(xn2_out, 16 * B)
            for e in range(EARLY, E):
                weights(e)
            for e in range(E):
                sp.wait_ge(weights_in[e], 48 if e == 0 else 32)
                sp.sem_inc(weights_ready, 1)
            for i in range(2):
                sp.wait_ge(scat[i], 16 * ((MAX_BLOCKS + 1 - i) // 2))
            sp.wait_ge(f2_full, MAX_BLOCKS)
            yv = y_dram.rearrange("(c i p) d -> p c i d", p=P, c=2)
            for b in range(B):
                for c in range(2):
                    sp.dma_start(W[:, b // 2, 2048 * (b % 2) + 1024 * c:2048 * (b % 2) + 1024 * (c + 1)]
                                 .rearrange("p (i d) -> p i d", d=D),
                                 yv[:, c, QT * b:QT * b + QT, :]).then_inc(y_in[b], 16)
            for b in range(B):
                sp.wait_ge(sum_s, QT * b + QT)
                sp.dma_start(out[b].rearrange("(i p) d -> p i d", p=P),
                             xres[:, QT * b:QT * b + QT, :]).then_inc(out_done, 16)
            sp.wait_ge(out_done, 16 * B)

        @block.gpsimd
        def _(pool):
            def rsqrt(n, b):
                pool.wait_ge(eps_in[n], b + 1)
                pool.tensor_tensor(rstd[n][:, :], veps[n][:, :], minus_half[:, :], ALU.pow).then_inc(rstd_s[n], 1)

            def rope_one(b, i, t, rows):
                pool.wait_ge(shuffled, 3 * b + i + 1)
                raw, rot = qraw[0:rows, t, :], qrot[0:rows, t, :]
                pool.tensor_tensor(raw, raw, ropes[0:rows, 0, :], ALU.mult).then_inc(rope_mul, 1)
                pool.tensor_tensor(rot, rot, ropes[0:rows, 1, :], ALU.mult).then_inc(rope_mul, 1)
                pool.wait_ge(rope_mul, 6 * b + 2 * i + 2)
                pool.tensor_tensor(raw, raw, rot, ALU.add).then_inc(roped, 1)

            def rope_all(b):
                rope_one(b, 0, 0, P)
                rope_one(b, 1, 2, 96)
                rope_one(b, 2, 1, P)

            def add_bo(b):
                pool.wait_ge(xh_s[0], QT * b + QT)
                xb = xres[:, bass.ds(QT * b, QT), :]
                pool.tensor_tensor(xb, xb, bob[:, :].unsqueeze(1).broadcast_to([P, QT, D]),
                                   ALU.add).then_inc(bo_added, 1)

            def scatter_ids(b):
                pool.wait_ge(route, ROUTE * b + ROUTE)
                settle(pool, b)
                for c in range(2):
                    for i in range(QT):
                        pool.indirect_dma_start(
                            out=list_dram[:, :], out_offset=bass.IndirectOffsetOnAxis(ap=pos[:, c, i:i + 1], axis=0),
                            in_=idi[:, c, i:i + 1], in_offset=None).then_inc(listed, 16)

            def prologue():
                pool.wait_ge(prep, 2)
                rsqrt(0, 0)
                pool.wait_ge(setup_in, 16 * NSETUP)
                rsqrt(0, 1)
                rope_all(0)
                add_bo(0)
                pool.wait_ge(list_init, 16)

            def step(s, par, a, d, ln):
                if a:
                    rope_all(s + 1)
                    add_bo(s + 1)
                if d:
                    rsqrt(1, s - 1)
                    scatter_ids(s - 1)
                if ln:
                    rsqrt(0, s + 2)

            def last():
                rsqrt(1, B - 1)
                scatter_ids(B - 1)

            steps(pool, prologue, step, last)
            pool.wait_ge(table, ROWS_AT)
            pool.wait_ge(listed, 16 * 2 * QT * B)
            pool.indirect_dma_start(
                out=ids_r[:, :], out_offset=None, in_=list_dram.rearrange("(r n) a -> r (n a)", n=P),
                in_offset=bass.IndirectOffsetOnAxis(ap=rowi[0:MAX_BLOCKS, 0:1], axis=0)).then_inc(rows_in, 16)
            pool.wait_ge(table, TABLE)
            pool.wait_ge(xn2_out, 16 * B)

            def gather(t, par, again):
                if again:
                    pool.wait_ge(gath[par], 8 * (t - par))
                    pool.wait_ge(xgt_full, t - 1)
                pool.tensor_copy(tok_now[par][:, :], slot_tok[:, bass.ds(t, 1)]).then_inc(now_s, 1)
                pool.wait_ge(now_s, t + 1)
                settle(pool, t)
                pool.indirect_dma_start(
                    out=xg[par][:, :], out_offset=None, in_=xn2_dram[:, :],
                    in_offset=bass.IndirectOffsetOnAxis(ap=tok_now[par][:, 0:1], axis=0)).then_inc(gath[par], 16)

            def scatter(t, par, again):
                if again:
                    pool.wait_ge(scat[par], 8 * (t - par))
                pool.tensor_copy(slot_now[par][:, :], slots[:, bass.ds(t, 1)]).then_inc(snow_s, 1)
                pool.wait_ge(y_s, t + 1)
                pool.wait_ge(snow_s, t + 1)
                settle(pool, t)
                pool.indirect_dma_start(
                    out=y_dram[:, :], out_offset=bass.IndirectOffsetOnAxis(ap=slot_now[par][:, 0:1], axis=0),
                    in_=yrow[par][:, :], in_offset=None, bounds_check=2 * N - 1,
                    oob_is_err=False).then_inc(scat[par], 16)

            for t in range(2):
                gather(t, t, False)
            for t in range(2):
                gather(t + 2, t, True)
                scatter(t, t, False)
            with pool.Fori(1, (MAX_BLOCKS - 3) // 2) as j:
                for par in range(2):
                    gather(2 * j + par + 2, par, True)
                    scatter(2 * j + par, par, True)
            gather(MAX_BLOCKS - 1, 0, True)
            for t in range(MAX_BLOCKS - 3, MAX_BLOCKS):
                scatter(t, t % 2, True)

        @block.scalar
        def _(act):
            def evac_xT(n, b, k):
                act.wait_ge(xt_full[n], KD * b + k + 1)
                if n == 0 and not (isinstance(b, int) and b == 0):
                    act.wait_ge(qkv_full, 3 * b)
                if n == 1 and not (isinstance(b, int) and b == 0):
                    act.wait_ge(sc_full, b)
                act.activation(xT[n][:, k, :], M[1 - k if n == 0 else k][:, :], ACT.Copy).then_inc(xt_sb[n], 1)

            def evac_qkv(b):
                for i, t, bank in ((0, 0, 1), (1, 2, 0), (2, 1, 1)):
                    act.wait_ge(qkv_full, 3 * b + i + 1)
                    if not (isinstance(b, int) and b == 0):
                        act.wait_ge(split_s, 3 * b)
                        act.wait_ge(v_full, 2 * b)
                    bias = biasT[:, E * KF + t:E * KF + t + 1]
                    act.activation(qraw[:, t, :], M[bank][:, :], ACT.Identity, bias=bias,
                                   scale=1.0 if t == 2 else QSCALE).then_inc(qkv_sb, 1)

            def evac_v(b, par):
                for u in range(2):
                    act.wait_ge(v_full, 2 * b + u + 1)
                    if not (isinstance(b, int) and b < 2):
                        act.wait_ge(pv_full, 3 * GROUPS * (b - 1))
                    act.activation(Va[par][:, 2 * u:2 * u + 2, 0:HD],
                                   M[u][:, 0:64].rearrange("p (i w) -> p i w", w=32)[:, :, 0:HD],
                                   ACT.Copy).then_inc(v_sb, 1)

            def exp_bank(s, g, k):
                stage = 0 if k < 4 else 1 if k < 8 else 2
                act.wait_ge(t_full, GROUPS * T_BANKS * s + T_BANKS * g + k + 1)
                if not (isinstance(s, int) and s == 0 and g == 0):
                    act.wait_ge(pv_full, 3 * GROUPS * s + 3 * g + stage - 2)
                act.activation(prob[:, k, :], TT[k % 2][:, :], ACT.Exp).then_inc(exps, 1)

            def evac_oT(s, g):
                act.wait_ge(pv_full, 3 * GROUPS * s + 3 * g + 3)
                if not (isinstance(s, int) and s == 0):
                    act.wait_ge(otr_full, QT * s)
                act.activation(oT[:, g, :], PV[g % 2][:, :], ACT.Copy).then_inc(ot_sb, 1)

            def evac_oTT(b, k):
                act.wait_ge(ott_full, KD * b + k + 1)
                if not (isinstance(b, int) and b == 0):
                    act.wait_ge(wo_full, 2 * b)
                act.activation(oT2[:, k, :], M[k][:, :], ACT.Copy).then_inc(ott_sb, 1)

            def gate_exp(b):
                act.wait_ge(route, ROUTE * b + R_DIFF)
                act.activation(gex[:, :], gex[:, :], ACT.Exp).then_inc(gexp, 1)

            def prologue():
                act.wait_ge(prep, PREP)
                for k in range(KD):
                    evac_xT(0, 0, k)
                evac_qkv(0)
                evac_v(0, 0)

            def step(s, par, a, d, _):
                act.wait_ge(mt_full, s + 1)
                if not (isinstance(s, int) and s == 0):
                    act.wait_ge(m_in, 64 * s)
                act.activation(mT[:, :], M[0][0:2 * H, :], ACT.Copy).then_inc(mt_sb, 1)
                if a:
                    for k in range(KD):
                        evac_xT(0, s + 1, k)
                    evac_qkv(s + 1)
                for g in range(GROUPS):
                    for k in range(T_BANKS):
                        exp_bank(s, g, k)
                        if g >= 1 and k == 8:
                            evac_oT(s, g - 1)
                        if d and (g, k) in ((0, 8), (0, 9)):
                            evac_oTT(s - 1, k - 8)
                        if d and (g, k) in ((2, 3), (2, 4)):
                            evac_xT(1, s - 1, k - 3)
                        if d and (g, k) == (3, 3):
                            gate_exp(s - 1)
                if a:
                    evac_v(s + 1, 1 - par)
                evac_oT(s, GROUPS - 1)

            def last():
                for k in range(KD):
                    evac_oTT(B - 1, k)
                for k in range(KD):
                    evac_xT(1, B - 1, k)
                gate_exp(B - 1)

            steps(act, prologue, step, last)

            def evac_xgT(t, par):
                act.wait_ge(xgt_full, t + 1)
                if not (isinstance(t, int) and t < 2):
                    act.wait_ge(f1_full, 2 * t - 2)
                act.activation(xgT[par][:, :, :], M[0][:, 0:D].rearrange("p (k n) -> p k n", k=KD),
                               ACT.Copy).then_inc(xgt_sb, 1)

            def evac_h1(t):
                act.wait_ge(f1_full, 2 * t + 2)
                if not (isinstance(t, int) and t == 0):
                    act.wait_ge(htr_full, 2 * t)
                act.activation(hs[:, 512:1024], S[1][:, :], ACT.Copy).then_inc(hs1, 1)

            act.wait_ge(table, TABLE)
            evac_xgT(0, 0)
            evac_h1(0)

            def body(t, par, following):
                if following:
                    evac_xgT(t + 1, 1 - par)
                for c in range(2):
                    act.wait_ge(z_s, 2 * t + c + 1)
                    half = hT[:, 4 * c:4 * c + 4, :]
                    act.activation(half, half, ACT.Gelu_apprx_tanh).then_inc(gelu_s, 1)
                if following:
                    evac_h1(t + 1)

            blocks(act, body)

        @block.vector
        def _(dve):
            def tile_of(b, i):
                return xres[:, bass.ds(QT * b + i, 1), :].rearrange("p a d -> p (a d)")

            def ln_stats(n, b, par):
                for i in range(QT):
                    if n == 0 and i == 0:
                        dve.wait_ge(x_in[par], 8 * (b - par) + 16)
                        settle(dve, b)
                    if n == 1 and i % 2 == 0:
                        dve.wait_ge(x2_s, 2 * b + i // 2 + 1)
                        settle(dve, b)
                    dve.bn_stats(st[n][:, i, :], tile_of(b, i)).then_inc(stats[n], 1)
                for i in range(QT):
                    dve.wait_ge(stats[n], QT * b + i + 1)
                    settle(dve, b)
                    dve.bn_aggr(mv[n][:, i, :], st[n][:, i, :]).then_inc(aggr[n], 1)
                dve.wait_ge(aggr[n], QT * b + QT)
                dve.tensor_scalar(veps[n][:, :], mv[n][:, :, 1], EPS, None, ALU.add).then_inc(eps_in[n], 1)

            def ln_apply(n, b):
                dve.wait_ge(rstd_s[n], b + 1)
                if not (isinstance(b, int) and b == 0):
                    dve.wait_ge(xt_full[n], KD * b)
                    if n == 1:
                        dve.wait_ge(xn2_out, 16 * b)
                for i in range(QT):
                    dve.tensor_scalar(xh[n][:, i, :], tile_of(b, i),
                                      mv[n][:, i, 0:1], rstd[n][:, i:i + 1], ALU.subtract, ALU.mult)\
                       .then_inc(xh_s[n], 1)

            def shuffle_one(b, i, t):
                dve.wait_ge(qkv_sb, 3 * b + i + 1)
                settle(dve, b)
                dve.stream_shuffle(qrot[:, t, :], qraw[:, t, :], ROT).then_inc(shuffled, 1)

            def split_q(b, i, t):
                dve.wait_ge(roped, 3 * b + i + 1)
                if not (isinstance(b, int) and b == 0):
                    dve.wait_ge(stack_in[t], 16 * 12 * b)
                dve.tensor_copy(qhi[:, t, :], qraw[:, t, :]).then_inc(hi_s, 1)
                dve.wait_ge(hi_s, 3 * b + i + 1)
                dve.tensor_tensor(qlo[:, t, :], qraw[:, t, :], qhi[:, t, :].bitcast(F32),
                                  ALU.subtract).then_inc(split_s, 1)

            def split_k(b, par):
                dve.wait_ge(roped, 3 * b + 2)
                dve.tensor_copy(khl[0:96, :], qraw[0:96, 2, :]).then_inc(hi_s, 1)
                dve.wait_ge(hi_s, 3 * b + 2)
                dve.tensor_tensor(khl[32:64, :], qraw[32:64, 2, :], khl[32:64, :].bitcast(F32),
                                  ALU.subtract).then_inc(klo_s, 1)
                dve.wait_ge(klo_s, b + 1)
                if not (isinstance(b, int) and b < 2):
                    dve.wait_ge(t_full, GROUPS * T_BANKS * (b - 1))
                dve.tensor_scalar(KK[par][0][:, :], khl[:, :].bitcast(F32), cst[:, C_MA:C_MA + 1], None,
                                  ALU.mult).then_inc(ka_s, 1)
                dve.tensor_scalar(KK[par][1][:, :], khl[:, :].bitcast(F32), cst[:, C_MB:C_MB + 1], None,
                                  ALU.mult).then_inc(split_s, 1)

            def maxima(b, n):
                qt, h, nh = BANKS[n]
                w = P * (qt + 1)
                dve.wait_ge(s_full, S_BANKS * b + n + 1)
                dve.tensor_reduce(nmax[:, qt, h:h + nh], S[n % 2][:, 0:nh * w].rearrange("p (h w) -> p h w", h=nh),
                                  AX.X, ALU.max, negate=True).then_inc(s_max, 1)

            def split_maxima(b):
                dve.wait_ge(s_max, S_BANKS * b + S_BANKS)
                if not (isinstance(b, int) and b == 0):
                    dve.wait_ge(mt_full, b)
                dve.tensor_copy(nsplit[:, :, 0:H], nmax[:, :, :]).then_inc(nsplit_s, 1)
                dve.wait_ge(nsplit_s, 2 * b + 1)
                dve.tensor_tensor(nsplit[:, :, H:2 * H], nmax[:, :, :], nsplit[:, :, 0:H].bitcast(F32),
                                  ALU.subtract).then_inc(nsplit_s, 1)

            def normalise(b, i):
                bank = M[i % 2][:, :].rearrange("p (h w) -> p h w", w=32)
                dve.wait_ge(otr_full, QT * b + i + 1)
                dve.reciprocal(rden[:, i, :], bank[:, :, HD]).then_inc(rden_s, 1)
                dve.wait_ge(rden_s, QT * b + i + 1)
                if not (isinstance(b, int) and b == 0):
                    dve.wait_ge(ott_full, KD * b)
                dve.tensor_tensor(on[:, i, :].rearrange("p (h d) -> p h d", d=HD), bank[:, :, 0:HD],
                                  rden[:, i, :].unsqueeze(2).broadcast_to([P, H, HD]), ALU.mult).then_inc(on_s, 1)

            def residual(b, u):
                dve.wait_ge(wo_full, 2 * b + u + 1)
                dve.wait_ge(bo_added, b + 1)
                two = xres[:, bass.ds(QT * b + 2 * u, 2), :]
                dve.tensor_tensor(two, M[u][:, :].rearrange("p (i d) -> p i d", i=2), two, ALU.add)\
                   .then_inc(x2_s, 1)

            def over_experts(ap):
                return ap.unsqueeze(2).broadcast_to([P, QT, E])

            def over_tiles(at):
                return cst[:, at:at + E].unsqueeze(1).broadcast_to([P, QT, E])

            def after(b, n):
                dve.wait_ge(route, ROUTE * b + n)

            def route_first(b):
                dve.wait_ge(sc_full, b + 1)
                dve.tensor_tensor(sc[:, :, :], M[0][:, 0:QT * E].rearrange("p (i e) -> p i e", e=E),
                                  brb[:, :].unsqueeze(1).broadcast_to([P, QT, E]), ALU.add).then_inc(route, 1)
                after(b, 1)
                dve.tensor_reduce(top[:, 0, :], sc[:, :, :], AX.X, ALU.max).then_inc(route, 1)
                after(b, 2)
                dve.tensor_tensor(tmp[:, :, :], sc[:, :, :], over_experts(top[:, 0, :]), ALU.is_equal).then_inc(route, 1)
                after(b, 3)
                dve.tensor_tensor(tmp[:, :, :], tmp[:, :, :], over_tiles(C_REV), ALU.mult).then_inc(route, 1)

            def route_first_end(b):
                after(b, 4)
                dve.tensor_reduce(first[:, :], tmp[:, :, :], AX.X, ALU.max).then_inc(route, 1)
                after(b, 5)
                dve.tensor_tensor(oh[:, 0, :, :], tmp[:, :, :], over_experts(first[:, :]), ALU.is_equal)\
                   .then_inc(route, 1)

            def route_second(b):
                after(b, 6)
                dve.scalar_tensor_tensor(out=tmp[:, :, :], in0=oh[:, 0, :, :], scalar=-3e38, in1=sc[:, :, :],
                                         op0=ALU.mult, op1=ALU.add).then_inc(route, 1)
                after(b, 7)
                dve.tensor_reduce(top[:, 1, :], tmp[:, :, :], AX.X, ALU.max).then_inc(route, 1)
                after(b, 8)
                dve.tensor_tensor(tmp[:, :, :], tmp[:, :, :], over_experts(top[:, 1, :]), ALU.is_equal).then_inc(route, 1)
                after(b, 9)
                dve.tensor_tensor(tmp[:, :, :], tmp[:, :, :], over_tiles(C_REV), ALU.mult).then_inc(route, 1)

            def route_second_end(b):
                after(b, 10)
                dve.tensor_reduce(first[:, :], tmp[:, :, :], AX.X, ALU.max).then_inc(route, 1)
                after(b, 11)
                dve.tensor_tensor(oh[:, 1, :, :], tmp[:, :, :], over_experts(first[:, :]), ALU.is_equal)\
                   .then_inc(route, 1)
                after(b, 12)
                dve.tensor_tensor(tmp[:, :, :], oh[:, 0, :, :], oh[:, 1, :, :], ALU.add).then_inc(route, 1)

            def route_counts(b):
                after(b, 13)
                if not (isinstance(b, int) and b == 0):
                    dve.wait_ge(rank_full, b)
                dve.tensor_copy(maskb[:, :, :], tmp[:, :, :]).then_inc(route, 1)
                for i in range(QT):
                    if i:
                        after(b, 14 + i)
                    dve.tensor_tensor(cum[:, i + 1, :], cum[:, i, :], tmp[:, i, :], ALU.add).then_inc(route, 1)
                after(b, 18)
                dve.tensor_copy(cumb[:, :, :], cum[:, 0:QT, :]).then_inc(route, 1)
                after(b, 19)
                dve.tensor_copy(cum[:, 0, :], cum[:, QT, :]).then_inc(route, 1)
                if not (isinstance(b, int) and b == 0):
                    dve.wait_ge(gexp, b)
                dve.tensor_tensor(gex[:, :], top[:, 1, :], top[:, 0, :], ALU.subtract).then_inc(route, 1)

            def route_gates(b):
                dve.wait_ge(gexp, b + 1)
                dve.tensor_scalar(gsum[:, :], gex[:, :], 1.0, None, ALU.add).then_inc(route, 1)
                after(b, 22)
                dve.reciprocal(gate[:, 0, bass.ds(QT * b, QT)], gsum[:, :]).then_inc(route, 1)
                after(b, 23)
                dve.tensor_tensor(gate[:, 1, bass.ds(QT * b, QT)], gex[:, :], gate[:, 0, bass.ds(QT * b, QT)],
                                  ALU.mult).then_inc(route, 1)

            def route_places(b):
                dve.wait_ge(rank_full, b + 1)
                dve.tensor_tensor(rank[:, :, :], M[1][:, 0:QT * E].rearrange("p (i e) -> p i e", e=E),
                                  over_tiles(C_BASE), ALU.add).then_inc(route, 1)
                for c in range(2):
                    after(b, 25 + 2 * c)
                    dve.tensor_tensor(tmp[:, :, :], oh[:, c, :, :], rank[:, :, :], ALU.mult).then_inc(route, 1)
                    after(b, 26 + 2 * c)
                    dve.tensor_reduce(posf[:, c, :], tmp[:, :, :], AX.X, ALU.add).then_inc(route, 1)
                after(b, 29)
                if not (isinstance(b, int) and b == 0):
                    dve.wait_ge(listed, 16 * 2 * QT * b)
                dve.tensor_copy(pos[:, :, :], posf[:, :, :]).then_inc(route, 1)
                dve.tensor_scalar(idf[:, :, :], idf[:, :, :], float(T), None, ALU.add).then_inc(route, 1)
                after(b, 31)
                dve.tensor_copy(idi[:, :, :], idf[:, :, :]).then_inc(route, 1)

            def prologue():
                dve.memset(padrows[:, :], PAD).then_inc(prep, 1)
                dve.memset(minus_half[:, :], -0.5).then_inc(prep, 1)
                dve.memset(ones[:, :], 1.0).then_inc(prep, 1)
                for v in Va:
                    dve.memset(v[:, :, HD:32], 1.0).then_inc(prep, 1)
                dve.memset(zeros8[:, :], 0.0).then_inc(prep, 1)
                dve.memset(cum[:, 0, :], 0.0).then_inc(prep, 1)
                dve.wait_ge(prep, 3)
                dve.tensor_copy(khl[96:128, :], ones[96:128, :]).then_inc(prep, 1)
                ln_stats(0, 0, 0)
                ln_apply(0, 0)
                dve.wait_ge(setup_in, 16 * NSETUP)
                dve.tensor_copy(cstb[:, :], prob[:, 0:2, :].rearrange("p a n -> p (a n)")[:, 0:CB_END])\
                   .then_inc(prep, 1)
                dve.tensor_copy(wkv[:, :, 0:96].rearrange("p k (r d) -> p k r d", d=HD),
                                wkv1[:, :, 0:HD].unsqueeze(2).broadcast_to([P, KD, 6, HD])).then_inc(prep, 1)
                dve.tensor_copy(wkv[:, :, 96:128].rearrange("p k (r d) -> p k r d", d=HD),
                                wkv1[:, :, HD:2 * HD].unsqueeze(2).broadcast_to([P, KD, 2, HD])).then_inc(prep, 1)
                dve.tensor_copy(idf[:, :, :], cst[:, C_IDS:C_END].rearrange("p (c i) -> p c i", c=2)).then_inc(prep, 1)
                dve.wait_ge(bias_row, 1)
                at = E * KF
                dve.tensor_copy(biasT[:, 0:at], M[0][:, 0:at]).then_inc(prep, 1)
                dve.tensor_scalar(biasT[:, at:at + KD], M[0][:, at:at + KD], QSCALE, None, ALU.mult).then_inc(prep, 1)
                dve.tensor_copy(biasT[:, at + KD:NBIAS], M[0][:, at + KD:NBIAS]).then_inc(prep, 1)
                ln_stats(0, 1, 1)
                shuffle_one(0, 0, 0)
                shuffle_one(0, 1, 2)
                shuffle_one(0, 2, 1)
                split_q(0, 0, 0)
                split_k(0, 0)
                split_q(0, 2, 1)
                ln_apply(0, 1)
                for n in range(S_BANKS):
                    maxima(0, n)

            def step(s, par, a, d, ln):
                split_maxima(s)
                if a:
                    shuffle_one(s + 1, 0, 0)
                    shuffle_one(s + 1, 1, 2)
                    shuffle_one(s + 1, 2, 1)
                if d:
                    normalise(s - 1, 0)
                    normalise(s - 1, 1)
                if a:
                    split_q(s + 1, 0, 0)
                if d:
                    normalise(s - 1, 2)
                    normalise(s - 1, 3)
                if a:
                    split_k(s + 1, 1 - par)
                    split_q(s + 1, 2, 1)
                for g in range(1, GROUPS):
                    for k in range(T_BANKS):
                        if a:
                            for n in banks_of(g, k):
                                maxima(s + 1, n)
                        if d and (g, k) == (1, 2):
                            residual(s - 1, 0)
                        if d and (g, k) == (1, 4):
                            residual(s - 1, 1)
                        if d and (g, k) == (1, 5):
                            ln_stats(1, s - 1, 1 - par)
                        if d and (g, k) == (1, 8):
                            ln_apply(1, s - 1)
                        if d and (g, k) == (2, 7):
                            route_first(s - 1)
                        if d and (g, k) == (2, 8):
                            route_first_end(s - 1)
                        if d and (g, k) == (2, 9):
                            route_second(s - 1)
                        if d and (g, k) == (3, 0):
                            route_second_end(s - 1)
                        if d and (g, k) == (3, 1):
                            route_counts(s - 1)
                        if d and (g, k) == (3, 4):
                            route_gates(s - 1)
                        if d and (g, k) == (3, 5):
                            route_places(s - 1)
                        if ln and (g, k) == (3, 6):
                            ln_stats(0, s + 2, par)
                        if ln and (g, k) == (3, 8):
                            ln_apply(0, s + 2)

            def last():
                b = B - 1
                for i in range(QT):
                    normalise(b, i)
                residual(b, 0)
                residual(b, 1)
                ln_stats(1, b, b % 2)
                ln_apply(1, b)
                route_first(b)
                route_first_end(b)
                route_second(b)
                route_second_end(b)
                route_counts(b)
                route_gates(b)
                route_places(b)

            ROT = rotation()
            steps(dve, prologue, step, last)

            def did(n):
                dve.wait_ge(table, n)

            dve.wait_ge(route, ROUTE * B)
            dve.tensor_copy(cumlast[:, :], cum[:, 0, :]).then_inc(table, 1)
            dve.wait_ge(tot_full, 1)
            dve.tensor_copy(tot[:, :], M[0][:, 0:E]).then_inc(table, 1)
            did(2)
            dve.tensor_tensor(over[:, :, :], tot[:, :].unsqueeze(2).broadcast_to([P, E, N // P]),
                              cst[:, C_CNT:C_CNT + N // P].unsqueeze(1).broadcast_to([P, E, N // P]),
                              ALU.is_gt).then_inc(table, 1)
            did(3)
            dve.tensor_reduce(nblk[:, :], over[:, :, :], AX.X, ALU.add).then_inc(table, 1)
            did(4)
            dve.tensor_tensor_scan(ends[:, :], nblk[:, :], zeros8[:, :], 0.0, ALU.add, ALU.add).then_inc(table, 1)
            did(5)
            dve.tensor_scalar(lec[:, :], ends[:, :], cst[:, C_COL:C_COL + 1], None, ALU.is_le).then_inc(table, 1)
            did(6)
            dve.tensor_reduce(colv[:, 0:1], lec[:, :], AX.X, ALU.add).then_inc(table, 1)
            dve.tensor_tensor(lecn[:, :], lec[:, :], nblk[:, :], ALU.mult).then_inc(table, 1)
            did(8)
            dve.tensor_reduce(colv[:, 1:2], lecn[:, :], AX.X, ALU.add).then_inc(table, 1)
            did(9)
            dve.scalar_tensor_tensor(out=colv[:, 2:3], in0=colv[:, 0:1], scalar=float(N // P),
                                     in1=cst[:, C_COL:C_COL + 1], op0=ALU.mult, op1=ALU.add).then_inc(table, 1)
            did(10)
            dve.tensor_tensor(colv[:, 3:4], colv[:, 2:3], colv[:, 1:2], ALU.subtract).then_inc(table, 1)
            did(11)
            dve.tensor_scalar(rowi[:, :], colv[:, 3:4], float(LIST_ROWS - 1), None, ALU.min).then_inc(table, 1)
            dve.tensor_tensor(le[:, :, :], ends[:, :].unsqueeze(1).broadcast_to([P, MAX_BLOCKS, E]),
                              cst[:, C_BLK:C_BLK + MAX_BLOCKS].unsqueeze(2).broadcast_to([P, MAX_BLOCKS, E]),
                              ALU.is_le).then_inc(table, 1)
            did(13)
            dve.tensor_reduce(blk_f[:, :], le[:, :, :], AX.X, ALU.add).then_inc(table, 1)
            did(14)
            dve.tensor_scalar(blk_f[:, :], blk_f[:, :], float(E - 1), None, ALU.min).then_inc(table, 1)
            did(15)
            dve.tensor_copy(blk_expert[:, :], blk_f[:, :]).then_inc(table, 1)
            dve.wait_ge(rows_in, 16)
            dve.tensor_copy(ids_f[:, :], ids_r[:, :]).then_inc(table, 1)
            dve.wait_ge(slots_full, 1)
            dve.tensor_copy(sl_f[:, :], M[1][:, 0:MAX_BLOCKS]).then_inc(table, 1)
            did(18)
            dve.tensor_copy(slots[:, :], sl_f[:, :]).then_inc(table, 1)
            for n in (19, 21):
                did(n)
                dve.tensor_scalar(sl_g[:, :], sl_f[:, :], float(N), -float(N), ALU.is_ge, ALU.mult).then_inc(table, 1)
                did(n + 1)
                dve.tensor_tensor(sl_f[:, :], sl_f[:, :], sl_g[:, :], ALU.add).then_inc(table, 1)
            did(23)
            dve.tensor_copy(slot_tok[:, :], sl_f[:, :]).then_inc(table, 1)
            did(TABLE)

            def evac_h0(t):
                dve.wait_ge(f1_full, 2 * t + 1)
                if not (isinstance(t, int) and t == 0):
                    dve.wait_ge(htr_full, 2 * t)
                dve.tensor_copy(hs[:, 0:512], S[0][:, :]).then_inc(hs0, 1)

            evac_h0(0)

            def body(t, par, following):
                e = dve.value_load(blk_expert[0:1, bass.ds(t, 1)], min_val=0, max_val=E - 1)
                for c in range(2):
                    dve.wait_ge(htr_full, 2 * t + c + 1)
                    if not (isinstance(t, int) and t == 0):
                        dve.wait_ge(f2_full, t)
                    dve.tensor_tensor(hT[:, 4 * c:4 * c + 4, :], TT[c][:, :].rearrange("p (k n) -> p k n", n=P),
                                      biasT[:, bass.ds(KF * e + 4 * c, 4)].unsqueeze(2).broadcast_to([P, 4, P]),
                                      ALU.add).then_inc(z_s, 1)
                if following:
                    evac_h0(t + 1)
                dve.wait_ge(f2_full, t + 1)
                if not (isinstance(t, int) and t < 2):
                    dve.wait_ge(scat[par], 8 * (t - par))
                dve.tensor_tensor(yrow[par][:, :], PV[par][:, 0:D], b2b[:, bass.ds(e, 1), :].rearrange("p a d -> p (a d)"),
                                  ALU.add).then_inc(y_s, 1)

            blocks(dve, body)

            for b in range(B):
                dve.wait_ge(y_in[b], 32)
                yb = W[:, b // 2, 2048 * (b % 2):2048 * (b % 2) + 2048].rearrange("p (c i d) -> p c i d", c=2, d=D)
                for c, done in ((0, half_sum), (1, sum_s)):
                    for i in range(QT):
                        t = QT * b + i
                        if c:
                            dve.wait_ge(half_sum, t + 1)
                        dve.scalar_tensor_tensor(out=xres[:, t, :], in0=yb[:, c, i, :], scalar=gate[:, c, t:t + 1],
                                                 in1=xres[:, t, :], op0=ALU.mult, op1=ALU.add).then_inc(done, 1)

        @block.tensor
        def _(pe):
            def transposes(dst, srcs, width, done):
                for i, src in enumerate(srcs):
                    last = pe.transpose(dst[:, width * i:width * i + width], src, ident)
                last.then_inc(done, 1)

            def xT_of(n, b, k):
                pe.wait_ge(xh_s[n], QT * b + QT)
                if n == 1:
                    if k == 0:
                        pe.wait_ge(x2_s, 2 * b + 1)
                    else:
                        pe.wait_ge(x2_s, 2 * b + 2)
                    bank = M[k]
                else:
                    if isinstance(b, int) and b == 0:
                        pe.wait_ge(prep, PREP)
                    elif k == 0:
                        pe.wait_ge(v_sb, 2 * b)
                    else:
                        pe.wait_ge(mt_sb, b)
                    bank = M[1 - k]
                transposes(bank, [xh[n][:, i, P * k:P * k + P] for i in range(QT)], P, xt_full[n])

            def project(b):
                pe.wait_ge(xt_sb[0], KD * b + 2)
                for i, t, bank in ((0, 0, 1), (1, 2, 0), (2, 1, 1)):
                    if i == 2:
                        pe.wait_ge(qkv_sb, 3 * b + 1)
                    for k in range(KD):
                        w = wkv[:, k, :] if t == 2 else wq[:, k, P * t:P * t + P]
                        last = pe.matmul(M[bank][:, :], w, xT[0][:, k, :], start=(k == 0), stop=(k == KD - 1))
                    last.then_inc(qkv_full, 1)

            def v_rows(b, d):
                pe.wait_ge(qkv_sb, 3 * b + 3)
                settle(pe, b)
                for u in range(2):
                    if d:
                        pe.wait_ge(route, ROUTE * (b - 2) + (R_SCORES, R_RANK)[u])
                        settle(pe, b)
                    for i in range(2):
                        at = P * (2 * u + i)
                        last = pe.transpose(M[u][:, 32 * i:32 * i + 32], qraw[96:128, 2, at:at + P],
                                            ident[96:128, 96:128])
                    last.then_inc(v_full, 1)

            def scores_bank(b, par, n):
                qt, h0, nh = BANKS[n]
                if n == 0:
                    pe.wait_ge(split_s, 3 * b + 2)
                if n % HALF_BANKS == 0:
                    pe.wait_ge(stack_in[n // HALF_BANKS], 16 * 12 * b + 16 * 12)
                if not (isinstance(b, int) and b == 0 and n < 2):
                    pe.wait_ge(s_max, S_BANKS * b + n - 1)
                w = P * (qt + 1)
                for i in range(nh):
                    h = h0 + i
                    pe.matmul(S[n % 2][:, w * i:w * i + w], QQ[par][0:96, h // 2, P * qt:P * qt + P],
                              KK[par][h % 2][0:96, 0:w], start=True, stop=True)
                    last = pe.matmul(S[n % 2][:, w * i + P * qt:w * i + w], identb, cstb[:, CB_S:CB_S + P],
                                     start=False, stop=True, skip_group_check=True)
                last.then_inc(s_full, 1)

            def max_rows(b):
                pe.wait_ge(nsplit_s, 2 * b + 2)
                pe.wait_ge(v_sb, 2 * b + 1)
                for i in range(QT):
                    last = pe.transpose(M[0][0:2 * H, P * i:P * i + P], nsplit[:, i, :].bitcast(F32), ident)
                last.then_inc(mt_full, 1)

            def soft_part(par, bank, at, h, kt):
                w = T - P * kt
                pe.matmul(bank[:, at:at + w], KK[par][h % 2][0:100, P * kt:P * kt + P],
                          QQ[par][0:100, h // 2, P * kt:T], start=True, stop=True)
                return pe.matmul(bank[:, at:at + P], identb, cstb[:, CB_T:CB_T + P],
                                 start=False, stop=True, skip_group_check=True)

            def soft_bank(s, par, g, k):
                n = T_BANKS * g + k
                if not (isinstance(s, int) and s == 0 and n < 2):
                    pe.wait_ge(exps, GROUPS * T_BANKS * s + n - 1)
                bank = TT[k % 2]
                if k < 4:
                    last = soft_part(par, bank, 0, 4 * g + k, 0)
                elif k < 8:
                    soft_part(par, bank, 0, 4 * g + k - 4, 1)
                    last = soft_part(par, bank, 3 * P, 4 * g + k - 4, 3)
                else:
                    soft_part(par, bank, 0, 4 * g + 2 * (k - 8), 2)
                    last = soft_part(par, bank, 2 * P, 4 * g + 2 * (k - 8) + 1, 2)
                last.then_inc(t_full, 1)

            def pv(s, par, g, stage):
                pe.wait_ge(exps, GROUPS * T_BANKS * s + T_BANKS * g + (4, 8, 10)[stage])
                if stage == 0:
                    pe.wait_ge(v_sb, 2 * s + 2)
                    if not (isinstance(s, int) and s == 0 and g < 2):
                        pe.wait_ge(ot_sb, GROUPS * s + g - 1)
                for kt in ((0,), (1, 3), (2,))[stage]:
                    for j in range(4):
                        slot, at = {0: (j, 0), 1: (4 + j, 0), 3: (4 + j, 3 * P), 2: (8 + j // 2, 2 * P * (j % 2))}[kt]
                        last = pe.matmul(PV[g % 2][32 * j:32 * j + 32, P * kt:T], Va[par][:, kt, :],
                                         prob[:, slot, at:at + T - P * kt], start=(kt == 0), stop=(kt == 2),
                                         skip_group_check=True)
                last.then_inc(pv_full, 1)

            def heads_rows(b, i, before):
                if i == 0:
                    pe.wait_ge(ot_sb, GROUPS * b + GROUPS)
                if i < 2:
                    before(i)
                else:
                    pe.wait_ge(on_s, QT * b + i - 1)
                transposes(M[i % 2], [oT[:, g, P * i:P * i + P] for g in range(GROUPS)], P, otr_full)

            def heads_back(b, k):
                pe.wait_ge(on_s, QT * b + QT)
                transposes(M[k], [on[:, i, P * k:P * k + P] for i in range(QT)], P, ott_full)

            def output(b, u):
                pe.wait_ge(ott_sb, KD * b + 2)
                for j in range(2):
                    for k in range(KD):
                        at = P * (2 * u + j)
                        last = pe.matmul(M[u][:, D * j:D * j + D], oT2[:, k, at:at + P], wo[:, k, :],
                                         start=(k == 0), stop=(k == KD - 1))
                last.then_inc(wo_full, 1)

            def router(b):
                pe.wait_ge(xt_sb[1], KD * b + 2)
                for i in range(QT):
                    for k in range(KD):
                        last = pe.matmul(M[0][:, E * i:E * i + E], xT[1][:, k, P * i:P * i + P], wr[:, k, :],
                                         start=(k == 0), stop=(k == KD - 1))
                last.then_inc(sc_full, 1)

            def ranks(b):
                pe.wait_ge(route, ROUTE * b + R_MASKS)
                pe.matmul(M[1][:, 0:QT * E], cstb[:, CB_U:CB_U + P], maskb[:, :, :].rearrange("p i e -> p (i e)"),
                          start=True, stop=False)
                pe.matmul(M[1][:, 0:QT * E], cstb[:, CB_ONE:CB_ONE + P], cumb[:, :, :].rearrange("p i e -> p (i e)"),
                          start=False, stop=True).then_inc(rank_full, 1)

            def prologue():
                pe.wait_ge(setup_in, 16 * NSETUP)
                pe.transpose(M[0][:, 0:NBIAS], brow[:, :], ident[0:NBIAS, 0:NBIAS]).then_inc(bias_row, 1)
                xT_of(0, 0, 0)
                xT_of(0, 0, 1)
                project(0)
                v_rows(0, False)
                for n in range(S_BANKS):
                    scores_bank(0, 0, n)

            def step(s, par, a, d, _):
                max_rows(s)
                if a:
                    xT_of(0, s + 1, 0)
                    xT_of(0, s + 1, 1)
                    project(s + 1)
                pe.wait_ge(m_in, 64 * s + 64)

                def before(i):
                    if a:
                        pe.wait_ge(qkv_sb, 3 * s + 3 + (2, 3)[i])
                    elif i == 0:
                        pe.wait_ge(mt_sb, s + 1)
                    else:
                        pe.wait_ge(v_sb, 2 * s + 2)

                for g in range(GROUPS):
                    for k in range(T_BANKS):
                        if d and (g, k) in ((0, 1), (0, 2), (0, 4), (0, 5)):
                            heads_rows(s - 1, (1, 2, 4, 5).index(k), before)
                        if d and (g, k) in ((0, 7), (0, 8)):
                            heads_back(s - 1, k - 7)
                        if d and (g, k) in ((1, 1), (1, 3)):
                            output(s - 1, k // 2)
                        if d and (g, k) in ((2, 2), (2, 3)):
                            xT_of(1, s - 1, k - 2)
                        if d and (g, k) == (2, 6):
                            router(s - 1)
                        if d and (g, k) == (3, 3):
                            ranks(s - 1)
                        if g and k in (0, 4, 8):
                            pv(s, par, g - 1, k // 4)
                        soft_bank(s, par, g, k)
                        if a:
                            for n in banks_of(g, k):
                                scores_bank(s + 1, 1 - par, n)
                if a:
                    v_rows(s + 1, d)
                for stage in range(3):
                    pv(s, par, GROUPS - 1, stage)

            def last():
                b = B - 1
                for i in range(QT):
                    heads_rows(b, i, lambda i: pe.wait_ge(route, ROUTE * (b - 1) + (R_SCORES, R_RANK)[i]))
                heads_back(b, 0)
                heads_back(b, 1)
                output(b, 0)
                output(b, 1)
                xT_of(1, b, 0)
                xT_of(1, b, 1)
                router(b)
                ranks(b)

            steps(pe, prologue, step, last)

            pe.wait_ge(table, 1)
            pe.matmul(M[0][:, 0:E], cstb[:, CB_ONE:CB_ONE + P], cumlast[:, :], start=True, stop=True)\
              .then_inc(tot_full, 1)
            pe.wait_ge(table, IDS_AT)
            pe.transpose(M[1][:, 0:MAX_BLOCKS], ids_f[:, :], ident[0:MAX_BLOCKS, 0:MAX_BLOCKS]).then_inc(slots_full, 1)
            pe.wait_ge(table, TABLE)

            def block_xT(t, par):
                pe.wait_ge(gath[par], 8 * (t - par) + 16)
                if not (isinstance(t, int) and t == 0):
                    pe.wait_ge(xgt_sb, t)
                transposes(M[0], [xg[par][:, P * k:P * k + P] for k in range(KD)], P, xgt_full)

            def layer1(t, par):
                e = pe.value_load(blk_expert[0:1, bass.ds(t, 1)], min_val=0, max_val=E - 1)
                pe.wait_ge(weights_ready, e + 1)
                pe.wait_ge(xgt_sb, t + 1)
                for c in range(2):
                    if not (isinstance(t, int) and t == 0):
                        pe.wait_ge((hs0, hs1)[c], t)
                    for k in range(KD):
                        last = pe.matmul(S[c][:, :], xgT[par][:, k, :],
                                         Wf[:, bass.ds(WE * e + F * k + 512 * c, 512)],
                                         start=(k == 0), stop=(k == KD - 1))
                    last.then_inc(f1_full, 1)

            def hidden_T(t):
                for c in range(2):
                    pe.wait_ge((hs0, hs1)[c], t + 1)
                    if not (isinstance(t, int) and t == 0):
                        pe.wait_ge(z_s, 2 * t)
                    transposes(TT[c], [hs[:, P * k:P * k + P] for k in range(4 * c, 4 * c + 4)], P, htr_full)

            def layer2(t, par):
                e = pe.value_load(blk_expert[0:1, bass.ds(t, 1)], min_val=0, max_val=E - 1)
                if not (isinstance(t, int) and t < 2):
                    pe.wait_ge(y_s, t - 1)
                for k in range(KF):
                    if k % 4 == 0:
                        pe.wait_ge(gelu_s, 2 * t + k // 4 + 1)
                    last = pe.matmul(PV[par][:, 0:D], hT[:, k, :],
                                     Wf[:, bass.ds(WE * e + KD * F + D * k, D)],
                                     start=(k == 0), stop=(k == KF - 1))
                last.then_inc(f2_full, 1)

            Wf = W[:, :, :].rearrange("p e w -> p (e w)")
            block_xT(0, 0)
            layer1(0, 0)

            def body(t, par, following):
                if following:
                    block_xT(t + 1, 1 - par)
                hidden_T(t)
                if following:
                    layer1(t + 1, 1 - par)
                layer2(t, par)

            blocks(pe, body)


_INS = ["L0_attn_x", "L0_attn_Wq", "L0_attn_bq", "L0_attn_Wk", "L0_attn_bk", "L0_attn_Wv", "L0_attn_bv",
        "L0_attn_Wo", "L0_attn_bo", "L0_ffn_W1", "L0_ffn_b1", "L0_ffn_W2", "L0_ffn_b2", "L0_ffn_Wr", "L0_ffn_br"]


def kernel(**inputs):
    import numpy as _np
    import concourse.bacc as _bacc
    from concourse import mybir as _mybir
    from concourse.bass_utils import run_bass_kernel_spmd as _run

    nc = _bacc.Bacc("TRN2", target_bir_lowering=False, num_devices=1)
    arrays, args = {}, []
    named = [(n, _np.ascontiguousarray(inputs[n])) for n in _INS]
    named += list(zip(("const", "constb", "rope"), constants()))
    for name, a in named:
        arrays[f"in_{name}"] = a
        args.append(nc.dram_tensor(f"in_{name}", a.shape, _mybir.dt.from_np(a.dtype), kind="ExternalInput").ap())
    args.append(nc.dram_tensor("out", (B, T, D), _mybir.dt.float32, kind="ExternalOutput").ap())
    layer(nc, *args)
    r = _run(nc, [arrays], core_ids=[0])
    return r.results[0]["out"]
```

```python
from contextlib import ExitStack

import numpy as np

import concourse.bass as bass
from concourse import mybir

F32 = mybir.dt.float32
F32R = mybir.dt.float32r
BF16 = mybir.dt.bfloat16
I32 = mybir.dt.int32
ALU = mybir.AluOpType
ACT = mybir.ActivationFunctionType
AX = mybir.AxisListType

P = 128
B, T, D = 8, 512, 256
H, HD = 16, 16
QT = T // P
KD = D // P
NT = B * QT
N = B * T
E, F = 8, 1024
KF = F // P
EPS = 1e-5
QSCALE = HD ** -0.5
PAIRS = H // 2
GROUPS = H // 4
BIG = -1e38

S_BANKS = 4 * (1 + 2 + 4 + 4)
QUARTER_BANKS = S_BANKS // 4
T_BANKS = 10

MAX_BLOCKS = (2 * N + E * (P - 1)) // P
LIST_ROWS = E * (N // P) + 1
PAD = 2 * N
WE = KD * F + KF * D

NBIAS = E * KF + KD + 1
EARLY = 1

PREP = 15
ROUTE = 32
R_SCORES, R_MASKS, R_DIFF, R_RANK = 1, 20, 21, 25
TABLE, ROWS_AT, IDS_AT = 24, 12, 17

C_ID, C_MA, C_MB, C_SA, C_SB, C_REV, C_BASE, C_CNT, C_BLK, C_COL, C_IDS = (
    0, 128, 129, 130, 131, 132, 140, 148, 180, 180 + MAX_BLOCKS, 181 + MAX_BLOCKS)
C_END = C_IDS + 2 * QT
CB_ID, CB_S, CB_T, CB_U, CB_ONE, CB_END = 0, 128, 256, 384, 512, 640


def constants():
    row = np.arange(P)
    c = np.zeros((P, C_END), np.float32)
    c[:, C_ID:C_ID + P] = np.eye(P)
    c[:96, C_MA] = (row[:96] % 32) < 16
    c[:96, C_MB] = (row[:96] % 32) >= 16
    c[:, C_SA:C_SB + 1] = c[:, C_MA:C_MB + 1]
    c[96:100, C_MA] = [1, 0, 1, 0]
    c[96:100, C_MB] = [0, 1, 0, 1]
    c[:, C_REV:C_REV + E] = E - np.arange(E)
    c[:, C_BASE:C_BASE + E] = N * np.arange(E)
    c[:, C_CNT:C_CNT + N // P] = P * np.arange(N // P)
    c[:, C_BLK:C_BLK + MAX_BLOCKS] = np.arange(MAX_BLOCKS)
    c[:, C_COL] = row
    c[:, C_IDS:C_END] = row[:, None] + (N * np.arange(2)[:, None] + P * np.arange(QT) - T).reshape(1, -1)
    b = np.zeros((P, CB_END), np.float32)
    b[:, CB_ID:CB_ID + P] = np.eye(P)
    b[:, CB_S:CB_S + P] = np.where(row[None, :] > row[:, None], BIG, 0)
    b[:, CB_T:CB_T + P] = np.where(row[:, None] > row[None, :], BIG, 0)
    b[:, CB_U:CB_U + P] = row[:, None] < row[None, :]
    b[:, CB_ONE:CB_ONE + P] = 1
    half = HD // 2
    theta = np.float32(10000.0) ** (-np.arange(half, dtype=np.float32) / np.float32(half))
    freqs = np.arange(T, dtype=np.float32)[:, None] * theta[None, :].astype(np.float32)
    cos, sin = np.cos(freqs).astype(np.float32).T, np.sin(freqs).astype(np.float32).T
    rope = np.zeros((P, 2, T), np.float32)
    for r in range(P):
        d = r % HD
        if d < half:
            rope[r, 0] = cos[d]
            rope[r, 1] = -sin[d] if d < half // 2 else sin[d]
        else:
            rope[r, 0] = 1
    return c, b, rope


def rotation():
    q = HD // 4
    return [i + q if i % HD < q else i - q if i % HD < 2 * q else i for i in range(32)]


def layer(nc, x, Wq, bq, Wk, bk, Wv, bv, Wo, bo, W1, b1, W2, b2, Wr, br, const, constb, rope, out):
    xn2_dram = nc.dram_tensor("xn2_rows", (N, D), F32, kind="Internal").ap()
    list_dram = nc.dram_tensor("expert_lists", (LIST_ROWS * P, 1), I32, kind="Internal").ap()
    y_dram = nc.dram_tensor("expert_rows", (2 * N, D), F32, kind="Internal").ap()

    with ExitStack() as ctx:
        def sem(name):
            return ctx.enter_context(nc.semaphore(name))

        def sb(name, shape, dt=F32, stack=ctx):
            return stack.enter_context(nc.sbuf_tensor(name, shape, dt))

        S = [ctx.enter_context(nc.psum_tensor(f"S{i}", [P, 512], F32)) for i in range(3)]
        TT = [ctx.enter_context(nc.psum_tensor(f"T{i}", [P, 512], F32)) for i in range(2)]
        PV = ctx.enter_context(nc.psum_tensor("PV", [P, 512], F32))
        M = [ctx.enter_context(nc.psum_tensor(f"M{i}", [P, 512], F32)) for i in range(2)]

        Y = [PV, S[2]]

        cst = sb("cst", [P, C_END])
        cstb = sb("cstb", [P, CB_END], BF16)
        ident = cst[:, C_ID:C_ID + P]
        identb = cstb[:, CB_ID:CB_ID + P]
        xres = sb("xres", [P, NT, D])
        gate = sb("gate", [P, 2, NT])
        biasT = sb("biasT", [P, NBIAS])
        blk_expert = sb("blk_expert", [P, MAX_BLOCKS], I32)
        slots = sb("slots", [P, MAX_BLOCKS], I32)
        slot_tok = sb("slot_tok", [P, MAX_BLOCKS], I32)
        b2b = sb("b2b", [P, E, D])

        ffn = ExitStack()
        W = sb("W", [P, E, WE], F32, ffn)
        slot_now = [sb(f"slot_now{i}", [P, 1], I32, ffn) for i in range(2)]
        tok_now = [sb(f"tok_now{i}", [P, 1], I32, ffn) for i in range(2)]
        xg = [sb(f"xg{i}", [P, D], F32, ffn) for i in range(2)]
        xgT = [sb(f"xgT{i}", [P, KD, P], F32, ffn) for i in range(2)]
        hs = sb("hs", [P, F], F32, ffn)
        hT = sb("hT", [P, KF, P], F32, ffn)
        yrow = [sb(f"yrow{i}", [P, D], F32, ffn) for i in range(2)]
        ffn.close()

        sb("early_experts", [P, EARLY, WE])
        ropes = sb("ropes", [P, 2, T])
        wq = sb("wq", [P, KD, D])
        wkv1 = sb("wkv1", [P, KD, 2 * HD])
        wkv = sb("wkv", [P, KD, P])
        wo = sb("wo", [P, KD, D])
        wr = sb("wr", [P, KD, E])
        bob = sb("bob", [P, D])
        brb = sb("brb", [P, E])
        brow = sb("brow", [NBIAS, P])
        padrows = sb("padrows", [P, LIST_ROWS], I32)
        minus_half = sb("minus_half", [P, QT])
        ones = sb("ones", [P, T])
        st = [sb(f"st{i}", [P, QT, 6]) for i in range(2)]
        mv = [sb(f"mv{i}", [P, QT, 2]) for i in range(2)]
        veps = [sb(f"veps{i}", [P, QT]) for i in range(2)]
        rstd = [sb(f"rstd{i}", [P, QT]) for i in range(2)]
        xh = [sb(f"xh{i}", [P, QT, D]) for i in range(2)]
        xT = [sb(f"xT{i}", [P, KD, T]) for i in range(2)]
        qraw = sb("qraw", [P, 3, T])
        qrot = sb("qrot", [P, 3, T])
        qhi = sb("qhi", [P, 2, T], F32R)
        qlo = sb("qlo", [P, 2, T], F32R)
        khl = sb("khl", [P, T], F32R)
        KK = [[sb(f"K{p}{s}", [P, T], F32R) for s in range(2)] for p in range(2)]
        KS = [sb(f"KS{s}", [P, T], F32R) for s in range(2)]
        QQ = [sb(f"Q{p}", [P, PAIRS, T], F32R) for p in range(2)]
        Va = [sb(f"V{p}", [P, QT, 32]) for p in range(2)]
        nmax = sb("nmax", [P, QT, H])
        nsplit = sb("nsplit", [P, QT, 2 * H], F32R)
        mT = sb("mT", [2 * H, T], F32R)
        prob = sb("prob", [P, T_BANKS, 512])
        oT = sb("oT", [P, GROUPS, T])
        rden = sb("rden", [P, QT, H])
        on = sb("on", [P, QT, D])
        oT2 = sb("oT2", [P, KD, T])
        sc = sb("sc", [P, QT, E])
        tmp = sb("tmp", [P, QT, E])
        oh = sb("oh", [P, 2, QT, E])
        top = sb("top", [P, 2, QT])
        first = sb("first", [P, QT])
        gex = sb("gex", [P, QT])
        gsum = sb("gsum", [P, QT])
        maskb = sb("maskb", [P, QT, E], BF16)
        cum = sb("cum", [P, QT + 1, E])
        cumb = sb("cumb", [P, QT, E], BF16)
        rank = sb("rank", [P, QT, E])
        posf = sb("posf", [P, 2, QT])
        pos = sb("pos", [P, 2, QT], I32)
        idf = sb("idf", [P, 2, QT])
        idi = sb("idi", [P, 2, QT], I32)
        cumlast = sb("cumlast", [P, E], BF16)
        tot = sb("tot", [P, E])
        over = sb("over", [P, E, N // P])
        nblk = sb("nblk", [P, E])
        ends = sb("ends", [P, E])
        zeros8 = sb("zeros8", [P, E])
        le = sb("le", [P, MAX_BLOCKS, E])
        lec = sb("lec", [P, E])
        lecn = sb("lecn", [P, E])
        colv = sb("colv", [P, 4])
        rowi = sb("rowi", [P, 1], I32)
        ids_r = sb("ids_r", [MAX_BLOCKS, P], I32)
        ids_f = sb("ids_f", [MAX_BLOCKS, P])
        sl_f = sb("sl_f", [P, MAX_BLOCKS])
        sl_g = sb("sl_g", [P, MAX_BLOCKS])
        blk_f = sb("blk_f", [P, MAX_BLOCKS])

        x_in = [sem(f"x_in{i}") for i in range(2)]
        setup_in = sem("setup_in")
        list_init = sem("list_init")
        weights_in = [sem(f"weights_in{e}") for e in range(E)]
        weights_ready = sem("weights_ready")
        prep = sem("prep")
        bias_row = sem("bias_row")
        stats = [sem("stats_ln1"), sem("stats_ln2")]
        aggr = [sem("aggr_ln1"), sem("aggr_ln2")]
        eps_in = [sem("eps_ln1"), sem("eps_ln2")]
        rstd_s = [sem("rstd_ln1"), sem("rstd_ln2")]
        xh_s = [sem("xh_ln1"), sem("xh_ln2")]
        xt_full = [sem("xt_full_ln1"), sem("xt_full_ln2")]
        xt_sb = [sem("xt_sb_ln1"), sem("xt_sb_ln2")]
        bo_added = sem("bo_added")
        qkv_full = sem("qkv_full")
        qkv_sb = sem("qkv_sb")
        shuffled = sem("shuffled")
        cos_mul = sem("cos_mul")
        sin_mul = sem("sin_mul")
        roped = sem("roped")
        hi_s = sem("hi_s")
        klo_s = sem("klo_s")
        ks_s = sem("ks_s")
        ka_s = sem("ka_s")
        q_zero = sem("q_zero")
        split_s = sem("split_s")
        stack_in = [sem(f"stack_in{u}") for u in range(4)]
        s_full = sem("s_full")
        s_max = sem("s_max")
        nsplit_s = sem("nsplit_s")
        mt_full = sem("mt_full")
        mt_sb = sem("mt_sb")
        m_in = sem("m_in")
        t_full = sem("t_full")
        exps = sem("exps")
        v_full = sem("v_full")
        v_sb = sem("v_sb")
        pv_full = sem("pv_full")
        ot_sb = sem("ot_sb")
        otr_full = sem("otr_full")
        rden_s = sem("rden_s")
        on_s = sem("on_s")
        ott_full = sem("ott_full")
        ott_sb = sem("ott_sb")
        wo_full = sem("wo_full")
        x2_s = sem("x2_s")
        xn2_out = sem("xn2_out")
        sc_full = sem("sc_full")
        gexp = sem("gexp")
        route = sem("route")
        rank_full = sem("rank_full")
        listed = sem("listed")
        table = sem("table")
        tot_full = sem("tot_full")
        rows_in = sem("rows_in")
        slots_full = sem("slots_full")
        now_s = sem("now_s")
        gath = [sem("gath0"), sem("gath1")]
        xgt_full = sem("xgt_full")
        xgt_sb = sem("xgt_sb")
        f1_full = sem("f1_full")
        hs0 = sem("hs0")
        hs1 = sem("hs1")
        htr_full = sem("htr_full")
        z_s = sem("z_s")
        gelu_s = sem("gelu_s")
        f2_full = sem("f2_full")
        y_s = sem("y_s")
        snow_s = sem("snow_s")
        scat = [sem("scat0"), sem("scat1")]
        y_in = [sem(f"y_in{c}") for c in range(B)]
        half_sum = sem("half_sum")
        sum_s = sem("sum_s")
        out_done = sem("out_done")
        settled = sem("settled")

        NSETUP = 20
        S_FIRST, S_SLOTS = 7, 30

        def steps(eng, prologue, step, last):
            prologue()
            step(0, 0, True, False, True)
            with eng.Fori(0, 2) as j:
                step(2 * j + 1, 1, True, True, True)
                step(2 * j + 2, 0, True, True, True)
            step(5, 1, True, True, True)
            step(6, 0, True, True, False)
            step(7, 1, False, True, False)
            last()

        def quarter_banks(u):
            for qt, nh in ((0, 4), (1, 2), (2, 1), (3, 1)):
                for h in range(4 * u, 4 * u + 4, nh):
                    yield qt, h, nh

        PARTS = ((0, 1), (2, 0), (1, 1))
        BANKS = [bank for u in range(4) for bank in quarter_banks(u)]

        def banks_of(g, k):
            at = T_BANKS * g + k - S_FIRST
            if at < 0:
                return range(0)
            return range(min(S_BANKS, S_BANKS * at // S_SLOTS), min(S_BANKS, S_BANKS * (at + 1) // S_SLOTS))

        def blocks(eng, body):
            body(0, 0, True)
            body(1, 1, True)
            with eng.Fori(1, (MAX_BLOCKS - 1) // 2) as j:
                body(2 * j, 0, True)
                body(2 * j + 1, 1, True)
            body(MAX_BLOCKS - 1, 0, False)

        def settle(eng, at):
            if not isinstance(at, int):
                eng.sem_inc(settled, 1)

        assert MAX_BLOCKS % 2 == 1 and S_BANKS % 2 == 0

        block = ctx.enter_context(nc.Block())

        @block.sync
        def _(sp):
            def load(dst, src):
                sp.dma_start(dst, src).then_inc(setup_in, 16)

            for b in range(B):
                if b == 2:
                    load(cst[:, :], const)
                    load(prob[:, 0:2, :].rearrange("p a n -> p (a n)")[:, 0:CB_END], constb)
                    load(wq[:, :, :], Wq.rearrange("(k p) n -> p k n", p=P))
                    load(wkv1[:, :, 0:HD], Wk.rearrange("(k p) n -> p k n", p=P))
                    load(wkv1[:, :, HD:2 * HD], Wv.rearrange("(k p) n -> p k n", p=P))
                    load(brow[0:E * KF, :], b1.rearrange("e (k p) -> (e k) p", p=P))
                    load(brow[E * KF:E * KF + KD, :], bq.rearrange("(k p) -> k p", p=P))
                    for r in range(6):
                        load(brow[NBIAS - 1:NBIAS, HD * r:HD * r + HD], bk.rearrange("(a n) -> a n", a=1))
                    for r in range(6, 8):
                        load(brow[NBIAS - 1:NBIAS, HD * r:HD * r + HD], bv.rearrange("(a n) -> a n", a=1))
                    load(ropes[:, :, :], rope)
                    load(wo[:, :, :], Wo.rearrange("(k p) n -> p k n", p=P))
                    load(wr[:, :, :], Wr.rearrange("(k p) n -> p k n", p=P))
                    load(bob[:, :], bo.partition_broadcast(P))
                    load(brb[:, :], br.partition_broadcast(P))
                if b >= 2:
                    sp.wait_ge(x_in[b % 2], 16 * (b // 2))
                sp.dma_start(xres[:, QT * b:QT * b + QT, :],
                             x[b].rearrange("(i p) d -> p i d", p=P)).then_inc(x_in[b % 2], 16)
            sp.wait_ge(prep, 1)
            sp.dma_start(list_dram.rearrange("(p n) a -> p (n a)", p=P), padrows[:, :]).then_inc(list_init, 16)

            def weights(e):
                sp.dma_start(W[:, e, 0:KD * F].rearrange("p (k n) -> p k n", k=KD),
                             W1[e].rearrange("(k p) n -> p k n", p=P)).then_inc(weights_in[e], 16)
                sp.dma_start(W[:, e, KD * F:WE].rearrange("p (k n) -> p k n", k=KF),
                             W2[e].rearrange("(k p) n -> p k n", p=P)).then_inc(weights_in[e], 16)

            def stack(b, par, t):
                sp.wait_ge(split_s, 3 * b + (1 if t == 0 else 3))
                for g in range(4):
                    pair = 4 * t + g
                    for part, src in ((0, qhi), (1, qhi), (2, qlo)):
                        sp.dma_start(QQ[par][32 * part:32 * part + 32, pair, :].bitcast(F32),
                                     src[32 * g:32 * g + 32, t, :].bitcast(F32)).then_inc(
                                           stack_in[pair // 2], 16)

            def prologue():
                stack(0, 0, 0)
                stack(0, 0, 1)
                sp.wait_ge(q_zero, 2)
                maxima_in(0, 0)
                for e in range(EARLY):
                    weights(e)
                sp.dma_start(b2b[:, :, :], b2.partition_broadcast(P)).then_inc(weights_in[0], 16)

            def maxima_in(b, par):
                sp.wait_ge(mt_sb, b + 1)
                for part in range(2):
                    for one in range(2):
                        at = H * part + one
                        sp.dma_start(QQ[par][96 + 2 * part + one:97 + 2 * part + one, :, :].bitcast(F32),
                                     mT[at:at + H - 1:2, :].bitcast(F32)).then_inc(m_in, 16)

            def step(s, par, a, d, _):
                if a:
                    stack(s + 1, 1 - par, 0)
                    stack(s + 1, 1 - par, 1)
                if d:
                    store(s - 1)
                if a:
                    maxima_in(s + 1, 1 - par)

            def store(b):
                sp.wait_ge(xh_s[1], QT * b + QT)
                sp.dma_start(xn2_dram[bass.ds(T * b, T), :].rearrange("(i p) d -> p i d", p=P),
                             xh[1][:, :, :]).then_inc(xn2_out, 16)

            steps(sp, prologue, step, lambda: store(B - 1))
            sp.wait_ge(table, TABLE)
            sp.wait_ge(xn2_out, 16 * B)
            for e in range(EARLY, E):
                weights(e)
            for e in range(E):
                sp.wait_ge(weights_in[e], 48 if e == 0 else 32)
                sp.sem_inc(weights_ready, 1)
            for i in range(2):
                sp.wait_ge(scat[i], 16 * ((MAX_BLOCKS + 1 - i) // 2))
            sp.wait_ge(f2_full, MAX_BLOCKS)
            yv = y_dram.rearrange("(c i p) d -> p c i d", p=P, c=2)
            for b in range(B):
                for c in range(2):
                    sp.dma_start(W[:, b // 2, 2048 * (b % 2) + 1024 * c:2048 * (b % 2) + 1024 * (c + 1)]
                                 .rearrange("p (i d) -> p i d", d=D),
                                 yv[:, c, QT * b:QT * b + QT, :]).then_inc(y_in[b], 16)
            for b in range(B):
                sp.wait_ge(sum_s, QT * b + QT)
                sp.dma_start(out[b].rearrange("(i p) d -> p i d", p=P),
                             xres[:, QT * b:QT * b + QT, :]).then_inc(out_done, 16)
            sp.wait_ge(out_done, 16 * B)

        @block.gpsimd
        def _(pool):
            def rsqrt(n, b):
                pool.wait_ge(eps_in[n], b + 1)
                pool.tensor_tensor(rstd[n][:, :], veps[n][:, :], minus_half[:, :], ALU.pow).then_inc(rstd_s[n], 1)

            def rope_one(b, i, t, rows):
                pool.wait_ge(shuffled, 3 * b + i + 1)
                raw = qraw[0:rows, t, :]
                pool.tensor_tensor(raw, raw, ropes[0:rows, 0, :], ALU.mult).then_inc(cos_mul, 1)

            def rope_all(b):
                rope_one(b, 0, 0, P)
                rope_one(b, 1, 2, 96)
                rope_one(b, 2, 1, P)

            def add_bo(b):
                pool.wait_ge(xh_s[0], QT * b + QT)
                xb = xres[:, bass.ds(QT * b, QT), :]
                pool.tensor_tensor(xb, xb, bob[:, :].unsqueeze(1).broadcast_to([P, QT, D]),
                                   ALU.add).then_inc(bo_added, 1)

            def scatter_ids(b):
                pool.wait_ge(route, ROUTE * b + ROUTE)
                settle(pool, b)
                for c in range(2):
                    for i in range(QT):
                        pool.indirect_dma_start(
                            out=list_dram[:, :], out_offset=bass.IndirectOffsetOnAxis(ap=pos[:, c, i:i + 1], axis=0),
                            in_=idi[:, c, i:i + 1], in_offset=None).then_inc(listed, 16)

            def prologue():
                for i, q in enumerate(QQ):
                    pool.memset(q[96:128, :, :].bitcast(F32), 0.0).then_inc(q_zero, 1)
                    pool.wait_ge(q_zero, i + 1)
                pool.wait_ge(prep, 2)
                rsqrt(0, 0)
                pool.wait_ge(setup_in, 16 * NSETUP)
                rsqrt(0, 1)
                rope_all(0)
                add_bo(0)
                pool.wait_ge(list_init, 16)

            def step(s, par, a, d, ln):
                if a:
                    rope_all(s + 1)
                    add_bo(s + 1)
                if d:
                    rsqrt(1, s - 1)
                if ln:
                    rsqrt(0, s + 2)
                if d:
                    scatter_ids(s - 1)

            def last():
                rsqrt(1, B - 1)
                scatter_ids(B - 1)

            steps(pool, prologue, step, last)
            pool.wait_ge(table, ROWS_AT)
            pool.wait_ge(listed, 16 * 2 * QT * B)
            pool.indirect_dma_start(
                out=ids_r[:, :], out_offset=None, in_=list_dram.rearrange("(r n) a -> r (n a)", n=P),
                in_offset=bass.IndirectOffsetOnAxis(ap=rowi[0:MAX_BLOCKS, 0:1], axis=0)).then_inc(rows_in, 16)
            pool.wait_ge(table, TABLE)
            pool.wait_ge(xn2_out, 16 * B)

            def gather(t, par, again):
                if again:
                    pool.wait_ge(gath[par], 8 * (t - par))
                    pool.wait_ge(xgt_full, t - 1)
                pool.tensor_copy(tok_now[par][:, :], slot_tok[:, bass.ds(t, 1)]).then_inc(now_s, 1)
                pool.wait_ge(now_s, t + 1)
                settle(pool, t)
                pool.indirect_dma_start(
                    out=xg[par][:, :], out_offset=None, in_=xn2_dram[:, :],
                    in_offset=bass.IndirectOffsetOnAxis(ap=tok_now[par][:, 0:1], axis=0)).then_inc(gath[par], 16)

            def scatter(t, par, again):
                if again:
                    pool.wait_ge(scat[par], 8 * (t - par))
                pool.tensor_copy(slot_now[par][:, :], slots[:, bass.ds(t, 1)]).then_inc(snow_s, 1)
                pool.wait_ge(y_s, t + 1)
                pool.wait_ge(snow_s, t + 1)
                settle(pool, t)
                pool.indirect_dma_start(
                    out=y_dram[:, :], out_offset=bass.IndirectOffsetOnAxis(ap=slot_now[par][:, 0:1], axis=0),
                    in_=yrow[par][:, :], in_offset=None, bounds_check=2 * N - 1,
                    oob_is_err=False).then_inc(scat[par], 16)

            for t in range(2):
                gather(t, t, False)
            for t in range(2):
                gather(t + 2, t, True)
                scatter(t, t, False)
            with pool.Fori(1, (MAX_BLOCKS - 3) // 2) as j:
                for par in range(2):
                    gather(2 * j + par + 2, par, True)
                    scatter(2 * j + par, par, True)
            gather(MAX_BLOCKS - 1, 0, True)
            for t in range(MAX_BLOCKS - 3, MAX_BLOCKS):
                scatter(t, t % 2, True)

        @block.scalar
        def _(act):
            def evac_xT(n, b, k):
                act.wait_ge(xt_full[n], KD * b + k + 1)
                if n == 0 and not (isinstance(b, int) and b == 0):
                    act.wait_ge(qkv_full, 3 * b)
                if n == 1 and not (isinstance(b, int) and b == 0):
                    act.wait_ge(sc_full, b)
                act.activation(xT[n][:, k, :], M[1 - k if n == 0 else k][:, :], ACT.Copy).then_inc(xt_sb[n], 1)

            def evac_qkv(b, i):
                t, bank = PARTS[i]
                act.wait_ge(qkv_full, 3 * b + i + 1)
                if not (isinstance(b, int) and b == 0):
                    act.wait_ge(split_s, 3 * b)
                    act.wait_ge(v_full, 2 * b)
                bias = biasT[:, E * KF + t:E * KF + t + 1]
                act.activation(qraw[:, t, :], M[bank][:, :], ACT.Identity, bias=bias,
                               scale=1.0 if t == 2 else QSCALE).then_inc(qkv_sb, 1)

            def evac_v(b, par):
                for u in range(2):
                    act.wait_ge(v_full, 2 * b + u + 1)
                    if not (isinstance(b, int) and b < 2):
                        act.wait_ge(pv_full, 3 * GROUPS * (b - 1))
                    act.activation(Va[par][:, 2 * u:2 * u + 2, 0:HD],
                                   M[u][:, 0:64].rearrange("p (i w) -> p i w", w=32)[:, :, 0:HD],
                                   ACT.Copy).then_inc(v_sb, 1)

            def exp_bank(s, g, k):
                stage = 0 if k < 4 else 1 if k < 8 else 2
                act.wait_ge(t_full, GROUPS * T_BANKS * s + T_BANKS * g + k + 1)
                if not (isinstance(s, int) and s == 0 and g == 0):
                    act.wait_ge(pv_full, 3 * GROUPS * s + 3 * g + stage - 2)
                act.activation(prob[:, k, :], TT[k % 2][:, :], ACT.Exp).then_inc(exps, 1)

            def evac_oT(s, g):
                act.wait_ge(pv_full, 3 * GROUPS * s + 3 * g + 3)
                if not (isinstance(s, int) and s == 0):
                    act.wait_ge(otr_full, QT * s)
                act.activation(oT[:, g, :], PV[:, :], ACT.Copy).then_inc(ot_sb, 1)

            def evac_oTT(b, k):
                act.wait_ge(ott_full, KD * b + k + 1)
                if not (isinstance(b, int) and b == 0):
                    act.wait_ge(wo_full, 2 * b)
                act.activation(oT2[:, k, :], M[k][:, :], ACT.Copy).then_inc(ott_sb, 1)

            def gate_exp(b):
                act.wait_ge(route, ROUTE * b + R_DIFF)
                act.activation(gex[:, :], gex[:, :], ACT.Exp).then_inc(gexp, 1)

            def prologue():
                act.wait_ge(prep, PREP)
                for k in range(KD):
                    evac_xT(0, 0, k)
                for i in range(3):
                    evac_qkv(0, i)
                evac_v(0, 0)
                evac_mT(0)

            def evac_mT(b):
                act.wait_ge(mt_full, b + 1)
                if not (isinstance(b, int) and b == 0):
                    act.wait_ge(m_in, 64 * b)
                act.activation(mT[:, :], M[0][0:2 * H, :], ACT.Copy).then_inc(mt_sb, 1)

            def step(s, par, a, d, _):
                if a:
                    evac_xT(0, s + 1, 0)
                    evac_xT(0, s + 1, 1)
                    evac_qkv(s + 1, 0)
                    evac_qkv(s + 1, 1)
                for g in range(GROUPS):
                    for k in range(T_BANKS):
                        exp_bank(s, g, k)
                        if a and (g, k) == (0, 0):
                            evac_qkv(s + 1, 2)
                        if g >= 1 and k == 8:
                            evac_oT(s, g - 1)
                        if d and (g, k) in ((0, 8), (0, 9)):
                            evac_oTT(s - 1, k - 8)
                        if d and (g, k) in ((2, 2), (2, 3)):
                            evac_xT(1, s - 1, k - 2)
                        if d and (g, k) == (3, 3):
                            gate_exp(s - 1)
                if a:
                    evac_v(s + 1, 1 - par)
                    evac_mT(s + 1)
                evac_oT(s, GROUPS - 1)

            def last():
                for k in range(KD):
                    evac_oTT(B - 1, k)
                for k in range(KD):
                    evac_xT(1, B - 1, k)
                gate_exp(B - 1)

            steps(act, prologue, step, last)

            def evac_xgT(t, par):
                act.wait_ge(xgt_full, t + 1)
                if not (isinstance(t, int) and t < 2):
                    act.wait_ge(f1_full, 2 * t - 2)
                act.activation(xgT[par][:, :, :], M[0][:, 0:D].rearrange("p (k n) -> p k n", k=KD),
                               ACT.Copy).then_inc(xgt_sb, 1)

            def evac_h1(t):
                act.wait_ge(f1_full, 2 * t + 2)
                if not (isinstance(t, int) and t == 0):
                    act.wait_ge(htr_full, 2 * t)
                act.activation(hs[:, 512:1024], S[1][:, :], ACT.Copy).then_inc(hs1, 1)

            act.wait_ge(table, TABLE)
            evac_xgT(0, 0)
            evac_h1(0)

            def body(t, par, following):
                if following:
                    evac_xgT(t + 1, 1 - par)
                for c in range(2):
                    act.wait_ge(z_s, 2 * t + c + 1)
                    half = hT[:, 4 * c:4 * c + 4, :]
                    act.activation(half, half, ACT.Gelu_apprx_tanh).then_inc(gelu_s, 1)
                if following:
                    evac_h1(t + 1)

            blocks(act, body)

        @block.vector
        def _(dve):
            def tile_of(b, i):
                return xres[:, bass.ds(QT * b + i, 1), :].rearrange("p a d -> p (a d)")

            def ln_stats(n, b, par, half):
                if n == 0 and half == 0:
                    dve.wait_ge(x_in[par], 8 * (b - par) + 16)
                    settle(dve, b)
                if n == 1:
                    dve.wait_ge(x2_s, 2 * b + half + 1)
                    settle(dve, b)
                for i in (2 * half, 2 * half + 1):
                    dve.bn_stats(st[n][:, i, :], tile_of(b, i)).then_inc(stats[n], 1)
                dve.wait_ge(stats[n], QT * b + 2 * half + 2)
                settle(dve, b)
                for i in (2 * half, 2 * half + 1):
                    dve.bn_aggr(mv[n][:, i, :], st[n][:, i, :]).then_inc(aggr[n], 1)
                if half:
                    dve.wait_ge(aggr[n], QT * b + QT)
                    dve.tensor_scalar(veps[n][:, :], mv[n][:, :, 1], EPS, None, ALU.add).then_inc(eps_in[n], 1)

            def ln_apply(n, b, half):
                if half == 0:
                    dve.wait_ge(rstd_s[n], b + 1)
                    if not (isinstance(b, int) and b == 0):
                        dve.wait_ge(xt_full[n], KD * b)
                        if n == 1:
                            dve.wait_ge(xn2_out, 16 * b)
                for i in (2 * half, 2 * half + 1):
                    dve.tensor_scalar(xh[n][:, i, :], tile_of(b, i),
                                      mv[n][:, i, 0:1], rstd[n][:, i:i + 1], ALU.subtract, ALU.mult)\
                       .then_inc(xh_s[n], 1)

            def shuffle_one(b, i, t):
                dve.wait_ge(qkv_sb, 3 * b + i + 1)
                settle(dve, b)
                dve.stream_shuffle(qrot[:, t, :], qraw[:, t, :], ROT).then_inc(shuffled, 1)

            def sin_one(b, i, t, rows):
                dve.wait_ge(shuffled, 3 * b + i + 1)
                rot = qrot[0:rows, t, :]
                dve.tensor_tensor(rot, rot, ropes[0:rows, 1, :], ALU.mult).then_inc(sin_mul, 1)

            def add_one(b, i, t, rows):
                dve.wait_ge(cos_mul, 3 * b + i + 1)
                dve.wait_ge(sin_mul, 3 * b + i + 1)
                dve.tensor_tensor(qraw[0:rows, t, :], qraw[0:rows, t, :], qrot[0:rows, t, :],
                                  ALU.add).then_inc(roped, 1)

            def heads_first(b):
                shuffle_one(b, 0, 0)
                sin_one(b, 0, 0, P)
                shuffle_one(b, 1, 2)
                sin_one(b, 1, 2, 96)
                add_one(b, 0, 0, P)
                split_q(b, 0, 0)

            def heads_keys(b, par):
                add_one(b, 1, 2, 96)
                split_k(b, par)

            def heads_second(b):
                shuffle_one(b, 2, 1)
                sin_one(b, 2, 1, P)
                add_one(b, 2, 1, P)
                split_q(b, 2, 1)

            def split_q(b, i, t):
                dve.wait_ge(roped, 3 * b + i + 1)
                if not (isinstance(b, int) and b == 0):
                    for u in (2 * t, 2 * t + 1):
                        dve.wait_ge(stack_in[u], 16 * 6 * b)
                dve.tensor_copy(qhi[:, t, :], qraw[:, t, :]).then_inc(hi_s, 1)
                dve.wait_ge(hi_s, 3 * b + i + 1)
                dve.tensor_tensor(qlo[:, t, :], qraw[:, t, :], qhi[:, t, :].bitcast(F32),
                                  ALU.subtract).then_inc(split_s, 1)

            def split_k(b, par):
                dve.wait_ge(roped, 3 * b + 2)
                dve.tensor_copy(khl[0:96, :], qraw[0:96, 2, :]).then_inc(hi_s, 1)
                dve.wait_ge(hi_s, 3 * b + 2)
                dve.tensor_tensor(khl[32:64, :], qraw[32:64, 2, :], khl[32:64, :].bitcast(F32),
                                  ALU.subtract).then_inc(klo_s, 1)
                dve.wait_ge(klo_s, b + 1)
                if not (isinstance(b, int) and b < 2):
                    dve.wait_ge(t_full, GROUPS * T_BANKS * (b - 1))
                for one in range(2):
                    dve.tensor_scalar(KS[one][:, :], khl[:, :].bitcast(F32), cst[:, C_SA + one:C_SA + one + 1], None,
                                      ALU.mult).then_inc(ks_s, 1)
                dve.tensor_scalar(KK[par][0][:, :], khl[:, :].bitcast(F32), cst[:, C_MA:C_MA + 1], None,
                                  ALU.mult).then_inc(ka_s, 1)
                dve.tensor_scalar(KK[par][1][:, :], khl[:, :].bitcast(F32), cst[:, C_MB:C_MB + 1], None,
                                  ALU.mult).then_inc(split_s, 1)

            def maxima(b, n):
                qt, h, nh = BANKS[n]
                w = P * (qt + 1)
                dve.wait_ge(s_full, S_BANKS * b + n + 1)
                dve.tensor_reduce(nmax[:, qt, h:h + nh], S[n % 3][:, 0:nh * w].rearrange("p (h w) -> p h w", h=nh),
                                  AX.X, ALU.max, negate=True).then_inc(s_max, 1)

            def split_maxima(b):
                dve.wait_ge(s_max, S_BANKS * b + S_BANKS)
                if not (isinstance(b, int) and b == 0):
                    dve.wait_ge(mt_full, b)
                dve.tensor_copy(nsplit[:, :, 0:H], nmax[:, :, :]).then_inc(nsplit_s, 1)
                dve.wait_ge(nsplit_s, 2 * b + 1)
                dve.tensor_tensor(nsplit[:, :, H:2 * H], nmax[:, :, :], nsplit[:, :, 0:H].bitcast(F32),
                                  ALU.subtract).then_inc(nsplit_s, 1)

            def normalise(b, i):
                bank = M[i % 2][:, :].rearrange("p (h w) -> p h w", w=32)
                dve.wait_ge(otr_full, QT * b + i + 1)
                dve.reciprocal(rden[:, i, :], bank[:, :, HD]).then_inc(rden_s, 1)
                dve.wait_ge(rden_s, QT * b + i + 1)
                if not (isinstance(b, int) and b == 0):
                    dve.wait_ge(ott_full, KD * b)
                dve.tensor_tensor(on[:, i, :].rearrange("p (h d) -> p h d", d=HD), bank[:, :, 0:HD],
                                  rden[:, i, :].unsqueeze(2).broadcast_to([P, H, HD]), ALU.mult).then_inc(on_s, 1)

            def residual(b, u):
                dve.wait_ge(wo_full, 2 * b + u + 1)
                dve.wait_ge(bo_added, b + 1)
                two = xres[:, bass.ds(QT * b + 2 * u, 2), :]
                dve.tensor_tensor(two, M[u][:, :].rearrange("p (i d) -> p i d", i=2), two, ALU.add)\
                   .then_inc(x2_s, 1)

            def over_experts(ap):
                return ap.unsqueeze(2).broadcast_to([P, QT, E])

            def over_tiles(at):
                return cst[:, at:at + E].unsqueeze(1).broadcast_to([P, QT, E])

            def after(b, n):
                dve.wait_ge(route, ROUTE * b + n)

            def route_first(b):
                dve.wait_ge(sc_full, b + 1)
                dve.tensor_tensor(sc[:, :, :], M[0][:, 0:QT * E].rearrange("p (i e) -> p i e", e=E),
                                  brb[:, :].unsqueeze(1).broadcast_to([P, QT, E]), ALU.add).then_inc(route, 1)
                after(b, 1)
                dve.tensor_reduce(top[:, 0, :], sc[:, :, :], AX.X, ALU.max).then_inc(route, 1)
                after(b, 2)
                dve.tensor_tensor(tmp[:, :, :], sc[:, :, :], over_experts(top[:, 0, :]), ALU.is_equal).then_inc(route, 1)
                after(b, 3)
                dve.tensor_tensor(tmp[:, :, :], tmp[:, :, :], over_tiles(C_REV), ALU.mult).then_inc(route, 1)

            def route_first_end(b):
                after(b, 4)
                dve.tensor_reduce(first[:, :], tmp[:, :, :], AX.X, ALU.max).then_inc(route, 1)
                after(b, 5)
                dve.tensor_tensor(oh[:, 0, :, :], tmp[:, :, :], over_experts(first[:, :]), ALU.is_equal)\
                   .then_inc(route, 1)

            def route_second(b):
                after(b, 6)
                dve.scalar_tensor_tensor(out=tmp[:, :, :], in0=oh[:, 0, :, :], scalar=-3e38, in1=sc[:, :, :],
                                         op0=ALU.mult, op1=ALU.add).then_inc(route, 1)
                after(b, 7)
                dve.tensor_reduce(top[:, 1, :], tmp[:, :, :], AX.X, ALU.max).then_inc(route, 1)
                after(b, 8)
                dve.tensor_tensor(tmp[:, :, :], tmp[:, :, :], over_experts(top[:, 1, :]), ALU.is_equal).then_inc(route, 1)
                after(b, 9)
                dve.tensor_tensor(tmp[:, :, :], tmp[:, :, :], over_tiles(C_REV), ALU.mult).then_inc(route, 1)

            def route_second_end(b):
                after(b, 10)
                dve.tensor_reduce(first[:, :], tmp[:, :, :], AX.X, ALU.max).then_inc(route, 1)
                after(b, 11)
                dve.tensor_tensor(oh[:, 1, :, :], tmp[:, :, :], over_experts(first[:, :]), ALU.is_equal)\
                   .then_inc(route, 1)
                after(b, 12)
                dve.tensor_tensor(tmp[:, :, :], oh[:, 0, :, :], oh[:, 1, :, :], ALU.add).then_inc(route, 1)

            def route_counts(b):
                after(b, 13)
                if not (isinstance(b, int) and b == 0):
                    dve.wait_ge(rank_full, b)
                dve.tensor_copy(maskb[:, :, :], tmp[:, :, :]).then_inc(route, 1)
                for i in range(QT):
                    if i:
                        after(b, 14 + i)
                    dve.tensor_tensor(cum[:, i + 1, :], cum[:, i, :], tmp[:, i, :], ALU.add).then_inc(route, 1)
                after(b, 18)
                dve.tensor_copy(cumb[:, :, :], cum[:, 0:QT, :]).then_inc(route, 1)
                after(b, 19)
                dve.tensor_copy(cum[:, 0, :], cum[:, QT, :]).then_inc(route, 1)
                if not (isinstance(b, int) and b == 0):
                    dve.wait_ge(gexp, b)
                dve.tensor_tensor(gex[:, :], top[:, 1, :], top[:, 0, :], ALU.subtract).then_inc(route, 1)

            def route_gates(b):
                dve.wait_ge(gexp, b + 1)
                dve.tensor_scalar(gsum[:, :], gex[:, :], 1.0, None, ALU.add).then_inc(route, 1)
                after(b, 22)
                dve.reciprocal(gate[:, 0, bass.ds(QT * b, QT)], gsum[:, :]).then_inc(route, 1)
                after(b, 23)
                dve.tensor_tensor(gate[:, 1, bass.ds(QT * b, QT)], gex[:, :], gate[:, 0, bass.ds(QT * b, QT)],
                                  ALU.mult).then_inc(route, 1)

            def route_places(b):
                dve.wait_ge(rank_full, b + 1)
                dve.tensor_tensor(rank[:, :, :], M[1][:, 0:QT * E].rearrange("p (i e) -> p i e", e=E),
                                  over_tiles(C_BASE), ALU.add).then_inc(route, 1)
                for c in range(2):
                    after(b, 25 + 2 * c)
                    dve.tensor_tensor(tmp[:, :, :], oh[:, c, :, :], rank[:, :, :], ALU.mult).then_inc(route, 1)
                    after(b, 26 + 2 * c)
                    dve.tensor_reduce(posf[:, c, :], tmp[:, :, :], AX.X, ALU.add).then_inc(route, 1)
                after(b, 29)
                if not (isinstance(b, int) and b == 0):
                    dve.wait_ge(listed, 16 * 2 * QT * b)
                dve.tensor_copy(pos[:, :, :], posf[:, :, :]).then_inc(route, 1)
                dve.tensor_scalar(idf[:, :, :], idf[:, :, :], float(T), None, ALU.add).then_inc(route, 1)
                after(b, 31)
                dve.tensor_copy(idi[:, :, :], idf[:, :, :]).then_inc(route, 1)

            def prologue():
                dve.memset(padrows[:, :], PAD).then_inc(prep, 1)
                dve.memset(minus_half[:, :], -0.5).then_inc(prep, 1)
                dve.memset(ones[:, :], 1.0).then_inc(prep, 1)
                for v in Va:
                    dve.memset(v[:, :, HD:32], 1.0).then_inc(prep, 1)
                dve.memset(zeros8[:, :], 0.0).then_inc(prep, 1)
                dve.memset(cum[:, 0, :], 0.0).then_inc(prep, 1)
                dve.wait_ge(prep, 3)
                dve.tensor_copy(khl[96:128, :], ones[96:128, :]).then_inc(prep, 1)
                ln_stats(0, 0, 0, 0)
                ln_stats(0, 0, 0, 1)
                ln_apply(0, 0, 0)
                ln_apply(0, 0, 1)
                dve.wait_ge(setup_in, 16 * NSETUP)
                dve.tensor_copy(cstb[:, :], prob[:, 0:2, :].rearrange("p a n -> p (a n)")[:, 0:CB_END])\
                   .then_inc(prep, 1)
                dve.tensor_copy(wkv[:, :, 0:96].rearrange("p k (r d) -> p k r d", d=HD),
                                wkv1[:, :, 0:HD].unsqueeze(2).broadcast_to([P, KD, 6, HD])).then_inc(prep, 1)
                dve.tensor_copy(wkv[:, :, 96:128].rearrange("p k (r d) -> p k r d", d=HD),
                                wkv1[:, :, HD:2 * HD].unsqueeze(2).broadcast_to([P, KD, 2, HD])).then_inc(prep, 1)
                dve.tensor_copy(idf[:, :, :], cst[:, C_IDS:C_END].rearrange("p (c i) -> p c i", c=2)).then_inc(prep, 1)
                dve.wait_ge(bias_row, 1)
                at = E * KF
                dve.tensor_copy(biasT[:, 0:at], M[0][:, 0:at]).then_inc(prep, 1)
                dve.tensor_scalar(biasT[:, at:at + KD], M[0][:, at:at + KD], QSCALE, None, ALU.mult).then_inc(prep, 1)
                dve.tensor_copy(biasT[:, at + KD:NBIAS], M[0][:, at + KD:NBIAS]).then_inc(prep, 1)
                ln_stats(0, 1, 1, 0)
                ln_stats(0, 1, 1, 1)
                heads_first(0)
                heads_keys(0, 0)
                heads_second(0)
                ln_apply(0, 1, 0)
                ln_apply(0, 1, 1)
                for n in range(S_BANKS):
                    maxima(0, n)
                split_maxima(0)

            def step(s, par, a, d, ln):
                if a:
                    heads_first(s + 1)
                if d:
                    normalise(s - 1, 0)
                    normalise(s - 1, 1)
                if a:
                    heads_keys(s + 1, 1 - par)
                if d:
                    normalise(s - 1, 2)
                    normalise(s - 1, 3)
                if a:
                    heads_second(s + 1)
                for g in range(GROUPS):
                    for k in range(T_BANKS):
                        if a:
                            for n in banks_of(g, k):
                                maxima(s + 1, n)
                        if d and (g, k) in ((1, 2), (1, 3)):
                            residual(s - 1, k - 2)
                            ln_stats(1, s - 1, 1 - par, k - 2)
                        if d and (g, k) in ((1, 6), (1, 7)):
                            ln_apply(1, s - 1, k - 6)
                        if d and (g, k) == (2, 6):
                            route_first(s - 1)
                        if d and (g, k) == (2, 7):
                            route_first_end(s - 1)
                        if d and (g, k) == (2, 8):
                            route_second(s - 1)
                        if d and (g, k) == (2, 9):
                            route_second_end(s - 1)
                        if d and (g, k) == (3, 0):
                            route_counts(s - 1)
                        if d and (g, k) == (3, 5):
                            route_gates(s - 1)
                        if d and (g, k) == (3, 6):
                            route_places(s - 1)
                        if ln and (g, k) in ((3, 1), (3, 2)):
                            ln_stats(0, s + 2, par, k - 1)
                if a:
                    split_maxima(s + 1)
                if ln:
                    ln_apply(0, s + 2, 0)
                    ln_apply(0, s + 2, 1)

            def last():
                b = B - 1
                for i in range(QT):
                    normalise(b, i)
                residual(b, 0)
                residual(b, 1)
                ln_stats(1, b, b % 2, 0)
                ln_stats(1, b, b % 2, 1)
                ln_apply(1, b, 0)
                ln_apply(1, b, 1)
                route_first(b)
                route_first_end(b)
                route_second(b)
                route_second_end(b)
                route_counts(b)
                route_gates(b)
                route_places(b)

            ROT = rotation()
            steps(dve, prologue, step, last)

            def did(n):
                dve.wait_ge(table, n)

            dve.wait_ge(route, ROUTE * B)
            dve.tensor_copy(cumlast[:, :], cum[:, 0, :]).then_inc(table, 1)
            dve.wait_ge(tot_full, 1)
            dve.tensor_copy(tot[:, :], M[0][:, 0:E]).then_inc(table, 1)
            did(2)
            dve.tensor_tensor(over[:, :, :], tot[:, :].unsqueeze(2).broadcast_to([P, E, N // P]),
                              cst[:, C_CNT:C_CNT + N // P].unsqueeze(1).broadcast_to([P, E, N // P]),
                              ALU.is_gt).then_inc(table, 1)
            did(3)
            dve.tensor_reduce(nblk[:, :], over[:, :, :], AX.X, ALU.add).then_inc(table, 1)
            did(4)
            dve.tensor_tensor_scan(ends[:, :], nblk[:, :], zeros8[:, :], 0.0, ALU.add, ALU.add).then_inc(table, 1)
            did(5)
            dve.tensor_scalar(lec[:, :], ends[:, :], cst[:, C_COL:C_COL + 1], None, ALU.is_le).then_inc(table, 1)
            did(6)
            dve.tensor_reduce(colv[:, 0:1], lec[:, :], AX.X, ALU.add).then_inc(table, 1)
            dve.tensor_tensor(lecn[:, :], lec[:, :], nblk[:, :], ALU.mult).then_inc(table, 1)
            did(8)
            dve.tensor_reduce(colv[:, 1:2], lecn[:, :], AX.X, ALU.add).then_inc(table, 1)
            did(9)
            dve.scalar_tensor_tensor(out=colv[:, 2:3], in0=colv[:, 0:1], scalar=float(N // P),
                                     in1=cst[:, C_COL:C_COL + 1], op0=ALU.mult, op1=ALU.add).then_inc(table, 1)
            did(10)
            dve.tensor_tensor(colv[:, 3:4], colv[:, 2:3], colv[:, 1:2], ALU.subtract).then_inc(table, 1)
            did(11)
            dve.tensor_scalar(rowi[:, :], colv[:, 3:4], float(LIST_ROWS - 1), None, ALU.min).then_inc(table, 1)
            dve.tensor_tensor(le[:, :, :], ends[:, :].unsqueeze(1).broadcast_to([P, MAX_BLOCKS, E]),
                              cst[:, C_BLK:C_BLK + MAX_BLOCKS].unsqueeze(2).broadcast_to([P, MAX_BLOCKS, E]),
                              ALU.is_le).then_inc(table, 1)
            did(13)
            dve.tensor_reduce(blk_f[:, :], le[:, :, :], AX.X, ALU.add).then_inc(table, 1)
            did(14)
            dve.tensor_scalar(blk_f[:, :], blk_f[:, :], float(E - 1), None, ALU.min).then_inc(table, 1)
            did(15)
            dve.tensor_copy(blk_expert[:, :], blk_f[:, :]).then_inc(table, 1)
            dve.wait_ge(rows_in, 16)
            dve.tensor_copy(ids_f[:, :], ids_r[:, :]).then_inc(table, 1)
            dve.wait_ge(slots_full, 1)
            dve.tensor_copy(sl_f[:, :], M[1][:, 0:MAX_BLOCKS]).then_inc(table, 1)
            did(18)
            dve.tensor_copy(slots[:, :], sl_f[:, :]).then_inc(table, 1)
            for n in (19, 21):
                did(n)
                dve.tensor_scalar(sl_g[:, :], sl_f[:, :], float(N), -float(N), ALU.is_ge, ALU.mult).then_inc(table, 1)
                did(n + 1)
                dve.tensor_tensor(sl_f[:, :], sl_f[:, :], sl_g[:, :], ALU.add).then_inc(table, 1)
            did(23)
            dve.tensor_copy(slot_tok[:, :], sl_f[:, :]).then_inc(table, 1)
            did(TABLE)

            def evac_h0(t):
                dve.wait_ge(f1_full, 2 * t + 1)
                if not (isinstance(t, int) and t == 0):
                    dve.wait_ge(htr_full, 2 * t)
                dve.tensor_copy(hs[:, 0:512], S[0][:, :]).then_inc(hs0, 1)

            evac_h0(0)

            def body(t, par, following):
                e = dve.value_load(blk_expert[0:1, bass.ds(t, 1)], min_val=0, max_val=E - 1)
                for c in range(2):
                    dve.wait_ge(htr_full, 2 * t + c + 1)
                    if not (isinstance(t, int) and t == 0):
                        dve.wait_ge(f2_full, t)
                    dve.tensor_tensor(hT[:, 4 * c:4 * c + 4, :], TT[c][:, :].rearrange("p (k n) -> p k n", n=P),
                                      biasT[:, bass.ds(KF * e + 4 * c, 4)].unsqueeze(2).broadcast_to([P, 4, P]),
                                      ALU.add).then_inc(z_s, 1)
                if following:
                    evac_h0(t + 1)
                dve.wait_ge(f2_full, t + 1)
                if not (isinstance(t, int) and t < 2):
                    dve.wait_ge(scat[par], 8 * (t - par))
                dve.tensor_tensor(yrow[par][:, :], Y[par][:, 0:D], b2b[:, bass.ds(e, 1), :].rearrange("p a d -> p (a d)"),
                                  ALU.add).then_inc(y_s, 1)

            blocks(dve, body)

            for b in range(B):
                dve.wait_ge(y_in[b], 32)
                yb = W[:, b // 2, 2048 * (b % 2):2048 * (b % 2) + 2048].rearrange("p (c i d) -> p c i d", c=2, d=D)
                for c, done in ((0, half_sum), (1, sum_s)):
                    for i in range(QT):
                        t = QT * b + i
                        if c:
                            dve.wait_ge(half_sum, t + 1)
                        dve.scalar_tensor_tensor(out=xres[:, t, :], in0=yb[:, c, i, :], scalar=gate[:, c, t:t + 1],
                                                 in1=xres[:, t, :], op0=ALU.mult, op1=ALU.add).then_inc(done, 1)

        @block.tensor
        def _(pe):
            def transposes(dst, srcs, width, done):
                for i, src in enumerate(srcs):
                    last = pe.transpose(dst[:, width * i:width * i + width], src, ident)
                last.then_inc(done, 1)

            def xT_of(n, b, k):
                pe.wait_ge(xh_s[n], QT * b + QT)
                if n == 1:
                    if k == 0:
                        pe.wait_ge(x2_s, 2 * b + 1)
                    else:
                        pe.wait_ge(x2_s, 2 * b + 2)
                    bank = M[k]
                else:
                    if isinstance(b, int) and b == 0:
                        pe.wait_ge(prep, PREP)
                    elif k == 0:
                        pe.wait_ge(v_sb, 2 * b)
                    else:
                        pe.wait_ge(mt_sb, b)
                    bank = M[1 - k]
                transposes(bank, [xh[n][:, i, P * k:P * k + P] for i in range(QT)], P, xt_full[n])

            def project(b, i):
                t, bank = PARTS[i]
                if i == 0:
                    pe.wait_ge(xt_sb[0], KD * b + 2)
                if i == 2:
                    pe.wait_ge(qkv_sb, 3 * b + 1)
                for k in range(KD):
                    w = wkv[:, k, :] if t == 2 else wq[:, k, P * t:P * t + P]
                    last = pe.matmul(M[bank][:, :], w, xT[0][:, k, :], start=(k == 0), stop=(k == KD - 1))
                last.then_inc(qkv_full, 1)

            def v_rows(b, d):
                pe.wait_ge(qkv_sb, 3 * b + 3)
                settle(pe, b)
                for u in range(2):
                    if d:
                        pe.wait_ge(route, ROUTE * (b - 2) + (R_SCORES, R_RANK)[u])
                        settle(pe, b)
                    for i in range(2):
                        at = P * (2 * u + i)
                        last = pe.transpose(M[u][:, 32 * i:32 * i + 32], qraw[96:128, 2, at:at + P],
                                            ident[96:128, 96:128])
                    last.then_inc(v_full, 1)

            def scores_bank(b, par, n):
                qt, h0, nh = BANKS[n]
                if n == 0:
                    pe.wait_ge(split_s, 3 * b + 2)
                if n % QUARTER_BANKS == 0:
                    pe.wait_ge(stack_in[n // QUARTER_BANKS], 16 * 6 * b + 16 * 6)
                if not (isinstance(b, int) and b == 0 and n < 3):
                    pe.wait_ge(s_max, S_BANKS * b + n - (1 if n < 2 else 2))
                w = P * (qt + 1)
                for i in range(nh):
                    h = h0 + i
                    pe.matmul(S[n % 3][:, w * i:w * i + w], QQ[par][:, h // 2, P * qt:P * qt + P],
                              KS[h % 2][:, 0:w], start=True, stop=True)
                    last = pe.matmul(S[n % 3][:, w * i + P * qt:w * i + w], identb, cstb[:, CB_S:CB_S + P],
                                     start=False, stop=True, skip_group_check=True)
                last.then_inc(s_full, 1)

            def max_rows(b):
                pe.wait_ge(nsplit_s, 2 * b + 2)
                pe.wait_ge(v_sb, 2 * b + 1)
                for i in range(QT):
                    last = pe.transpose(M[0][0:2 * H, P * i:P * i + P], nsplit[:, i, :].bitcast(F32), ident)
                last.then_inc(mt_full, 1)

            def soft_part(par, bank, at, h, kt):
                w = T - P * kt
                pe.matmul(bank[:, at:at + w], KK[par][h % 2][:, P * kt:P * kt + P],
                          QQ[par][:, h // 2, P * kt:T], start=True, stop=True)
                return pe.matmul(bank[:, at:at + P], identb, cstb[:, CB_T:CB_T + P],
                                 start=False, stop=True, skip_group_check=True)

            def soft_bank(s, par, g, k):
                n = T_BANKS * g + k
                if not (isinstance(s, int) and s == 0 and n < 2):
                    pe.wait_ge(exps, GROUPS * T_BANKS * s + n - 1)
                bank = TT[k % 2]
                if k < 4:
                    last = soft_part(par, bank, 0, 4 * g + k, 0)
                elif k < 8:
                    soft_part(par, bank, 0, 4 * g + k - 4, 1)
                    last = soft_part(par, bank, 3 * P, 4 * g + k - 4, 3)
                else:
                    soft_part(par, bank, 0, 4 * g + 2 * (k - 8), 2)
                    last = soft_part(par, bank, 2 * P, 4 * g + 2 * (k - 8) + 1, 2)
                last.then_inc(t_full, 1)

            def pv(s, par, g, stage):
                pe.wait_ge(exps, GROUPS * T_BANKS * s + T_BANKS * g + (4, 8, 10)[stage])
                if stage == 0:
                    pe.wait_ge(v_sb, 2 * s + 2)
                    if not (isinstance(s, int) and s == 0 and g == 0):
                        pe.wait_ge(ot_sb, GROUPS * s + g)
                for kt in ((0,), (1, 3), (2,))[stage]:
                    for j in range(4):
                        slot, at = {0: (j, 0), 1: (4 + j, 0), 3: (4 + j, 3 * P), 2: (8 + j // 2, 2 * P * (j % 2))}[kt]
                        last = pe.matmul(PV[32 * j:32 * j + 32, P * kt:T], Va[par][:, kt, :],
                                         prob[:, slot, at:at + T - P * kt], start=(kt == 0), stop=(kt == 2),
                                         skip_group_check=True)
                last.then_inc(pv_full, 1)

            def heads_rows(b, i, before):
                if i == 0:
                    pe.wait_ge(ot_sb, GROUPS * b + GROUPS)
                if i < 2:
                    before(i)
                else:
                    pe.wait_ge(on_s, QT * b + i - 1)
                transposes(M[i % 2], [oT[:, g, P * i:P * i + P] for g in range(GROUPS)], P, otr_full)

            def heads_back(b, k):
                pe.wait_ge(on_s, QT * b + QT)
                transposes(M[k], [on[:, i, P * k:P * k + P] for i in range(QT)], P, ott_full)

            def output(b, u):
                pe.wait_ge(ott_sb, KD * b + 2)
                for j in range(2):
                    for k in range(KD):
                        at = P * (2 * u + j)
                        last = pe.matmul(M[u][:, D * j:D * j + D], oT2[:, k, at:at + P], wo[:, k, :],
                                         start=(k == 0), stop=(k == KD - 1))
                last.then_inc(wo_full, 1)

            def router(b):
                pe.wait_ge(xt_sb[1], KD * b + 2)
                for i in range(QT):
                    for k in range(KD):
                        last = pe.matmul(M[0][:, E * i:E * i + E], xT[1][:, k, P * i:P * i + P], wr[:, k, :],
                                         start=(k == 0), stop=(k == KD - 1))
                last.then_inc(sc_full, 1)

            def ranks(b):
                pe.wait_ge(route, ROUTE * b + R_MASKS)
                pe.matmul(M[1][:, 0:QT * E], cstb[:, CB_U:CB_U + P], maskb[:, :, :].rearrange("p i e -> p (i e)"),
                          start=True, stop=False)
                pe.matmul(M[1][:, 0:QT * E], cstb[:, CB_ONE:CB_ONE + P], cumb[:, :, :].rearrange("p i e -> p (i e)"),
                          start=False, stop=True).then_inc(rank_full, 1)

            def prologue():
                pe.wait_ge(setup_in, 16 * NSETUP)
                pe.wait_ge(q_zero, 2)
                pe.transpose(M[0][:, 0:NBIAS], brow[:, :], ident[0:NBIAS, 0:NBIAS]).then_inc(bias_row, 1)
                xT_of(0, 0, 0)
                xT_of(0, 0, 1)
                for i in range(3):
                    project(0, i)
                v_rows(0, False)
                for n in range(S_BANKS):
                    scores_bank(0, 0, n)
                max_rows(0)

            def step(s, par, a, d, _):
                if a:
                    xT_of(0, s + 1, 0)
                    xT_of(0, s + 1, 1)
                    project(s + 1, 0)
                    project(s + 1, 1)
                pe.wait_ge(m_in, 64 * s + 64)

                def before(i):
                    if a:
                        pe.wait_ge(qkv_sb, 3 * s + 3 + (2, 3)[i])
                    elif i == 0:
                        pe.wait_ge(mt_sb, s + 1)
                    else:
                        pe.wait_ge(v_sb, 2 * s + 2)

                for g in range(GROUPS):
                    for k in range(T_BANKS):
                        if a and (g, k) == (0, 1):
                            project(s + 1, 2)
                        if d and (g, k) in ((0, 2), (0, 3), (0, 5), (0, 6)):
                            heads_rows(s - 1, (2, 3, 5, 6).index(k), before)
                        if d and (g, k) in ((0, 8), (0, 9)):
                            heads_back(s - 1, k - 8)
                        if d and (g, k) in ((1, 1), (1, 2)):
                            output(s - 1, k - 1)
                        if d and (g, k) in ((2, 1), (2, 2)):
                            xT_of(1, s - 1, k - 1)
                        if d and (g, k) == (2, 5):
                            router(s - 1)
                        if d and (g, k) == (3, 3):
                            ranks(s - 1)
                        if g and k in (0, 4, 8):
                            pv(s, par, g - 1, k // 4)
                        soft_bank(s, par, g, k)
                        if a:
                            for n in banks_of(g, k):
                                scores_bank(s + 1, 1 - par, n)
                if a:
                    v_rows(s + 1, d)
                pv(s, par, GROUPS - 1, 0)
                if a:
                    max_rows(s + 1)
                pv(s, par, GROUPS - 1, 1)
                pv(s, par, GROUPS - 1, 2)

            def last():
                b = B - 1
                for i in range(QT):
                    heads_rows(b, i, lambda i: pe.wait_ge(route, ROUTE * (b - 1) + (R_SCORES, R_RANK)[i]))
                heads_back(b, 0)
                heads_back(b, 1)
                output(b, 0)
                output(b, 1)
                xT_of(1, b, 0)
                xT_of(1, b, 1)
                router(b)
                ranks(b)

            steps(pe, prologue, step, last)

            pe.wait_ge(table, 1)
            pe.matmul(M[0][:, 0:E], cstb[:, CB_ONE:CB_ONE + P], cumlast[:, :], start=True, stop=True)\
              .then_inc(tot_full, 1)
            pe.wait_ge(table, IDS_AT)
            pe.transpose(M[1][:, 0:MAX_BLOCKS], ids_f[:, :], ident[0:MAX_BLOCKS, 0:MAX_BLOCKS]).then_inc(slots_full, 1)
            pe.wait_ge(table, TABLE)

            def block_xT(t, par):
                pe.wait_ge(gath[par], 8 * (t - par) + 16)
                if not (isinstance(t, int) and t == 0):
                    pe.wait_ge(xgt_sb, t)
                transposes(M[0], [xg[par][:, P * k:P * k + P] for k in range(KD)], P, xgt_full)

            def layer1(t, par):
                e = pe.value_load(blk_expert[0:1, bass.ds(t, 1)], min_val=0, max_val=E - 1)
                pe.wait_ge(weights_ready, e + 1)
                pe.wait_ge(xgt_sb, t + 1)
                for c in range(2):
                    if not (isinstance(t, int) and t == 0):
                        pe.wait_ge((hs0, hs1)[c], t)
                    for k in range(KD):
                        last = pe.matmul(S[c][:, :], xgT[par][:, k, :],
                                         Wf[:, bass.ds(WE * e + F * k + 512 * c, 512)],
                                         start=(k == 0), stop=(k == KD - 1))
                    last.then_inc(f1_full, 1)

            def hidden_T(t):
                for c in range(2):
                    pe.wait_ge((hs0, hs1)[c], t + 1)
                    if not (isinstance(t, int) and t == 0):
                        pe.wait_ge(z_s, 2 * t)
                    transposes(TT[c], [hs[:, P * k:P * k + P] for k in range(4 * c, 4 * c + 4)], P, htr_full)

            def layer2(t, par):
                e = pe.value_load(blk_expert[0:1, bass.ds(t, 1)], min_val=0, max_val=E - 1)
                if not (isinstance(t, int) and t < 2):
                    pe.wait_ge(y_s, t - 1)
                for k in range(KF):
                    if k % 4 == 0:
                        pe.wait_ge(gelu_s, 2 * t + k // 4 + 1)
                    last = pe.matmul(Y[par][:, 0:D], hT[:, k, :],
                                     Wf[:, bass.ds(WE * e + KD * F + D * k, D)],
                                     start=(k == 0), stop=(k == KF - 1))
                last.then_inc(f2_full, 1)

            Wf = W[:, :, :].rearrange("p e w -> p (e w)")
            block_xT(0, 0)
            layer1(0, 0)

            def body(t, par, following):
                if following:
                    block_xT(t + 1, 1 - par)
                hidden_T(t)
                if following:
                    layer1(t + 1, 1 - par)
                layer2(t, par)

            blocks(pe, body)


_INS = ["L0_attn_x", "L0_attn_Wq", "L0_attn_bq", "L0_attn_Wk", "L0_attn_bk", "L0_attn_Wv", "L0_attn_bv",
        "L0_attn_Wo", "L0_attn_bo", "L0_ffn_W1", "L0_ffn_b1", "L0_ffn_W2", "L0_ffn_b2", "L0_ffn_Wr", "L0_ffn_br"]


def kernel(**inputs):
    import numpy as _np
    import concourse.bacc as _bacc
    from concourse import mybir as _mybir
    from concourse.bass_utils import run_bass_kernel_spmd as _run

    nc = _bacc.Bacc("TRN2", target_bir_lowering=False, num_devices=1)
    arrays, args = {}, []
    named = [(n, _np.ascontiguousarray(inputs[n])) for n in _INS]
    named += list(zip(("const", "constb", "rope"), constants()))
    for name, a in named:
        arrays[f"in_{name}"] = a
        args.append(nc.dram_tensor(f"in_{name}", a.shape, _mybir.dt.from_np(a.dtype), kind="ExternalInput").ap())
    args.append(nc.dram_tensor("out", (B, T, D), _mybir.dt.float32, kind="ExternalOutput").ap())
    layer(nc, *args)
    r = _run(nc, [arrays], core_ids=[0])
    return r.results[0]["out"]
```

```python
from contextlib import ExitStack

import numpy as np

import concourse.bass as bass
from concourse import mybir

F32 = mybir.dt.float32
F32R = mybir.dt.float32r
BF16 = mybir.dt.bfloat16
I32 = mybir.dt.int32
ALU = mybir.AluOpType
ACT = mybir.ActivationFunctionType
AX = mybir.AxisListType

P = 128
B, T, D = 8, 512, 256
H, HD = 16, 16
QT = T // P
KD = D // P
NT = B * QT
N = B * T
E, F = 8, 1024
KF = F // P
EPS = 1e-5
QSCALE = HD ** -0.5
PAIRS = H // 2
GROUPS = H // 4
BIG = -1e38

S_BANKS = 4 * (1 + 2 + 4 + 4)
QUARTER_BANKS = S_BANKS // 4
T_BANKS = 10

MAX_BLOCKS = (2 * N + E * (P - 1)) // P
LIST_ROWS = E * (N // P) + 1
PAD = 2 * N
WE = KD * F + KF * D

NBIAS = E * KF + KD + 1
UNROLL = 6
POOL_PART = 1280

PREP = 15
ROUTE = 32
R_SCORES, R_MASKS, R_DIFF, R_RANK = 1, 20, 21, 25
TABLE, ROWS_AT, IDS_AT = 30, 13, 22

C_ID, C_MA, C_MB, C_SA, C_SB, C_REV, C_BASE, C_CNT, C_BLK, C_COL, C_IDS = (
    0, 128, 129, 130, 131, 132, 140, 148, 180, 180 + MAX_BLOCKS, 181 + MAX_BLOCKS)
C_END = C_IDS + 2 * QT
CB_ID, CB_U, CB_ONE, CB_S, CB_T, CB_END = 0, 128, 256, 384, 384 + 7 * P, 384 + 14 * P


def constants():
    row = np.arange(P)
    c = np.zeros((P, C_END), np.float32)
    c[:, C_ID:C_ID + P] = np.eye(P)
    c[:96, C_MA] = (row[:96] % 32) < 16
    c[:96, C_MB] = (row[:96] % 32) >= 16
    c[:, C_SA:C_SB + 1] = c[:, C_MA:C_MB + 1]
    c[96:100, C_MA] = [1, 0, 1, 0]
    c[96:100, C_MB] = [0, 1, 0, 1]
    c[:, C_REV:C_REV + E] = E - np.arange(E)
    c[:, C_BASE:C_BASE + E] = N * np.arange(E)
    c[:, C_CNT:C_CNT + N // P] = P * np.arange(N // P)
    c[:, C_BLK:C_BLK + MAX_BLOCKS] = np.arange(MAX_BLOCKS)
    c[:, C_COL] = row
    c[:, C_IDS:C_END] = row[:, None] + (N * np.arange(2)[:, None] + P * np.arange(QT) - T).reshape(1, -1)
    b = np.zeros((P, CB_END), np.float32)
    b[:, CB_ID:CB_ID + P] = np.eye(P)
    for i in (3, 4, 5, 6):
        b[:, CB_S + P * i:CB_S + P * i + P] = np.where(row[None, :] > row[:, None], BIG, 0)
    for i in (0, 3):
        b[:, CB_T + P * i:CB_T + P * i + P] = np.where(row[:, None] > row[None, :], BIG, 0)
    b[:, CB_U:CB_U + P] = row[:, None] < row[None, :]
    b[:, CB_ONE:CB_ONE + P] = 1
    half = HD // 2
    theta = np.float32(10000.0) ** (-np.arange(half, dtype=np.float32) / np.float32(half))
    freqs = np.arange(T, dtype=np.float32)[:, None] * theta[None, :].astype(np.float32)
    cos, sin = np.cos(freqs).astype(np.float32).T, np.sin(freqs).astype(np.float32).T
    rope = np.zeros((P, 2, T), np.float32)
    for r in range(P):
        d = r % HD
        if d < half:
            rope[r, 0] = cos[d]
            rope[r, 1] = -sin[d] if d < half // 2 else sin[d]
        else:
            rope[r, 0] = 1
    return c, b, rope


def rotation():
    q = HD // 4
    return [i + q if i % HD < q else i - q if i % HD < 2 * q else i for i in range(32)]


def layer(nc, x, Wq, bq, Wk, bk, Wv, bv, Wo, bo, W1, b1, W2, b2, Wr, br, const, constb, rope, out):
    xn2_dram = nc.dram_tensor("xn2_rows", (N, D), F32, kind="Internal").ap()
    list_dram = nc.dram_tensor("expert_lists", (LIST_ROWS * P, 2), I32, kind="Internal").ap()
    out_rows = out.rearrange("b t d -> (b t) d")

    with ExitStack() as ctx:
        def sem(name):
            return ctx.enter_context(nc.semaphore(name))

        def sb(name, shape, dt=F32, stack=ctx):
            return stack.enter_context(nc.sbuf_tensor(name, shape, dt))

        S = [ctx.enter_context(nc.psum_tensor(f"S{i}", [P, 512], F32)) for i in range(3)]
        TT = [ctx.enter_context(nc.psum_tensor(f"T{i}", [P, 512], F32)) for i in range(2)]
        PV = ctx.enter_context(nc.psum_tensor("PV", [P, 512], F32))
        M = [ctx.enter_context(nc.psum_tensor(f"M{i}", [P, 512], F32)) for i in range(2)]

        Y = [PV, S[2]]

        cst = sb("cst", [P, C_END])
        cstb = sb("cstb", [P, CB_END], BF16)
        ident = cst[:, C_ID:C_ID + P]
        identb = cstb[:, CB_ID:CB_ID + P]
        xres = sb("xres", [P, NT, D])
        biasT = sb("biasT", [P, NBIAS])
        blocks_i = sb("blocks_i", [P, MAX_BLOCKS], I32)
        slots = sb("slots", [P, MAX_BLOCKS], I32)
        slot_tok = sb("slot_tok", [P, MAX_BLOCKS], I32)
        slot_gate = sb("slot_gate", [P, MAX_BLOCKS])
        b2b = sb("b2b", [P, E, D])

        raw = sb("raw", [P, WE])
        ffn = ExitStack()
        W = sb("W", [P, 2, 2, WE], F32R, ffn)
        slot_now = [sb(f"slot_now{i}", [P, 1], I32, ffn) for i in range(2)]
        tok_now = [sb(f"tok_now{i}", [P, 1], I32, ffn) for i in range(2)]
        xg = [sb(f"xg{i}", [P, D], F32, ffn) for i in range(2)]
        xgT = [[sb(f"xgT{i}{part}", [P, KD * P], F32R, ffn) for part in range(2)] for i in range(2)]
        hs = sb("hs", [P, F], F32, ffn)
        hT = sb("hT", [P, KF, P], F32, ffn)
        hG = sb("hG", [P, KF, P], F32, ffn)
        hTs = [sb(f"hTs{part}", [P, KF, P], F32R, ffn) for part in range(2)]
        yrow = [sb(f"yrow{i}", [P, D], F32, ffn) for i in range(2)]
        ffn.close()

        QQ = [sb(f"Q{p}", [P, PAIRS, T], F32R) for p in range(2)]
        prob = sb("prob", [P, T_BANKS, 512])
        KK = [[sb(f"K{p}{s}", [P, T], F32R) for s in range(2)] for p in range(2)]
        KS = [sb(f"KS{s}", [P, T], F32R) for s in range(2)]
        ropes = sb("ropes", [P, 2, T])
        wq = sb("wq", [P, KD, D])
        wkv1 = sb("wkv1", [P, KD, 2 * HD])
        wkv = sb("wkv", [P, KD, P])
        wo = sb("wo", [P, KD, D])
        wr = sb("wr", [P, KD, E])
        bob = sb("bob", [P, D])
        brb = sb("brb", [P, E])
        brow = sb("brow", [NBIAS, P])
        padrows = sb("padrows", [P, 2 * LIST_ROWS], I32)
        minus_half = sb("minus_half", [P, QT])
        ones = sb("ones", [P, T])
        st = [sb(f"st{i}", [P, QT, 6]) for i in range(2)]
        mv = [sb(f"mv{i}", [P, QT, 2]) for i in range(2)]
        veps = [sb(f"veps{i}", [P, QT]) for i in range(2)]
        rstd = [sb(f"rstd{i}", [P, QT]) for i in range(2)]
        xh = [sb(f"xh{i}", [P, QT, D]) for i in range(2)]
        xT = [sb(f"xT{i}", [P, KD, T]) for i in range(2)]
        qraw = sb("qraw", [P, 3, T])
        qrot = sb("qrot", [P, 3, T])
        qhi = sb("qhi", [P, 2, T], F32R)
        qlo = sb("qlo", [P, 2, T], F32R)
        khl = sb("khl", [P, T], F32R)
        Va = [sb(f"V{p}", [P, QT, 32]) for p in range(2)]
        nmax = sb("nmax", [P, QT, H])
        nsplit = sb("nsplit", [P, QT, 2 * H], F32R)
        mT = sb("mT", [2 * H, T], F32R)
        oT = sb("oT", [P, GROUPS, T])
        rden = sb("rden", [P, QT, H])
        on = sb("on", [P, QT, D])
        oT2 = sb("oT2", [P, KD, T])
        sc = sb("sc", [P, QT, E])
        tmp = sb("tmp", [P, QT, E])
        oh = sb("oh", [P, 2, QT, E])
        top = sb("top", [P, 2, QT])
        first = sb("first", [P, QT])
        gex = sb("gex", [P, QT])
        gsum = sb("gsum", [P, QT])
        maskb = sb("maskb", [P, QT, E], BF16)
        cum = sb("cum", [P, QT + 1, E])
        cumb = sb("cumb", [P, QT, E], BF16)
        rank = sb("rank", [P, QT, E])
        posf = sb("posf", [P, 2, QT])
        pos = sb("pos", [P, 2, QT], I32)
        idf = sb("idf", [P, 2, QT])
        entry = sb("entry", [P, 2, QT, 2], I32)
        cumlast = sb("cumlast", [P, E], BF16)
        tot = sb("tot", [P, E])
        over = sb("over", [P, E, N // P])
        nblk = sb("nblk", [P, E])
        ends = sb("ends", [P, E])
        zeros8 = sb("zeros8", [P, E])
        le, start = (prob[:, i, 0:MAX_BLOCKS * n].rearrange("p (t e) -> p t e", e=n)
                     for i, n in enumerate((E - 1, E - 2)))
        lec = sb("lec", [P, E])
        lecn = sb("lecn", [P, E])
        colv = sb("colv", [P, 4])
        rowi = sb("rowi", [P, 1], I32)
        ids_r = sb("ids_r", [MAX_BLOCKS, P, 2], I32)
        ids_f = sb("ids_f", [MAX_BLOCKS, 2, P])
        sl_f = sb("sl_f", [P, MAX_BLOCKS])
        sl_g = sb("sl_g", [P, MAX_BLOCKS])
        blk_f = sb("blk_f", [P, MAX_BLOCKS])
        code_f = sb("code_f", [P, MAX_BLOCKS])
        next_f = sb("next_f", [P, MAX_BLOCKS])

        x_in = [sem(f"x_in{i}") for i in range(2)]
        setup_in = sem("setup_in")
        list_init = sem("list_init")
        b2_in = sem("b2_in")
        raw_in = [sem("raw_w1"), sem("raw_w2")]
        w_hi = [sem("w1_hi"), sem("w2_hi")]
        w_lo = [sem("w1_lo"), sem("w2_lo")]
        prep = sem("prep")
        bias_row = sem("bias_row")
        stats = [sem("stats_ln1"), sem("stats_ln2")]
        aggr = [sem("aggr_ln1"), sem("aggr_ln2")]
        eps_in = [sem("eps_ln1"), sem("eps_ln2")]
        rstd_s = [sem("rstd_ln1"), sem("rstd_ln2")]
        xh_s = [sem("xh_ln1"), sem("xh_ln2")]
        xt_full = [sem("xt_full_ln1"), sem("xt_full_ln2")]
        xt_sb = [sem("xt_sb_ln1"), sem("xt_sb_ln2")]
        bo_added = sem("bo_added")
        qkv_full = sem("qkv_full")
        qkv_sb = sem("qkv_sb")
        shuffled = sem("shuffled")
        cos_mul = sem("cos_mul")
        sin_mul = sem("sin_mul")
        roped = sem("roped")
        hi_s = sem("hi_s")
        klo_s = sem("klo_s")
        ks_s = sem("ks_s")
        q_zero = sem("q_zero")
        split_s = sem("split_s")
        stack_in = [sem(f"stack_in{u}") for u in range(4)]
        s_full = sem("s_full")
        s_max = sem("s_max")
        nsplit_s = sem("nsplit_s")
        mt_full = sem("mt_full")
        mt_sb = sem("mt_sb")
        m_in = sem("m_in")
        t_full = sem("t_full")
        exps = sem("exps")
        v_full = sem("v_full")
        v_sb = sem("v_sb")
        pv_full = sem("pv_full")
        ot_sb = sem("ot_sb")
        otr_full = sem("otr_full")
        rden_s = sem("rden_s")
        on_s = sem("on_s")
        ott_full = sem("ott_full")
        ott_sb = sem("ott_sb")
        wo_full = sem("wo_full")
        x2_s = sem("x2_s")
        xn2_out = sem("xn2_out")
        sc_full = sem("sc_full")
        gexp = sem("gexp")
        route = sem("route")
        rank_full = sem("rank_full")
        listed = sem("listed")
        table = sem("table")
        tot_full = sem("tot_full")
        rows_in = sem("rows_in")
        slots_full = sem("slots_full")
        now_s = sem("now_s")
        gath = [sem("gath0"), sem("gath1")]
        xgt_full = sem("xgt_full")
        xg_hi = sem("xg_hi")
        xg_lo = sem("xg_lo")
        f1_full = sem("f1_full")
        hs0 = sem("hs0")
        hs1 = sem("hs1")
        htr_full = sem("htr_full")
        z_s = sem("z_s")
        gelu_s = sem("gelu_s")
        h_lo = sem("h_lo")
        f2_full = sem("f2_full")
        y_s = sem("y_s")
        snow_s = sem("snow_s")
        rows_b2 = sem("rows_b2")
        base_out = sem("base_out")
        added = sem("added")
        settled = sem("settled")

        NSETUP = 14
        HALF = WE // 2
        S_FIRST, S_SLOTS = 7, 30

        def steps(eng, prologue, step, last):
            prologue()
            step(0, 0, True, False, True)
            with eng.Fori(0, 2) as j:
                step(2 * j + 1, 1, True, True, True)
                step(2 * j + 2, 0, True, True, True)
            step(5, 1, True, True, True)
            step(6, 0, True, True, False)
            step(7, 1, False, True, False)
            last()

        def quarter_banks(u):
            for qt, nh in ((0, 4), (1, 2), (2, 1), (3, 1)):
                for h in range(4 * u, 4 * u + 4, nh):
                    yield qt, h, nh

        PARTS = ((0, 1), (2, 0), (1, 1))
        BANKS = [bank for u in range(4) for bank in quarter_banks(u)]

        def banks_of(g, k):
            at = T_BANKS * g + k - S_FIRST
            if at < 0:
                return range(0)
            return range(min(S_BANKS, S_BANKS * at // S_SLOTS), min(S_BANKS, S_BANKS * (at + 1) // S_SLOTS))

        def blocks(eng, body):
            body(0, 0, 2)
            body(1, 1, 2)
            with eng.Fori(0, (MAX_BLOCKS - 5) // UNROLL) as j:
                for i in range(UNROLL):
                    body(UNROLL * j + 2 + i, i % 2, 2)
            body(MAX_BLOCKS - 3, 0, 2)
            body(MAX_BLOCKS - 2, 1, 1)
            body(MAX_BLOCKS - 1, 0, 0)

        def block_of(eng, t):
            code = eng.value_load(blocks_i[0:1, bass.ds(t, 1)], min_val=0, max_val=2 * E * E - 1)
            return (code // 2) % E, code // (2 * E), (code // 2) % 2, code % 2

        def split_low(eng, m, cols, half):
            at = HALF * m + cols.start
            n = cols.stop - cols.start
            return eng.tensor_tensor(Wf[:, bass.ds(2 * WE * half + WE + at, n)], raw[:, at:at + n],
                                     Wf[:, bass.ds(2 * WE * half + at, n)].bitcast(F32), ALU.subtract)

        def settle(eng, at):
            if not isinstance(at, int):
                eng.sem_inc(settled, 1)

        assert MAX_BLOCKS % 2 == 1 and (MAX_BLOCKS - 5) % UNROLL == 0 and S_BANKS % 2 == 0

        Wf = W[:, :, :, :].rearrange("p a b w -> p (a b w)")
        VECTOR_COLS, POOL_COLS = slice(POOL_PART, HALF), slice(0, POOL_PART)

        block = ctx.enter_context(nc.Block())

        @block.sync
        def _(sp):
            def load(dst, src):
                sp.dma_start(dst, src).then_inc(setup_in, 16)

            for b in range(B):
                if b == 2:
                    load(cst[:, :], const)
                    load(prob[:, 0:5, :].rearrange("p a n -> p (a n)")[:, 0:CB_END], constb)
                    load(wq[:, :, :], Wq.rearrange("(k p) n -> p k n", p=P))
                    load(wkv1[:, :, 0:HD], Wk.rearrange("(k p) n -> p k n", p=P))
                    load(wkv1[:, :, HD:2 * HD], Wv.rearrange("(k p) n -> p k n", p=P))
                    load(brow[0:E * KF, :], b1.rearrange("e (k p) -> (e k) p", p=P))
                    load(brow[E * KF:E * KF + KD, :], bq.rearrange("(k p) -> k p", p=P))
                    for at, n, bias in ((0, 6, bk), (6 * HD, 2, bv)):
                        load(brow[NBIAS - 1:NBIAS, at:at + n * HD].rearrange("a (r n) -> a r n", n=HD),
                             bias.partition_broadcast(n).unsqueeze(0))
                    load(ropes[:, :, :], rope)
                    load(wo[:, :, :], Wo.rearrange("(k p) n -> p k n", p=P))
                    load(wr[:, :, :], Wr.rearrange("(k p) n -> p k n", p=P))
                    load(bob[:, :], bo.partition_broadcast(P))
                    load(brb[:, :], br.partition_broadcast(P))
                if b >= 2:
                    sp.wait_ge(x_in[b % 2], 16 * (b // 2))
                sp.dma_start(xres[:, QT * b:QT * b + QT, :],
                             x[b].rearrange("(i p) d -> p i d", p=P)).then_inc(x_in[b % 2], 16)
            sp.wait_ge(prep, 1)
            sp.dma_start(list_dram.rearrange("(p n) a -> p (n a)", p=P), padrows[:, :]).then_inc(list_init, 16)

            def weights(e, m):
                src, k = ((W1, KD), (W2, KF))[m]
                sp.dma_start(raw[:, HALF * m:HALF * m + HALF].rearrange("p (k n) -> p k n", k=k),
                             src[e].rearrange("(k p) n -> p k n", p=P)).then_inc(raw_in[m], 16)

            def stack(b, par, t):
                sp.wait_ge(split_s, 3 * b + (1 if t == 0 else 3))
                for g in range(4):
                    pair = 4 * t + g
                    for part, src in ((0, qhi), (1, qhi), (2, qlo)):
                        sp.dma_start(QQ[par][32 * part:32 * part + 32, pair, :].bitcast(F32),
                                     src[32 * g:32 * g + 32, t, :].bitcast(F32)).then_inc(
                                           stack_in[pair // 2], 16)

            def prologue():
                stack(0, 0, 0)
                stack(0, 0, 1)
                sp.wait_ge(q_zero, 2)
                maxima_in(0, 0)
                weights(0, 0)
                weights(0, 1)
                sp.dma_start(b2b[:, :, :], b2.partition_broadcast(P)).then_inc(b2_in, 16)

            def maxima_in(b, par):
                sp.wait_ge(mt_sb, b + 1)
                for part in range(2):
                    for one in range(2):
                        at = H * part + one
                        sp.dma_start(QQ[par][96 + 2 * part + one:97 + 2 * part + one, :, :].bitcast(F32),
                                     mT[at:at + H - 1:2, :].bitcast(F32)).then_inc(m_in, 16)

            def step(s, par, a, d, _):
                if a:
                    stack(s + 1, 1 - par, 0)
                    stack(s + 1, 1 - par, 1)
                if d:
                    store(s - 1)
                if a:
                    maxima_in(s + 1, 1 - par)

            def store(b):
                sp.wait_ge(x2_s, 2 * b + 2)
                sp.dma_start(out_rows[bass.ds(T * b, T), :].rearrange("(i p) d -> p i d", p=P),
                             xres[:, bass.ds(QT * b, QT), :]).then_inc(base_out, 16)
                sp.wait_ge(xh_s[1], QT * b + QT)
                sp.dma_start(xn2_dram[bass.ds(T * b, T), :].rearrange("(i p) d -> p i d", p=P),
                             xh[1][:, :, :]).then_inc(xn2_out, 16)

            steps(sp, prologue, step, lambda: store(B - 1))
            for e in range(1, E):
                for m in range(2):
                    sp.wait_ge(w_lo[m], 2 * e)
                    weights(e, m)
            sp.wait_ge(added, 16 * MAX_BLOCKS)

        @block.gpsimd
        def _(pool):
            def rsqrt(n, b):
                pool.wait_ge(eps_in[n], b + 1)
                pool.tensor_tensor(rstd[n][:, :], veps[n][:, :], minus_half[:, :], ALU.pow).then_inc(rstd_s[n], 1)

            def rope_one(b, i, t, rows):
                pool.wait_ge(shuffled, 3 * b + i + 1)
                raw = qraw[0:rows, t, :]
                pool.tensor_tensor(raw, raw, ropes[0:rows, 0, :], ALU.mult).then_inc(cos_mul, 1)

            def rope_all(b):
                rope_one(b, 0, 0, P)
                rope_one(b, 1, 2, 96)
                rope_one(b, 2, 1, P)

            def add_bo(b):
                pool.wait_ge(xh_s[0], QT * b + QT)
                xb = xres[:, bass.ds(QT * b, QT), :]
                pool.tensor_tensor(xb, xb, bob[:, :].unsqueeze(1).broadcast_to([P, QT, D]),
                                   ALU.add).then_inc(bo_added, 1)

            def scatter_ids(b):
                pool.wait_ge(route, ROUTE * b + ROUTE)
                settle(pool, b)
                for c in range(2):
                    for i in range(QT):
                        pool.indirect_dma_start(
                            out=list_dram[:, :], out_offset=bass.IndirectOffsetOnAxis(ap=pos[:, c, i:i + 1], axis=0),
                            in_=entry[:, c, i, :], in_offset=None).then_inc(listed, 16)

            def prologue():
                for i, q in enumerate(QQ):
                    pool.memset(q[96:128, :, :].bitcast(F32), 0.0).then_inc(q_zero, 1)
                    pool.wait_ge(q_zero, i + 1)
                pool.wait_ge(prep, 2)
                rsqrt(0, 0)
                pool.wait_ge(setup_in, 16 * NSETUP)
                rsqrt(0, 1)
                rope_all(0)
                add_bo(0)
                pool.wait_ge(list_init, 16)

            def step(s, par, a, d, ln):
                if a:
                    rope_all(s + 1)
                    add_bo(s + 1)
                if d:
                    rsqrt(1, s - 1)
                if ln:
                    rsqrt(0, s + 2)
                if d:
                    scatter_ids(s - 1)

            def last():
                rsqrt(1, B - 1)
                scatter_ids(B - 1)

            steps(pool, prologue, step, last)
            pool.wait_ge(table, ROWS_AT)
            pool.wait_ge(listed, 16 * 2 * QT * B)
            pool.indirect_dma_start(
                out=ids_r[:, :, :].rearrange("p n a -> p (n a)"), out_offset=None, in_=list_dram.rearrange("(r n) a -> r (n a)", n=P),
                in_offset=bass.IndirectOffsetOnAxis(ap=rowi[0:MAX_BLOCKS, 0:1], axis=0)).then_inc(rows_in, 16)

            def split(m, count, half):
                pool.wait_ge(w_hi[m], count)
                split_low(pool, m, POOL_COLS, half).then_inc(w_lo[m], 1)

            split(0, 1, 0)
            split(1, 1, 0)
            pool.wait_ge(table, TABLE)
            pool.wait_ge(xn2_out, 16 * B)
            pool.wait_ge(base_out, 16 * B)

            def gather(t, par, again):
                if again:
                    pool.wait_ge(gath[par], 8 * (t - par))
                    pool.wait_ge(xgt_full, t - 1)
                pool.tensor_copy(tok_now[par][:, :], slot_tok[:, bass.ds(t, 1)]).then_inc(now_s, 1)
                pool.wait_ge(now_s, t + 1)
                settle(pool, t)
                pool.indirect_dma_start(
                    out=xg[par][:, :], out_offset=None, in_=xn2_dram[:, :],
                    in_offset=bass.IndirectOffsetOnAxis(ap=tok_now[par][:, 0:1], axis=0)).then_inc(gath[par], 16)

            def scatter(t, par):
                if not (isinstance(t, int) and t == 0):
                    pool.wait_ge(added, 16 * t)
                pool.tensor_copy(slot_now[par][:, :], slots[:, bass.ds(t, 1)]).then_inc(snow_s, 1)
                pool.wait_ge(y_s, t + 1)
                pool.wait_ge(snow_s, t + 1)
                settle(pool, t)
                pool.indirect_dma_start(
                    out=out_rows, out_offset=bass.IndirectOffsetOnAxis(ap=slot_now[par][:, 0:1], axis=0),
                    in_=yrow[par][:, :], in_offset=None, bounds_check=N - 1,
                    oob_is_err=False, compute_op=ALU.add).then_inc(added, 16)

            def body(t, par, following):
                first = isinstance(t, int) and t == 0
                if following and not first:
                    e, _, half, new = block_of(pool, t)
                if not (isinstance(t, int) and t + 3 >= MAX_BLOCKS):
                    gather(t + 3, 1 - par, True)
                if first:
                    split(0, 2, 1)
                elif following:
                    with pool.If(new):
                        split(0, e + 2, 1 - half)
                if not first:
                    scatter(t - 1, 1 - par)
                if first:
                    split(1, 2, 1)
                elif following:
                    with pool.If(new):
                        split(1, e + 2, 1 - half)

            gather(0, 0, False)
            gather(1, 1, False)
            gather(2, 0, True)
            blocks(pool, body)
            scatter(MAX_BLOCKS - 1, 0)
            pool.wait_ge(added, 16 * MAX_BLOCKS)

        @block.scalar
        def _(act):
            def evac_xT(n, b, k):
                act.wait_ge(xt_full[n], KD * b + k + 1)
                if n == 0 and not (isinstance(b, int) and b == 0):
                    act.wait_ge(qkv_full, 3 * b)
                if n == 1 and not (isinstance(b, int) and b == 0):
                    act.wait_ge(sc_full, b)
                act.activation(xT[n][:, k, :], M[1 - k if n == 0 else k][:, :], ACT.Copy).then_inc(xt_sb[n], 1)

            def evac_qkv(b, i):
                t, bank = PARTS[i]
                act.wait_ge(qkv_full, 3 * b + i + 1)
                if not (isinstance(b, int) and b == 0):
                    act.wait_ge(split_s, 3 * b)
                    act.wait_ge(v_full, 2 * b)
                bias = biasT[:, E * KF + t:E * KF + t + 1]
                act.activation(qraw[:, t, :], M[bank][:, :], ACT.Identity, bias=bias,
                               scale=1.0 if t == 2 else QSCALE).then_inc(qkv_sb, 1)

            def evac_v(b, par):
                for u in range(2):
                    act.wait_ge(v_full, 2 * b + u + 1)
                    if not (isinstance(b, int) and b < 2):
                        act.wait_ge(pv_full, 3 * GROUPS * (b - 1))
                    act.activation(Va[par][:, 2 * u:2 * u + 2, 0:HD],
                                   M[u][:, 0:64].rearrange("p (i w) -> p i w", w=32)[:, :, 0:HD],
                                   ACT.Copy).then_inc(v_sb, 1)

            def exp_bank(s, g, k):
                stage = 0 if k < 4 else 1 if k < 8 else 2
                act.wait_ge(t_full, GROUPS * T_BANKS * s + T_BANKS * g + k + 1)
                if not (isinstance(s, int) and s == 0 and g == 0):
                    act.wait_ge(pv_full, 3 * GROUPS * s + 3 * g + stage - 2)
                act.activation(prob[:, k, :], TT[k % 2][:, :], ACT.Exp).then_inc(exps, 1)

            def evac_oT(s, g):
                act.wait_ge(pv_full, 3 * GROUPS * s + 3 * g + 3)
                if not (isinstance(s, int) and s == 0):
                    act.wait_ge(otr_full, QT * s)
                act.activation(oT[:, g, :], PV[:, :], ACT.Copy).then_inc(ot_sb, 1)

            def evac_oTT(b, k):
                act.wait_ge(ott_full, KD * b + k + 1)
                if not (isinstance(b, int) and b == 0):
                    act.wait_ge(wo_full, 2 * b)
                act.activation(oT2[:, k, :], M[k][:, :], ACT.Copy).then_inc(ott_sb, 1)

            def gate_exp(b):
                act.wait_ge(route, ROUTE * b + R_DIFF)
                act.activation(gex[:, :], gex[:, :], ACT.Exp).then_inc(gexp, 1)

            def prologue():
                act.wait_ge(prep, PREP)
                for k in range(KD):
                    evac_xT(0, 0, k)
                for i in range(3):
                    evac_qkv(0, i)
                evac_v(0, 0)
                evac_mT(0)

            def evac_mT(b):
                act.wait_ge(mt_full, b + 1)
                if not (isinstance(b, int) and b == 0):
                    act.wait_ge(m_in, 64 * b)
                act.activation(mT[:, :], M[0][0:2 * H, :], ACT.Copy).then_inc(mt_sb, 1)

            def step(s, par, a, d, _):
                if a:
                    evac_xT(0, s + 1, 0)
                    evac_xT(0, s + 1, 1)
                    evac_qkv(s + 1, 0)
                    evac_qkv(s + 1, 1)
                for g in range(GROUPS):
                    for k in range(T_BANKS):
                        exp_bank(s, g, k)
                        if a and (g, k) == (0, 0):
                            evac_qkv(s + 1, 2)
                        if g >= 1 and k == 8:
                            evac_oT(s, g - 1)
                        if d and (g, k) in ((0, 8), (0, 9)):
                            evac_oTT(s - 1, k - 8)
                        if d and (g, k) in ((2, 2), (2, 3)):
                            evac_xT(1, s - 1, k - 2)
                        if d and (g, k) == (3, 3):
                            gate_exp(s - 1)
                if a:
                    evac_v(s + 1, 1 - par)
                    evac_mT(s + 1)
                evac_oT(s, GROUPS - 1)

            def last():
                for k in range(KD):
                    evac_oTT(B - 1, k)
                for k in range(KD):
                    evac_xT(1, B - 1, k)
                gate_exp(B - 1)

            steps(act, prologue, step, last)

            def high_xgT(t, par):
                act.wait_ge(xgt_full, t + 1)
                if not (isinstance(t, int) and t < 2):
                    act.wait_ge(f1_full, 2 * t - 2)
                act.activation(xgT[par][0][:, :], M[0][:, 0:D], ACT.Copy).then_inc(xg_hi, 1)

            def evac_h1(t):
                act.wait_ge(f1_full, 2 * t + 2)
                if not (isinstance(t, int) and t == 0):
                    act.wait_ge(htr_full, 2 * t)
                act.activation(hs[:, 512:1024], S[1][:, :], ACT.Copy).then_inc(hs1, 1)

            act.wait_ge(table, TABLE)
            high_xgT(0, 0)
            evac_h1(0)
            high_xgT(1, 1)

            def body(t, par, following):
                for c in range(2):
                    act.wait_ge(z_s, 2 * t + c + 1)
                    half = hT[:, 4 * c:4 * c + 4, :]
                    if not (isinstance(t, int) and t == 0):
                        act.wait_ge(f2_full, t)
                        act.wait_ge(h_lo, 2 * t)
                    act.activation(hTs[0][:, 4 * c:4 * c + 4, :], half, ACT.Gelu_apprx_tanh)
                    act.activation(hG[:, 4 * c:4 * c + 4, :], half, ACT.Gelu_apprx_tanh).then_inc(gelu_s, 1)
                if following:
                    evac_h1(t + 1)
                if following == 2:
                    high_xgT(t + 2, par)

            blocks(act, body)

        @block.vector
        def _(dve):
            def tile_of(b, i):
                return xres[:, bass.ds(QT * b + i, 1), :].rearrange("p a d -> p (a d)")

            def ln_stats(n, b, par, half):
                if n == 0 and half == 0:
                    dve.wait_ge(x_in[par], 8 * (b - par) + 16)
                    settle(dve, b)
                if n == 1:
                    dve.wait_ge(x2_s, 2 * b + half + 1)
                    settle(dve, b)
                for i in (2 * half, 2 * half + 1):
                    dve.bn_stats(st[n][:, i, :], tile_of(b, i)).then_inc(stats[n], 1)
                dve.wait_ge(stats[n], QT * b + 2 * half + 2)
                settle(dve, b)
                for i in (2 * half, 2 * half + 1):
                    dve.bn_aggr(mv[n][:, i, :], st[n][:, i, :]).then_inc(aggr[n], 1)
                if half:
                    dve.wait_ge(aggr[n], QT * b + QT)
                    dve.tensor_scalar(veps[n][:, :], mv[n][:, :, 1], EPS, None, ALU.add).then_inc(eps_in[n], 1)

            def ln_apply(n, b, half):
                if half == 0:
                    dve.wait_ge(rstd_s[n], b + 1)
                    if not (isinstance(b, int) and b == 0):
                        dve.wait_ge(xt_full[n], KD * b)
                        if n == 1:
                            dve.wait_ge(xn2_out, 16 * b)
                for i in (2 * half, 2 * half + 1):
                    dve.tensor_scalar(xh[n][:, i, :], tile_of(b, i),
                                      mv[n][:, i, 0:1], rstd[n][:, i:i + 1], ALU.subtract, ALU.mult)\
                       .then_inc(xh_s[n], 1)

            def shuffle_one(b, i, t):
                dve.wait_ge(qkv_sb, 3 * b + i + 1)
                settle(dve, b)
                dve.stream_shuffle(qrot[:, t, :], qraw[:, t, :], ROT).then_inc(shuffled, 1)

            def sin_one(b, i, t, rows):
                dve.wait_ge(shuffled, 3 * b + i + 1)
                rot = qrot[0:rows, t, :]
                dve.tensor_tensor(rot, rot, ropes[0:rows, 1, :], ALU.mult).then_inc(sin_mul, 1)

            def add_one(b, i, t, rows):
                dve.wait_ge(cos_mul, 3 * b + i + 1)
                dve.wait_ge(sin_mul, 3 * b + i + 1)
                dve.tensor_tensor(qraw[0:rows, t, :], qraw[0:rows, t, :], qrot[0:rows, t, :],
                                  ALU.add).then_inc(roped, 1)

            def heads_first(b):
                shuffle_one(b, 0, 0)
                sin_one(b, 0, 0, P)
                shuffle_one(b, 1, 2)
                sin_one(b, 1, 2, 96)
                add_one(b, 0, 0, P)
                split_q(b, 0, 0)

            def heads_keys(b, par):
                add_one(b, 1, 2, 96)
                split_k(b, par)

            def heads_second(b):
                shuffle_one(b, 2, 1)
                sin_one(b, 2, 1, P)
                add_one(b, 2, 1, P)
                split_q(b, 2, 1)

            def split_q(b, i, t):
                dve.wait_ge(roped, 3 * b + i + 1)
                if not (isinstance(b, int) and b == 0):
                    for u in (2 * t, 2 * t + 1):
                        dve.wait_ge(stack_in[u], 16 * 6 * b)
                dve.tensor_copy(qhi[:, t, :], qraw[:, t, :]).then_inc(hi_s, 1)
                dve.wait_ge(hi_s, 3 * b + i + 1)
                dve.tensor_tensor(qlo[:, t, :], qraw[:, t, :], qhi[:, t, :].bitcast(F32),
                                  ALU.subtract).then_inc(split_s, 1)

            def split_k(b, par):
                dve.wait_ge(roped, 3 * b + 2)
                dve.tensor_copy(khl[0:96, :], qraw[0:96, 2, :]).then_inc(hi_s, 1)
                dve.wait_ge(hi_s, 3 * b + 2)
                dve.tensor_tensor(khl[32:64, :], qraw[32:64, 2, :], khl[32:64, :].bitcast(F32),
                                  ALU.subtract).then_inc(klo_s, 1)
                dve.wait_ge(klo_s, b + 1)
                if not (isinstance(b, int) and b < 2):
                    dve.wait_ge(t_full, GROUPS * T_BANKS * (b - 1))
                for one in range(2):
                    dve.tensor_scalar(KS[one][:, :], khl[:, :].bitcast(F32), cst[:, C_SA + one:C_SA + one + 1], None,
                                      ALU.mult).then_inc(ks_s, 1)
                dve.tensor_scalar(KK[par][0][:, :], khl[:, :].bitcast(F32), cst[:, C_MA:C_MA + 1], None,
                                  ALU.mult)
                dve.tensor_scalar(KK[par][1][:, :], khl[:, :].bitcast(F32), cst[:, C_MB:C_MB + 1], None,
                                  ALU.mult).then_inc(split_s, 1)

            def maxima(b, n):
                qt, h, nh = BANKS[n]
                w = P * (qt + 1)
                dve.wait_ge(s_full, S_BANKS * b + n + 1)
                dve.tensor_reduce(nmax[:, qt, h:h + nh], S[n % 3][:, 0:nh * w].rearrange("p (h w) -> p h w", h=nh),
                                  AX.X, ALU.max, negate=True).then_inc(s_max, 1)

            def split_maxima(b):
                dve.wait_ge(s_max, S_BANKS * b + S_BANKS)
                if not (isinstance(b, int) and b == 0):
                    dve.wait_ge(mt_full, b)
                dve.tensor_copy(nsplit[:, :, 0:H], nmax[:, :, :]).then_inc(nsplit_s, 1)
                dve.wait_ge(nsplit_s, 2 * b + 1)
                dve.tensor_tensor(nsplit[:, :, H:2 * H], nmax[:, :, :], nsplit[:, :, 0:H].bitcast(F32),
                                  ALU.subtract).then_inc(nsplit_s, 1)

            def normalise(b, i):
                bank = M[i % 2][:, :].rearrange("p (h w) -> p h w", w=32)
                dve.wait_ge(otr_full, QT * b + i + 1)
                dve.reciprocal(rden[:, i, :], bank[:, :, HD]).then_inc(rden_s, 1)
                dve.wait_ge(rden_s, QT * b + i + 1)
                if not (isinstance(b, int) and b == 0):
                    dve.wait_ge(ott_full, KD * b)
                dve.tensor_tensor(on[:, i, :].rearrange("p (h d) -> p h d", d=HD), bank[:, :, 0:HD],
                                  rden[:, i, :].unsqueeze(2).broadcast_to([P, H, HD]), ALU.mult).then_inc(on_s, 1)

            def residual(b, u):
                dve.wait_ge(wo_full, 2 * b + u + 1)
                dve.wait_ge(bo_added, b + 1)
                two = xres[:, bass.ds(QT * b + 2 * u, 2), :]
                dve.tensor_tensor(two, M[u][:, :].rearrange("p (i d) -> p i d", i=2), two, ALU.add)\
                   .then_inc(x2_s, 1)

            def over_experts(ap):
                return ap.unsqueeze(2).broadcast_to([P, QT, E])

            def over_tiles(at):
                return cst[:, at:at + E].unsqueeze(1).broadcast_to([P, QT, E])

            def after(b, n):
                dve.wait_ge(route, ROUTE * b + n)

            def route_first(b):
                dve.wait_ge(sc_full, b + 1)
                dve.tensor_tensor(sc[:, :, :], M[0][:, 0:QT * E].rearrange("p (i e) -> p i e", e=E),
                                  brb[:, :].unsqueeze(1).broadcast_to([P, QT, E]), ALU.add).then_inc(route, 1)
                after(b, 1)
                dve.tensor_reduce(top[:, 0, :], sc[:, :, :], AX.X, ALU.max).then_inc(route, 1)
                after(b, 2)
                dve.tensor_tensor(tmp[:, :, :], sc[:, :, :], over_experts(top[:, 0, :]), ALU.is_equal).then_inc(route, 1)
                after(b, 3)
                dve.tensor_tensor(tmp[:, :, :], tmp[:, :, :], over_tiles(C_REV), ALU.mult).then_inc(route, 1)

            def route_first_end(b):
                after(b, 4)
                dve.tensor_reduce(first[:, :], tmp[:, :, :], AX.X, ALU.max).then_inc(route, 1)
                after(b, 5)
                dve.tensor_tensor(oh[:, 0, :, :], tmp[:, :, :], over_experts(first[:, :]), ALU.is_equal)\
                   .then_inc(route, 1)

            def route_second(b):
                after(b, 6)
                dve.scalar_tensor_tensor(out=tmp[:, :, :], in0=oh[:, 0, :, :], scalar=-3e38, in1=sc[:, :, :],
                                         op0=ALU.mult, op1=ALU.add).then_inc(route, 1)
                after(b, 7)
                dve.tensor_reduce(top[:, 1, :], tmp[:, :, :], AX.X, ALU.max).then_inc(route, 1)
                after(b, 8)
                dve.tensor_tensor(tmp[:, :, :], tmp[:, :, :], over_experts(top[:, 1, :]), ALU.is_equal).then_inc(route, 1)
                after(b, 9)
                dve.tensor_tensor(tmp[:, :, :], tmp[:, :, :], over_tiles(C_REV), ALU.mult).then_inc(route, 1)

            def route_second_end(b):
                after(b, 10)
                dve.tensor_reduce(first[:, :], tmp[:, :, :], AX.X, ALU.max).then_inc(route, 1)
                after(b, 11)
                dve.tensor_tensor(oh[:, 1, :, :], tmp[:, :, :], over_experts(first[:, :]), ALU.is_equal)\
                   .then_inc(route, 1)
                after(b, 12)
                dve.tensor_tensor(tmp[:, :, :], oh[:, 0, :, :], oh[:, 1, :, :], ALU.add).then_inc(route, 1)

            def route_counts(b):
                after(b, 13)
                if not (isinstance(b, int) and b == 0):
                    dve.wait_ge(rank_full, b)
                dve.tensor_copy(maskb[:, :, :], tmp[:, :, :]).then_inc(route, 1)
                for i in range(QT):
                    if i:
                        after(b, 14 + i)
                    dve.tensor_tensor(cum[:, i + 1, :], cum[:, i, :], tmp[:, i, :], ALU.add).then_inc(route, 1)
                after(b, 18)
                dve.tensor_copy(cumb[:, :, :], cum[:, 0:QT, :]).then_inc(route, 1)
                after(b, 19)
                dve.tensor_copy(cum[:, 0, :], cum[:, QT, :]).then_inc(route, 1)
                if not (isinstance(b, int) and b == 0):
                    dve.wait_ge(gexp, b)
                dve.tensor_tensor(gex[:, :], top[:, 1, :], top[:, 0, :], ALU.subtract).then_inc(route, 1)

            def route_gates(b):
                dve.wait_ge(gexp, b + 1)
                dve.tensor_scalar(gsum[:, :], gex[:, :], 1.0, None, ALU.add).then_inc(route, 1)
                after(b, 22)
                if not (isinstance(b, int) and b == 0):
                    dve.wait_ge(listed, 16 * 2 * QT * b)
                dve.reciprocal(entry[:, 0, :, 1].bitcast(F32), gsum[:, :]).then_inc(route, 1)
                after(b, 23)
                dve.tensor_tensor(entry[:, 1, :, 1].bitcast(F32), gex[:, :], entry[:, 0, :, 1].bitcast(F32),
                                  ALU.mult).then_inc(route, 1)

            def route_places(b):
                dve.wait_ge(rank_full, b + 1)
                dve.tensor_tensor(rank[:, :, :], M[1][:, 0:QT * E].rearrange("p (i e) -> p i e", e=E),
                                  over_tiles(C_BASE), ALU.add).then_inc(route, 1)
                for c in range(2):
                    after(b, 25 + 2 * c)
                    dve.tensor_tensor(tmp[:, :, :], oh[:, c, :, :], rank[:, :, :], ALU.mult).then_inc(route, 1)
                    after(b, 26 + 2 * c)
                    dve.tensor_reduce(posf[:, c, :], tmp[:, :, :], AX.X, ALU.add).then_inc(route, 1)
                after(b, 29)
                if not (isinstance(b, int) and b == 0):
                    dve.wait_ge(listed, 16 * 2 * QT * b)
                dve.tensor_copy(pos[:, :, :], posf[:, :, :]).then_inc(route, 1)
                dve.tensor_scalar(idf[:, :, :], idf[:, :, :], float(T), None, ALU.add).then_inc(route, 1)
                after(b, 31)
                dve.tensor_copy(entry[:, :, :, 0], idf[:, :, :]).then_inc(route, 1)

            def prologue():
                dve.memset(padrows[:, :], PAD).then_inc(prep, 1)
                dve.memset(minus_half[:, :], -0.5).then_inc(prep, 1)
                dve.memset(ones[:, :], 1.0).then_inc(prep, 1)
                for v in Va:
                    dve.memset(v[:, :, HD:32], 1.0).then_inc(prep, 1)
                dve.memset(zeros8[:, :], 0.0).then_inc(prep, 1)
                dve.memset(cum[:, 0, :], 0.0).then_inc(prep, 1)
                dve.wait_ge(prep, 3)
                dve.tensor_copy(khl[96:128, :], ones[96:128, :]).then_inc(prep, 1)
                ln_stats(0, 0, 0, 0)
                ln_stats(0, 0, 0, 1)
                ln_apply(0, 0, 0)
                ln_apply(0, 0, 1)
                dve.wait_ge(setup_in, 16 * NSETUP)
                dve.tensor_copy(cstb[:, :], prob[:, 0:5, :].rearrange("p a n -> p (a n)")[:, 0:CB_END])\
                   .then_inc(prep, 1)
                dve.tensor_copy(wkv[:, :, 0:96].rearrange("p k (r d) -> p k r d", d=HD),
                                wkv1[:, :, 0:HD].unsqueeze(2).broadcast_to([P, KD, 6, HD])).then_inc(prep, 1)
                dve.tensor_copy(wkv[:, :, 96:128].rearrange("p k (r d) -> p k r d", d=HD),
                                wkv1[:, :, HD:2 * HD].unsqueeze(2).broadcast_to([P, KD, 2, HD])).then_inc(prep, 1)
                dve.tensor_copy(idf[:, :, :], cst[:, C_IDS:C_END].rearrange("p (c i) -> p c i", c=2)).then_inc(prep, 1)
                dve.wait_ge(bias_row, 1)
                at = E * KF
                dve.tensor_copy(biasT[:, 0:at], M[0][:, 0:at]).then_inc(prep, 1)
                dve.tensor_scalar(biasT[:, at:at + KD], M[0][:, at:at + KD], QSCALE, None, ALU.mult).then_inc(prep, 1)
                dve.tensor_copy(biasT[:, at + KD:NBIAS], M[0][:, at + KD:NBIAS]).then_inc(prep, 1)
                ln_stats(0, 1, 1, 0)
                ln_stats(0, 1, 1, 1)
                heads_first(0)
                heads_keys(0, 0)
                heads_second(0)
                ln_apply(0, 1, 0)
                ln_apply(0, 1, 1)
                for n in range(S_BANKS):
                    maxima(0, n)
                split_maxima(0)

            def step(s, par, a, d, ln):
                if a:
                    heads_first(s + 1)
                if d:
                    normalise(s - 1, 0)
                    normalise(s - 1, 1)
                if a:
                    heads_keys(s + 1, 1 - par)
                if d:
                    normalise(s - 1, 2)
                    normalise(s - 1, 3)
                if a:
                    heads_second(s + 1)
                for g in range(GROUPS):
                    for k in range(T_BANKS):
                        if a:
                            for n in banks_of(g, k):
                                maxima(s + 1, n)
                        if d and (g, k) in ((1, 2), (1, 3)):
                            residual(s - 1, k - 2)
                            ln_stats(1, s - 1, 1 - par, k - 2)
                        if d and (g, k) in ((1, 6), (1, 7)):
                            ln_apply(1, s - 1, k - 6)
                        if d and (g, k) == (2, 6):
                            route_first(s - 1)
                        if d and (g, k) == (2, 7):
                            route_first_end(s - 1)
                        if d and (g, k) == (2, 8):
                            route_second(s - 1)
                        if d and (g, k) == (2, 9):
                            route_second_end(s - 1)
                        if d and (g, k) == (3, 0):
                            route_counts(s - 1)
                        if d and (g, k) == (3, 5):
                            route_gates(s - 1)
                        if d and (g, k) == (3, 6):
                            route_places(s - 1)
                        if ln and (g, k) in ((3, 1), (3, 2)):
                            ln_stats(0, s + 2, par, k - 1)
                if a:
                    split_maxima(s + 1)
                if ln:
                    ln_apply(0, s + 2, 0)
                    ln_apply(0, s + 2, 1)

            def last():
                b = B - 1
                for i in range(QT):
                    normalise(b, i)
                residual(b, 0)
                residual(b, 1)
                ln_stats(1, b, b % 2, 0)
                ln_stats(1, b, b % 2, 1)
                ln_apply(1, b, 0)
                ln_apply(1, b, 1)
                route_first(b)
                route_first_end(b)
                route_second(b)
                route_second_end(b)
                route_counts(b)
                route_gates(b)
                route_places(b)

            ROT = rotation()
            steps(dve, prologue, step, last)

            def did(n):
                dve.wait_ge(table, n)

            dve.wait_ge(route, ROUTE * B)
            dve.tensor_copy(cumlast[:, :], cum[:, 0, :]).then_inc(table, 1)
            dve.wait_ge(tot_full, 1)
            dve.tensor_copy(tot[:, :], M[0][:, 0:E]).then_inc(table, 1)
            did(2)
            dve.tensor_tensor(over[:, :, :], tot[:, :].unsqueeze(2).broadcast_to([P, E, N // P]),
                              cst[:, C_CNT:C_CNT + N // P].unsqueeze(1).broadcast_to([P, E, N // P]),
                              ALU.is_gt).then_inc(table, 1)
            did(3)
            dve.tensor_reduce(nblk[:, :], over[:, :, :], AX.X, ALU.add).then_inc(table, 1)
            did(4)
            dve.tensor_scalar(nblk[:, :], nblk[:, :], 1.0, None, ALU.max).then_inc(table, 1)
            did(5)
            dve.tensor_tensor_scan(ends[:, :], nblk[:, :], zeros8[:, :], 0.0, ALU.add, ALU.add).then_inc(table, 1)
            did(6)
            dve.tensor_scalar(lec[:, :], ends[:, :], cst[:, C_COL:C_COL + 1], None, ALU.is_le).then_inc(table, 1)
            did(7)
            dve.tensor_reduce(colv[:, 0:1], lec[:, :], AX.X, ALU.add).then_inc(table, 1)
            dve.tensor_tensor(lecn[:, :], lec[:, :], nblk[:, :], ALU.mult).then_inc(table, 1)
            did(9)
            dve.tensor_reduce(colv[:, 1:2], lecn[:, :], AX.X, ALU.add).then_inc(table, 1)
            dve.scalar_tensor_tensor(out=colv[:, 2:3], in0=colv[:, 0:1], scalar=float(N // P),
                                     in1=cst[:, C_COL:C_COL + 1], op0=ALU.mult, op1=ALU.add).then_inc(table, 1)
            did(11)
            dve.tensor_tensor(colv[:, 3:4], colv[:, 2:3], colv[:, 1:2], ALU.subtract).then_inc(table, 1)
            did(12)
            dve.tensor_scalar(rowi[:, :], colv[:, 3:4], float(LIST_ROWS - 1), None, ALU.min).then_inc(table, 1)

            def ends_of(n):
                return ends[:, 0:n].unsqueeze(1).broadcast_to([P, MAX_BLOCKS, n])

            def blocks_by(n):
                return cst[:, C_BLK:C_BLK + MAX_BLOCKS].unsqueeze(2).broadcast_to([P, MAX_BLOCKS, n])

            dve.wait_ge(pv_full, 3 * GROUPS * B)
            dve.tensor_tensor(le[:, :, 0:E - 1], ends_of(E - 1), blocks_by(E - 1), ALU.is_le).then_inc(table, 1)
            dve.tensor_tensor(start[:, :, :], ends_of(E - 2), blocks_by(E - 2), ALU.is_equal).then_inc(table, 1)
            did(14)
            dve.tensor_reduce(blk_f[:, :], le[:, :, 0:E - 1], AX.X, ALU.add).then_inc(table, 1)
            did(15)
            dve.tensor_reduce(next_f[:, :], start[:, :, :], AX.X, ALU.add).then_inc(table, 1)
            did(17)
            dve.scalar_tensor_tensor(out=code_f[:, :], in0=blk_f[:, :], scalar=2.0, in1=next_f[:, :],
                                     op0=ALU.mult, op1=ALU.add).then_inc(table, 1)
            did(18)
            dve.scalar_tensor_tensor(out=code_f[:, 1:MAX_BLOCKS], in0=blk_f[:, 0:MAX_BLOCKS - 1], scalar=2.0 * E,
                                     in1=code_f[:, 1:MAX_BLOCKS], op0=ALU.mult, op1=ALU.add).then_inc(table, 1)
            did(19)
            dve.tensor_copy(blocks_i[:, :], code_f[:, :]).then_inc(table, 1)

            def split(m, count, half):
                dve.wait_ge(raw_in[m], 16 * count)
                dve.tensor_copy(Wf[:, bass.ds(2 * WE * half + HALF * m, HALF)], raw[:, HALF * m:HALF * m + HALF])\
                   .then_inc(w_hi[m], 1)
                dve.wait_ge(w_hi[m], count)
                split_low(dve, m, VECTOR_COLS, half).then_inc(w_lo[m], 1)

            dve.wait_ge(exps, GROUPS * T_BANKS * B)
            split(0, 1, 0)
            split(1, 1, 0)
            dve.wait_ge(rows_in, 16)
            dve.tensor_copy(ids_f[:, 0, :], ids_r[:, :, 0]).then_inc(table, 1)
            dve.tensor_copy(ids_f[:, 1, :], ids_r[:, :, 1].bitcast(F32)).then_inc(table, 1)
            dve.wait_ge(slots_full, 1)
            dve.tensor_copy(sl_f[:, :], M[1][:, 0:MAX_BLOCKS]).then_inc(table, 1)
            dve.tensor_copy(slot_gate[:, :], M[1][:, MAX_BLOCKS:2 * MAX_BLOCKS]).then_inc(table, 1)
            for n, final in ((23, slots), (27, slot_tok)):
                did(n)
                dve.tensor_scalar(sl_g[:, :], sl_f[:, :], float(N), -float(N), ALU.is_ge, ALU.mult).then_inc(table, 1)
                did(n + 2 if n == 23 else n + 1)
                dve.tensor_tensor(sl_f[:, :], sl_f[:, :], sl_g[:, :], ALU.add).then_inc(table, 1)
                did(n + 3 if n == 23 else n + 2)
                dve.tensor_copy(final[:, :], sl_f[:, :]).then_inc(table, 1)
            did(TABLE)
            dve.wait_ge(b2_in, 16)

            def evac_h0(t):
                dve.wait_ge(f1_full, 2 * t + 1)
                if not (isinstance(t, int) and t == 0):
                    dve.wait_ge(htr_full, 2 * t)
                dve.tensor_copy(hs[:, 0:512], S[0][:, :]).then_inc(hs0, 1)

            def low_xgT(t, par):
                dve.wait_ge(xg_hi, t + 1)
                if not (isinstance(t, int) and t < 2):
                    dve.wait_ge(f1_full, 2 * t - 2)
                dve.tensor_tensor(xgT[par][1][:, :], M[0][:, 0:D], xgT[par][0][:, :].bitcast(F32),
                                  ALU.subtract).then_inc(xg_lo, 1)

            low_xgT(0, 0)
            evac_h0(0)
            low_xgT(1, 1)

            def rows_out(t, par, e):
                dve.wait_ge(f2_full, t + 1)
                if not (isinstance(t, int) and t < 2):
                    dve.wait_ge(added, 16 * t - 16)
                dve.tensor_tensor(yrow[par][:, :], Y[par][:, 0:D], b2b[:, bass.ds(e, 1), :].rearrange("p a d -> p (a d)"),
                                  ALU.add).then_inc(rows_b2, 1)

            def weigh_rows(t, par):
                dve.wait_ge(rows_b2, t + 1)
                dve.tensor_scalar(yrow[par][:, :], yrow[par][:, :], slot_gate[:, bass.ds(t, 1)], None,
                                  ALU.mult).then_inc(y_s, 1)

            def body(t, par, following):
                first = isinstance(t, int) and t == 0
                e, e_before, half, new = block_of(dve, t)
                for c in range(2):
                    dve.wait_ge(htr_full, 2 * t + c + 1)
                    if not first:
                        dve.wait_ge(h_lo, 2 * t)
                    dve.tensor_tensor(hT[:, 4 * c:4 * c + 4, :], TT[c][:, :].rearrange("p (k n) -> p k n", n=P),
                                      biasT[:, bass.ds(KF * e + 4 * c, 4)].unsqueeze(2).broadcast_to([P, 4, P]),
                                      ALU.add).then_inc(z_s, 1)
                if not first:
                    rows_out(t - 1, 1 - par, e_before)
                if first:
                    split(0, 2, 1)
                elif following:
                    with dve.If(new):
                        split(0, e + 2, 1 - half)
                for c in range(2):
                    dve.wait_ge(gelu_s, 2 * t + c + 1)
                    part = slice(4 * c, 4 * c + 4)
                    dve.tensor_tensor(hTs[1][:, part, :], hG[:, part, :], hTs[0][:, part, :].bitcast(F32),
                                      ALU.subtract).then_inc(h_lo, 1)
                if not first:
                    weigh_rows(t - 1, 1 - par)
                if following:
                    evac_h0(t + 1)
                if following == 2:
                    low_xgT(t + 2, par)
                if first:
                    split(1, 2, 1)
                elif following:
                    with dve.If(new):
                        split(1, e + 2, 1 - half)
                if not following:
                    rows_out(t, par, e)
                    weigh_rows(t, par)

            blocks(dve, body)

        @block.tensor
        def _(pe):
            def transposes(dst, srcs, width, done):
                for i, src in enumerate(srcs):
                    last = pe.transpose(dst[:, width * i:width * i + width], src, ident)
                last.then_inc(done, 1)

            def xT_of(n, b, k):
                pe.wait_ge(xh_s[n], QT * b + QT)
                if n == 1:
                    if k == 0:
                        pe.wait_ge(x2_s, 2 * b + 1)
                    else:
                        pe.wait_ge(x2_s, 2 * b + 2)
                    bank = M[k]
                else:
                    if isinstance(b, int) and b == 0:
                        pe.wait_ge(prep, PREP)
                    elif k == 0:
                        pe.wait_ge(v_sb, 2 * b)
                    else:
                        pe.wait_ge(mt_sb, b)
                    bank = M[1 - k]
                transposes(bank, [xh[n][:, i, P * k:P * k + P] for i in range(QT)], P, xt_full[n])

            def project(b, i):
                t, bank = PARTS[i]
                if i == 0:
                    pe.wait_ge(xt_sb[0], KD * b + 2)
                if i == 2:
                    pe.wait_ge(qkv_sb, 3 * b + 1)
                for k in range(KD):
                    w = wkv[:, k, :] if t == 2 else wq[:, k, P * t:P * t + P]
                    last = pe.matmul(M[bank][:, :], w, xT[0][:, k, :], start=(k == 0), stop=(k == KD - 1))
                last.then_inc(qkv_full, 1)

            def v_rows(b, d):
                pe.wait_ge(qkv_sb, 3 * b + 3)
                settle(pe, b)
                for u in range(2):
                    if d:
                        pe.wait_ge(route, ROUTE * (b - 2) + (R_SCORES, R_RANK)[u])
                        settle(pe, b)
                    for i in range(2):
                        at = P * (2 * u + i)
                        last = pe.transpose(M[u][:, 32 * i:32 * i + 32], qraw[96:128, 2, at:at + P],
                                            ident[96:128, 96:128])
                    last.then_inc(v_full, 1)

            def scores_bank(b, par, n):
                qt, h0, nh = BANKS[n]
                if n == 0:
                    pe.wait_ge(ks_s, 2 * b + 2)
                if n % QUARTER_BANKS == 0:
                    pe.wait_ge(stack_in[n // QUARTER_BANKS], 16 * 6 * b + 16 * 6)
                if not (isinstance(b, int) and b == 0 and n < 3):
                    pe.wait_ge(s_max, S_BANKS * b + n - (1 if n < 2 else 2))
                w = P * (qt + 1)
                for i in range(nh):
                    h = h0 + i
                    pe.matmul(S[n % 3][:, w * i:w * i + w], QQ[par][:, h // 2, P * qt:P * qt + P],
                              KS[h % 2][:, 0:w], start=True, stop=True)
                    last = pe.matmul(S[n % 3][:, w * i + P * qt:w * i + w], identb,
                                     cstb[:, CB_S + 3 * P:CB_S + 4 * P], start=False, stop=True,
                                     skip_group_check=True)
                last.then_inc(s_full, 1)

            def max_rows(b):
                pe.wait_ge(nsplit_s, 2 * b + 2)
                pe.wait_ge(v_sb, 2 * b + 1)
                for i in range(QT):
                    last = pe.transpose(M[0][0:2 * H, P * i:P * i + P], nsplit[:, i, :].bitcast(F32), ident)
                last.then_inc(mt_full, 1)

            def soft_part(par, bank, at, h, kt):
                w = T - P * kt
                return pe.matmul(bank[:, at:at + w], KK[par][h % 2][:, P * kt:P * kt + P],
                                 QQ[par][:, h // 2, P * kt:T], start=False, stop=True,
                                 skip_group_check=True)

            def soft_bank(s, par, g, k):
                n = T_BANKS * g + k
                if not (isinstance(s, int) and s == 0 and n < 2):
                    pe.wait_ge(exps, GROUPS * T_BANKS * s + n - 1)
                bank = TT[k % 2]
                at = CB_T if 4 <= k < 8 else CB_T + 3 * P
                mask = cstb[:, at:at + T]
                if k >= 8:
                    mask = cstb[:, at:at + 2 * P].unsqueeze(1).broadcast_to([P, 2, 2 * P])
                pe.matmul(bank[:, :], identb, mask, start=True, stop=True)
                if k < 4:
                    last = soft_part(par, bank, 0, 4 * g + k, 0)
                elif k < 8:
                    soft_part(par, bank, 0, 4 * g + k - 4, 1)
                    last = soft_part(par, bank, 3 * P, 4 * g + k - 4, 3)
                else:
                    soft_part(par, bank, 0, 4 * g + 2 * (k - 8), 2)
                    last = soft_part(par, bank, 2 * P, 4 * g + 2 * (k - 8) + 1, 2)
                last.then_inc(t_full, 1)

            def pv(s, par, g, stage):
                pe.wait_ge(exps, GROUPS * T_BANKS * s + T_BANKS * g + (4, 8, 10)[stage])
                if stage == 0:
                    pe.wait_ge(v_sb, 2 * s + 2)
                    if not (isinstance(s, int) and s == 0 and g == 0):
                        pe.wait_ge(ot_sb, GROUPS * s + g)
                for kt in ((0,), (1, 3), (2,))[stage]:
                    for j in range(4):
                        slot, at = {0: (j, 0), 1: (4 + j, 0), 3: (4 + j, 3 * P), 2: (8 + j // 2, 2 * P * (j % 2))}[kt]
                        last = pe.matmul(PV[32 * j:32 * j + 32, P * kt:T], Va[par][:, kt, :],
                                         prob[:, slot, at:at + T - P * kt], start=(kt == 0), stop=(kt == 2),
                                         skip_group_check=True)
                last.then_inc(pv_full, 1)

            def heads_rows(b, i, before):
                if i == 0:
                    pe.wait_ge(ot_sb, GROUPS * b + GROUPS)
                if i < 2:
                    before(i)
                else:
                    pe.wait_ge(on_s, QT * b + i - 1)
                transposes(M[i % 2], [oT[:, g, P * i:P * i + P] for g in range(GROUPS)], P, otr_full)

            def heads_back(b, k):
                pe.wait_ge(on_s, QT * b + QT)
                transposes(M[k], [on[:, i, P * k:P * k + P] for i in range(QT)], P, ott_full)

            def output(b, u):
                pe.wait_ge(ott_sb, KD * b + 2)
                for j in range(2):
                    for k in range(KD):
                        at = P * (2 * u + j)
                        last = pe.matmul(M[u][:, D * j:D * j + D], oT2[:, k, at:at + P], wo[:, k, :],
                                         start=(k == 0), stop=(k == KD - 1))
                last.then_inc(wo_full, 1)

            def router(b):
                pe.wait_ge(xt_sb[1], KD * b + 2)
                for i in range(QT):
                    for k in range(KD):
                        last = pe.matmul(M[0][:, E * i:E * i + E], xT[1][:, k, P * i:P * i + P], wr[:, k, :],
                                         start=(k == 0), stop=(k == KD - 1))
                last.then_inc(sc_full, 1)

            def ranks(b):
                pe.wait_ge(route, ROUTE * b + R_MASKS)
                pe.matmul(M[1][:, 0:QT * E], cstb[:, CB_U:CB_U + P], maskb[:, :, :].rearrange("p i e -> p (i e)"),
                          start=True, stop=False)
                pe.matmul(M[1][:, 0:QT * E], cstb[:, CB_ONE:CB_ONE + P], cumb[:, :, :].rearrange("p i e -> p (i e)"),
                          start=False, stop=True).then_inc(rank_full, 1)

            def prologue():
                pe.wait_ge(setup_in, 16 * NSETUP)
                pe.wait_ge(q_zero, 2)
                pe.transpose(M[0][:, 0:NBIAS], brow[:, :], ident[0:NBIAS, 0:NBIAS]).then_inc(bias_row, 1)
                xT_of(0, 0, 0)
                xT_of(0, 0, 1)
                for i in range(3):
                    project(0, i)
                v_rows(0, False)
                for n in range(S_BANKS):
                    scores_bank(0, 0, n)
                max_rows(0)

            def step(s, par, a, d, _):
                if a:
                    xT_of(0, s + 1, 0)
                    xT_of(0, s + 1, 1)
                    project(s + 1, 0)
                    project(s + 1, 1)
                pe.wait_ge(m_in, 64 * s + 64)

                def before(i):
                    if a:
                        pe.wait_ge(qkv_sb, 3 * s + 3 + (2, 3)[i])
                    elif i == 0:
                        pe.wait_ge(mt_sb, s + 1)
                    else:
                        pe.wait_ge(v_sb, 2 * s + 2)

                for g in range(GROUPS):
                    for k in range(T_BANKS):
                        if a and (g, k) == (0, 1):
                            project(s + 1, 2)
                        if d and (g, k) in ((0, 2), (0, 3), (0, 5), (0, 6)):
                            heads_rows(s - 1, (2, 3, 5, 6).index(k), before)
                        if d and (g, k) in ((0, 8), (0, 9)):
                            heads_back(s - 1, k - 8)
                        if d and (g, k) in ((1, 1), (1, 2)):
                            output(s - 1, k - 1)
                        if d and (g, k) in ((2, 1), (2, 2)):
                            xT_of(1, s - 1, k - 1)
                        if d and (g, k) == (2, 5):
                            router(s - 1)
                        if d and (g, k) == (3, 3):
                            ranks(s - 1)
                        if g and k in (0, 4, 8):
                            pv(s, par, g - 1, k // 4)
                        soft_bank(s, par, g, k)
                        if a:
                            for n in banks_of(g, k):
                                scores_bank(s + 1, 1 - par, n)
                if a:
                    v_rows(s + 1, d)
                pv(s, par, GROUPS - 1, 0)
                if a:
                    max_rows(s + 1)
                pv(s, par, GROUPS - 1, 1)
                pv(s, par, GROUPS - 1, 2)

            def last():
                b = B - 1
                for i in range(QT):
                    heads_rows(b, i, lambda i: pe.wait_ge(route, ROUTE * (b - 1) + (R_SCORES, R_RANK)[i]))
                heads_back(b, 0)
                heads_back(b, 1)
                output(b, 0)
                output(b, 1)
                xT_of(1, b, 0)
                xT_of(1, b, 1)
                router(b)
                ranks(b)

            steps(pe, prologue, step, last)

            pe.wait_ge(table, 1)
            pe.matmul(M[0][:, 0:E], cstb[:, CB_ONE:CB_ONE + P], cumlast[:, :], start=True, stop=True)\
              .then_inc(tot_full, 1)
            pe.wait_ge(table, IDS_AT)
            for a in range(2):
                last = pe.transpose(M[1][:, MAX_BLOCKS * a:MAX_BLOCKS * (a + 1)], ids_f[:, a, :],
                                    ident[0:MAX_BLOCKS, 0:MAX_BLOCKS])
            last.then_inc(slots_full, 1)
            pe.wait_ge(table, TABLE)

            def block_xT(t, par):
                pe.wait_ge(gath[par], 8 * (t - par) + 16)
                if not (isinstance(t, int) and t == 0):
                    pe.wait_ge(xg_lo, t)
                transposes(M[0], [xg[par][:, P * k:P * k + P] for k in range(KD)], P, xgt_full)

            PASSES = ((0, 0), (0, 1), (1, 0))

            def layer1(t, par):
                e, _, half, _ = block_of(pe, t)
                pe.wait_ge(w_lo[0], 2 * e + 2)
                pe.wait_ge(xg_lo, t + 1)
                for c in range(2):
                    if not (isinstance(t, int) and t == 0):
                        pe.wait_ge((hs0, hs1)[c], t)
                    for k in range(KD):
                        for n, (rows, part) in enumerate(PASSES):
                            last = pe.matmul(S[c][:, :], xgT[par][rows][:, P * k:P * k + P],
                                             Wf[:, bass.ds(2 * WE * half + WE * part + F * k + 512 * c, 512)],
                                             start=(k == 0 and n == 0), stop=(k == KD - 1 and n == 2))
                    last.then_inc(f1_full, 1)

            def hidden_T(t):
                for c in range(2):
                    pe.wait_ge((hs0, hs1)[c], t + 1)
                    if not (isinstance(t, int) and t == 0):
                        pe.wait_ge(z_s, 2 * t)
                    transposes(TT[c], [hs[:, P * k:P * k + P] for k in range(4 * c, 4 * c + 4)], P, htr_full)

            def layer2(t, par):
                e, _, half, _ = block_of(pe, t)
                pe.wait_ge(w_lo[1], 2 * e + 2)
                if not (isinstance(t, int) and t < 2):
                    pe.wait_ge(y_s, t - 1)
                for k in range(KF):
                    if k % 4 == 0:
                        pe.wait_ge(h_lo, 2 * t + k // 4 + 1)
                    for n, (rows, part) in enumerate(PASSES):
                        last = pe.matmul(Y[par][:, 0:D], hTs[rows][:, k, :],
                                         Wf[:, bass.ds(2 * WE * half + WE * part + HALF + D * k, D)],
                                         start=(k == 0 and n == 0), stop=(k == KF - 1 and n == 2))
                last.then_inc(f2_full, 1)

            block_xT(0, 0)
            layer1(0, 0)
            block_xT(1, 1)

            def body(t, par, following):
                hidden_T(t)
                if following:
                    layer1(t + 1, 1 - par)
                if following == 2:
                    block_xT(t + 2, par)
                layer2(t, par)

            blocks(pe, body)


_INS = ["L0_attn_x", "L0_attn_Wq", "L0_attn_bq", "L0_attn_Wk", "L0_attn_bk", "L0_attn_Wv", "L0_attn_bv",
        "L0_attn_Wo", "L0_attn_bo", "L0_ffn_W1", "L0_ffn_b1", "L0_ffn_W2", "L0_ffn_b2", "L0_ffn_Wr", "L0_ffn_br"]


def kernel(**inputs):
    import numpy as _np
    import concourse.bacc as _bacc
    from concourse import mybir as _mybir
    from concourse.bass_utils import run_bass_kernel_spmd as _run

    nc = _bacc.Bacc("TRN2", target_bir_lowering=False, num_devices=1)
    arrays, args = {}, []
    named = [(n, _np.ascontiguousarray(inputs[n])) for n in _INS]
    named += list(zip(("const", "constb", "rope"), constants()))
    for name, a in named:
        arrays[f"in_{name}"] = a
        args.append(nc.dram_tensor(f"in_{name}", a.shape, _mybir.dt.from_np(a.dtype), kind="ExternalInput").ap())
    args.append(nc.dram_tensor("out", (B, T, D), _mybir.dt.float32, kind="ExternalOutput").ap())
    layer(nc, *args)
    r = _run(nc, [arrays], core_ids=[0])
    return r.results[0]["out"]
```
